# Optimizing a Trainium2 kernel written in Bass

```python
import numpy as np
import jax
import jax.numpy as jnp

def _softmax(x, axis=-1):
    return jax.nn.softmax(x, axis=axis)

def _gelu(x):
    return jax.nn.gelu(x, approximate=True)

def _silu(x):
    return jax.nn.silu(x)

def _sigmoid(x):
    return jax.nn.sigmoid(x)

def _layernorm(x, axis=-1, eps=1e-05):
    m = jnp.mean(x, axis=axis, keepdims=True)
    v = jnp.var(x, axis=axis, keepdims=True)
    return (x - m) / jnp.sqrt(v + eps)

def _scatter_add(tgt, idx, src, axis=0):
    return tgt.at[idx].add(src)

def _segment_sum(src, seg, n):
    return jax.ops.segment_sum(src, seg, n)
kernel_name = 'mk_seq_preln_d2_jaxref_r4_36dde3'

def setup_inputs(seed: int=0):
    np.random.seed(seed)
    _w = jnp.asarray

    def _L0_attn_setup():
        import jax, jax.numpy as jnp
        import numpy as np
        from jax import lax
        D_MODEL = 256
        N_HEADS = 16
        D_HEAD = 64
        INNER = N_HEADS * D_HEAD
        EPS = 1e-12

        def _delta_net(x, Wq, Wk, Wv, Wbeta, b_beta, Wout):
            B, T, _ = x.shape
            H, D = (N_HEADS, D_HEAD)
            Q = (x @ Wq).reshape(B, T, H, D)
            K = (x @ Wk).reshape(B, T, H, D)
            V = (x @ Wv).reshape(B, T, H, D)
            beta = jax.nn.sigmoid(x @ Wbeta + b_beta)
            K = K / jnp.maximum(jnp.linalg.norm(K, axis=-1, keepdims=True), EPS)
            xs = (jnp.moveaxis(Q, 1, 0), jnp.moveaxis(K, 1, 0), jnp.moveaxis(V, 1, 0), jnp.moveaxis(beta, 1, 0))

            def step(W, inp):
                q_t, k_t, v_t, b_t = inp
                pred = jnp.einsum('bhij,bhj->bhi', W, k_t)
                err = v_t - pred
                W_new = W + b_t[..., None, None] * jnp.einsum('bhi,bhj->bhij', err, k_t)
                o_t = jnp.einsum('bhij,bhj->bhi', W_new, q_t)
                return (W_new, o_t)
            W0 = jnp.zeros((B, H, D, D), dtype=x.dtype)
            _, O = lax.scan(step, W0, xs)
            out = jnp.moveaxis(O, 0, 1).reshape(B, T, H * D)
            return out @ Wout
        key = jax.random.key(seed)
        ks = jax.random.split(key, 7)
        B, T = (4, 512)
        s = 1.0 / np.sqrt(D_MODEL)
        return {'x': jax.random.normal(ks[0], (B, T, D_MODEL), dtype=jnp.float32), 'Wq': jax.random.normal(ks[1], (D_MODEL, INNER), dtype=jnp.float32) * s, 'Wk': jax.random.normal(ks[2], (D_MODEL, INNER), dtype=jnp.float32) * s, 'Wv': jax.random.normal(ks[3], (D_MODEL, INNER), dtype=jnp.float32) * s, 'Wbeta': jax.random.normal(ks[4], (D_MODEL, N_HEADS), dtype=jnp.float32) * s, 'b_beta': jax.random.normal(ks[5], (N_HEADS,), dtype=jnp.float32) * 0.01, 'Wout': jax.random.normal(ks[6], (INNER, D_MODEL), dtype=jnp.float32) * (1.0 / np.sqrt(INNER))}
    _L0_attn_in = _L0_attn_setup()

    def _L0_ffn_setup():
        import jax, jax.numpy as jnp
        import numpy as np
        N_EXPERTS = 8
        CAP_FACTOR = 1.25
        BATCH, SEQ, DMODEL, DFF = (4, 512, 256, 1024)
        key = jax.random.key(seed)
        k0, k1, k2, k3 = jax.random.split(key, 4)
        x = jax.random.normal(k0, (BATCH, SEQ, DMODEL), dtype=jnp.float32)
        Wr = jax.random.normal(k1, (DMODEL, N_EXPERTS), dtype=jnp.float32) * 0.02
        W1 = jax.random.normal(k2, (N_EXPERTS, DMODEL, DFF), dtype=jnp.float32) * 0.02
        W2 = jax.random.normal(k3, (N_EXPERTS, DFF, DMODEL), dtype=jnp.float32) * 0.02
        return {'x': x, 'Wr': Wr, 'W1': W1, 'W2': W2}
    _L0_ffn_in = _L0_ffn_setup()

    def _L1_attn_setup():
        import jax, jax.numpy as jnp
        import numpy as np
        B, S, D = (2, 512, 256)
        H, P = (16, 64)
        NUM_OUT = 256
        key = jax.random.key(seed)
        ks = jax.random.split(key, 9)
        sc = 0.05
        return {'x': jax.random.normal(ks[0], (B, S, D), jnp.float32), 'q_w': jax.random.normal(ks[1], (H, P, D), jnp.float32) * sc, 'q_b': jax.random.normal(ks[2], (H, 1, P), jnp.float32) * sc, 'k_w': jax.random.normal(ks[3], (H, P, D), jnp.float32) * sc, 'k_b': jax.random.normal(ks[4], (H, 1, P), jnp.float32) * sc, 'v_w': jax.random.normal(ks[5], (H, P, D), jnp.float32) * sc, 'v_b': jax.random.normal(ks[6], (H, 1, P), jnp.float32) * sc, 'l_w': jax.random.normal(ks[7], (NUM_OUT, P * H), jnp.float32) * sc, 'l_b': jax.random.normal(ks[8], (1, NUM_OUT), jnp.float32) * sc}
    _L1_attn_in = _L1_attn_setup()

    def _L1_ffn_setup():
        import jax, jax.numpy as jnp
        import numpy as np
        NUM_EXPERTS = 8
        CAPACITY = 160
        key = jax.random.key(seed)
        ks = jax.random.split(key, 5)
        D, E, F = (256, NUM_EXPERTS, 1024)
        inputs = jax.random.normal(ks[0], (2, 512, D), dtype=jnp.float32)
        gate_w = jax.random.normal(ks[1], (D, E), dtype=jnp.float32) * 0.02
        gate_b = jnp.zeros((E,), dtype=jnp.float32)
        w1 = jax.random.normal(ks[2], (E, D, F), dtype=jnp.float32) * 0.02
        b1 = jnp.zeros((E, F), dtype=jnp.float32)
        w2 = jax.random.normal(ks[3], (E, F, D), dtype=jnp.float32) * 0.02
        b2 = jnp.zeros((E, D), dtype=jnp.float32)
        return {'inputs': inputs, 'gate_w': gate_w, 'gate_b': gate_b, 'w1': w1, 'b1': b1, 'w2': w2, 'b2': b2}
    _L1_ffn_in = _L1_ffn_setup()
    _d = {'L0_attn_x': _L0_attn_in['x'], 'L0_attn_Wq': _L0_attn_in['Wq'], 'L0_attn_Wk': _L0_attn_in['Wk'], 'L0_attn_Wv': _L0_attn_in['Wv'], 'L0_attn_Wbeta': _L0_attn_in['Wbeta'], 'L0_attn_b_beta': _L0_attn_in['b_beta'], 'L0_attn_Wout': _L0_attn_in['Wout'], 'L0_ffn_Wr': _L0_ffn_in['Wr'], 'L0_ffn_W1': _L0_ffn_in['W1'], 'L0_ffn_W2': _L0_ffn_in['W2'], 'L1_attn_q_w': _L1_attn_in['q_w'], 'L1_attn_q_b': _L1_attn_in['q_b'], 'L1_attn_k_w': _L1_attn_in['k_w'], 'L1_attn_k_b': _L1_attn_in['k_b'], 'L1_attn_v_w': _L1_attn_in['v_w'], 'L1_attn_v_b': _L1_attn_in['v_b'], 'L1_attn_l_w': _L1_attn_in['l_w'], 'L1_attn_l_b': _L1_attn_in['l_b'], 'L1_ffn_gate_w': _L1_ffn_in['gate_w'], 'L1_ffn_gate_b': _L1_ffn_in['gate_b'], 'L1_ffn_w1': _L1_ffn_in['w1'], 'L1_ffn_b1': _L1_ffn_in['b1'], 'L1_ffn_w2': _L1_ffn_in['w2'], 'L1_ffn_b2': _L1_ffn_in['b2']}
    _x0 = _d['L0_attn_x']
    _d['L0_attn_x'] = jax.random.normal(jax.random.fold_in(jax.random.key(seed), 1), (4, 1024, 256), dtype=_x0.dtype)
    del _x0
    return _d

def reference(L0_attn_x, L0_attn_Wq, L0_attn_Wk, L0_attn_Wv, L0_attn_Wbeta, L0_attn_b_beta, L0_attn_Wout, L0_ffn_Wr, L0_ffn_W1, L0_ffn_W2, L1_attn_q_w, L1_attn_q_b, L1_attn_k_w, L1_attn_k_b, L1_attn_v_w, L1_attn_v_b, L1_attn_l_w, L1_attn_l_b, L1_ffn_gate_w, L1_ffn_gate_b, L1_ffn_w1, L1_ffn_b1, L1_ffn_w2, L1_ffn_b2):

    def _L0_attn_ref(x, Wq, Wk, Wv, Wbeta, b_beta, Wout):
        import jax, jax.numpy as jnp
        import numpy as np
        from jax import lax
        D_MODEL = 256
        N_HEADS = 16
        D_HEAD = 64
        INNER = N_HEADS * D_HEAD
        EPS = 1e-12

        def _delta_net(x, Wq, Wk, Wv, Wbeta, b_beta, Wout):
            B, T, _ = x.shape
            H, D = (N_HEADS, D_HEAD)
            Q = (x @ Wq).reshape(B, T, H, D)
            K = (x @ Wk).reshape(B, T, H, D)
            V = (x @ Wv).reshape(B, T, H, D)
            beta = jax.nn.sigmoid(x @ Wbeta + b_beta)
            K = K / jnp.maximum(jnp.linalg.norm(K, axis=-1, keepdims=True), EPS)
            xs = (jnp.moveaxis(Q, 1, 0), jnp.moveaxis(K, 1, 0), jnp.moveaxis(V, 1, 0), jnp.moveaxis(beta, 1, 0))

            def step(W, inp):
                q_t, k_t, v_t, b_t = inp
                pred = jnp.einsum('bhij,bhj->bhi', W, k_t)
                err = v_t - pred
                W_new = W + b_t[..., None, None] * jnp.einsum('bhi,bhj->bhij', err, k_t)
                o_t = jnp.einsum('bhij,bhj->bhi', W_new, q_t)
                return (W_new, o_t)
            W0 = jnp.zeros((B, H, D, D), dtype=x.dtype)
            _, O = lax.scan(step, W0, xs)
            out = jnp.moveaxis(O, 0, 1).reshape(B, T, H * D)
            return out @ Wout
        return _delta_net(x, Wq, Wk, Wv, Wbeta, b_beta, Wout)

    def _L0_ffn_ref(x, Wr, W1, W2):
        import jax, jax.numpy as jnp
        import numpy as np
        N_EXPERTS = 8
        CAP_FACTOR = 1.25
        BATCH, SEQ, DMODEL, DFF = (4, 512, 256, 1024)
        B, S, D = x.shape
        E = W1.shape[0]
        cap = int(CAP_FACTOR * B * S / E)
        t = x.reshape(-1, D)
        probs = jax.nn.softmax(t @ Wr, axis=-1)
        idx = jnp.argmax(probs, axis=-1)
        pmax = jnp.max(probs, axis=-1)
        onehot = jax.nn.one_hot(idx, E, dtype=jnp.int32)
        pos = jnp.sum(jnp.cumsum(onehot, axis=0) * onehot, axis=-1) - 1
        kept = pos < cap
        flat = idx * cap + jnp.minimum(pos, cap - 1)
        disp = jnp.zeros((E * cap, D), t.dtype).at[flat].add(t * kept[:, None].astype(t.dtype))
        ein = disp.reshape(E, cap, D)
        h = jax.nn.relu(jnp.einsum('ecd,edf->ecf', ein, W1))
        eout = jnp.einsum('ecf,efd->ecd', h, W2).reshape(E * cap, D)
        comb = jnp.where(kept[:, None], eout[flat], t)
        factor = jnp.where(kept, pmax, jnp.ones_like(pmax))
        out = (comb * factor[:, None]).reshape(B, S, D)
        return out

    def _L1_attn_ref(x, q_w, q_b, k_w, k_b, v_w, v_b, l_w, l_b):
        import jax, jax.numpy as jnp
        import numpy as np
        B, S, D = (2, 512, 256)
        H, P = (16, 64)
        NUM_OUT = 256
        q = jnp.einsum('bsd,hpd->bhsp', x, q_w) + q_b
        k = jnp.einsum('bsd,hpd->bhsp', x, k_w) + k_b
        v = jnp.einsum('bsd,hpd->bhsp', x, v_w) + v_b
        scores = jnp.einsum('bhqp,bhkp->bhqk', q, k) / jnp.sqrt(jnp.float32(P))
        attn = jax.nn.softmax(scores, axis=2)
        ctx = jnp.einsum('bhqk,bhkp->bqhp', attn, v)
        concat = ctx.reshape(ctx.shape[0], ctx.shape[1], H * P)
        out = concat @ l_w.T + l_b
        return out

    def _L1_ffn_ref(inputs, gate_w, gate_b, w1, b1, w2, b2):
        import jax, jax.numpy as jnp
        import numpy as np
        NUM_EXPERTS = 8
        CAPACITY = 160
        D = inputs.shape[-1]
        tokens = inputs.reshape(-1, D)
        logits = tokens @ gate_w + gate_b
        probs = jax.nn.softmax(logits, axis=-1)
        expert_idx = jnp.argmax(probs, axis=-1)
        mask1 = jax.nn.one_hot(expert_idx, NUM_EXPERTS, dtype=jnp.float32)
        pos = jnp.sum(jnp.cumsum(mask1, axis=0) * mask1, axis=-1) - 1.0
        pos = pos.astype(jnp.int32)
        keep = (pos < CAPACITY).astype(jnp.float32)
        gate_prob = jnp.sum(probs * mask1, axis=-1)
        pos_oh = jax.nn.one_hot(pos, CAPACITY, dtype=jnp.float32)
        sec_mask = mask1[:, :, None] * pos_oh[:, None, :] * keep[:, None, None]
        combine_weights = sec_mask * gate_prob[:, None, None]
        dispatch = jnp.einsum('nec,nd->ecd', sec_mask, tokens)
        h = jax.nn.gelu(jnp.einsum('ecd,edf->ecf', dispatch, w1) + b1[:, None, :])
        expert_out = jnp.einsum('ecf,efd->ecd', h, w2) + b2[:, None, :]
        out = jnp.einsum('nec,ecd->nd', combine_weights, expert_out)
        return out.reshape(inputs.shape)
    x = L0_attn_x
    x = x + _L0_attn_ref(_layernorm(x, axis=-1), L0_attn_Wq, L0_attn_Wk, L0_attn_Wv, L0_attn_Wbeta, L0_attn_b_beta, L0_attn_Wout)
    x = x + _L0_ffn_ref(_layernorm(x, axis=-1), L0_ffn_Wr, L0_ffn_W1, L0_ffn_W2)
    x = x + _L1_attn_ref(_layernorm(x, axis=-1), L1_attn_q_w, L1_attn_q_b, L1_attn_k_w, L1_attn_k_b, L1_attn_v_w, L1_attn_v_b, L1_attn_l_w, L1_attn_l_b)
    x = x + _L1_ffn_ref(_layernorm(x, axis=-1), L1_ffn_gate_w, L1_ffn_gate_b, L1_ffn_w1, L1_ffn_b1, L1_ffn_w2, L1_ffn_b2)
    return x

_drawn_inputs = setup_inputs


def setup_inputs(seed=0):
    import zlib

    import numpy as np

    out = dict(_drawn_inputs(seed))
    spreads = {'L1_ffn_gate_b': (0.0, 0.8), 'L1_ffn_b1': (0.0, 0.8), 'L1_ffn_b2': (0.0, 2.0)}
    factors = {'L0_attn_b_beta': 8.0,
     'L0_ffn_Wr': 8.0,
     'L0_ffn_W1': 8.0,
     'L0_ffn_W2': 8.0,
     'L1_attn_q_w': 4.494,
     'L1_attn_q_b': 64.0,
     'L1_attn_k_w': 4.534,
     'L1_attn_k_b': 8.0,
     'L1_attn_v_w': 3.988,
     'L1_attn_v_b': 4.014,
     'L1_attn_l_w': 2.843,
     'L1_attn_l_b': 6.817,
     'L1_ffn_gate_w': 8.0,
     'L1_ffn_w1': 8.0,
     'L1_ffn_w2': 8.0}
    for name, (base, spread) in spreads.items():
        noise = np.random.default_rng([zlib.crc32(name.encode()), seed]).standard_normal(out[name].shape)
        drawn = base * np.exp(spread * noise) if base else spread * noise
        out[name] = jnp.asarray(drawn.astype(out[name].dtype))
    for name, factor in factors.items():
        out[name] = (out[name] * factor).astype(out[name].dtype)
    return out
```

```python
import numpy as np
from contextlib import ExitStack

import concourse.bass as bass
from concourse import mybir

F32 = mybir.dt.float32
BF16 = mybir.dt.bfloat16
I32 = mybir.dt.int32
U32 = mybir.dt.uint32
ALU = mybir.AluOpType
ACT = mybir.ActivationFunctionType
AX = mybir.AxisListType

P = 128
B, S, D = 4, 1024, 256
H, DH = 16, 64
HP = H // 2
KD = D // P
C = 64
NCH = S // C
LEVELS = 6
LN_EPS = 1e-5
NORM_EPS = 1e-12
SQ_EPS = NORM_EPS * NORM_EPS

C_ID = 0
C_ID2 = C_ID + P
C_LVL = C_ID2 + C
C_CAUSAL = C_LVL + LEVELS * C
C_TRI = C_CAUSAL + C
C_ONE = C_TRI + P
C_EXP = C_ONE + P
C_RANK = C_EXP + 8
C_ALL = C_RANK + 8


def shape_constants():
    c = np.zeros((P, C_ALL), np.float32)
    row = np.arange(P)[:, None]
    c[:, C_ID:C_ID + P] = row == np.arange(P)[None]
    s, t = row % C, np.arange(C)[None]
    c[:, C_ID2:C_ID2 + C] = s == t
    for l in range(LEVELS):
        same = (s >> (l + 1)) == (t >> (l + 1))
        c[:, C_LVL + l * C:C_LVL + (l + 1) * C] = same & ((t >> l) % 2 == 1) & ((s >> l) % 2 == 0)
    c[:, C_CAUSAL:C_CAUSAL + C] = -1.0 * (s <= t)
    c[:, C_TRI:C_TRI + P] = row <= np.arange(P)[None]
    c[:, C_ONE:C_ONE + P] = 1.0
    c[:, C_EXP:C_EXP + 8] = np.arange(8)[None]
    c[:, C_RANK:C_RANK + 8] = 8 - np.arange(8)[None]
    return c


def clear(nc, held):
    nc.clear_and_free_semaphores(held)
    nc.all_engine_barrier()


class Counts:

    def __init__(self, eng, name, n=3):
        self.eng, self.regs = eng, [eng.alloc_register(f"{name}_count{i}") for i in range(n)]

    def __call__(self, *values):
        for reg, value in zip(self.regs, values):
            self.eng.reg_mov(reg, value)
        return self.regs[:len(values)]


def delta_layer(nc, consts, x, Wq, Wk, Wv, Wbeta, b_beta, Wout, x1):
    held = []
    with ExitStack() as ctx:
        def sb(name, shape, dt=F32):
            return ctx.enter_context(nc.sbuf_tensor("dl_" + name, shape, dt))

        def sem(name):
            held.append(nc.alloc_semaphore(name="dl_" + name))
            return held[-1]

        bank = [ctx.enter_context(nc.psum_tensor(f"dl_bank{i}", [P, 512], F32)) for i in range(8)]

        cst = sb("cst", [P, C_TRI])
        wq, wk, wv = (sb(n, [P, KD, H * DH]) for n in ("wq", "wk", "wv"))
        wout = sb("wout", [P, HP, D])
        wbeta = sb("wbeta", [P, KD, H])
        bbeta = sb("bbeta", [P, HP])
        x_ln = sb("x_ln", [P, 2, D])
        x_res = sb("x_res", [P, 2, D])
        y = sb("y", [P, 2, D])
        bn = sb("bn", [P, 2, 6])
        mv = sb("mv", [P, 2, 2])
        std = sb("std", [P, 2])
        eps = sb("eps", [P, 1])
        rstd = sb("rstd", [P, 2])
        xn = sb("xn", [P, 2, D])
        xc = sb("xc", [P, KD, B * C])
        z = sb("z", [P, B, HP])
        ez = sb("ez", [P, B, HP])
        ez1 = sb("ez1", [P, B, HP])
        beta = sb("beta", [P, B, HP])
        sq = sb("sq", [P, 2, HP, DH])
        ss = sb("ss", [P, B, HP])
        ssc = sb("ssc", [P, B, HP])
        kn = sb("kn", [P, B, HP])
        rkn = sb("rkn", [P, B, HP])
        K = sb("K", [P, B, HP, DH])
        V = sb("V", [P, B, HP, DH])
        QT = sb("QT", [P, HP, B, C])
        KT = sb("KT", [P, B, HP, C])
        PT = sb("PT", [P, B, HP, C])
        G = sb("G", [P, 2, HP, C])
        BT = sb("BT", [P, 2, LEVELS, HP, C])
        T = sb("T", [P, 2, HP, C])
        TT = sb("TT", [P, B, HP, C])
        X = sb("X", [P, 2, HP, C])
        N = sb("N", [P, B, HP, DH])
        R = sb("R", [P, B, HP, DH])
        U = sb("U", [P, B, HP, DH])
        OT = sb("OT", [P, HP, B, C])

        weights, state0 = sem("weights"), sem("state0")
        x_in, r_in, stored = sem("x_in"), sem("r_in"), sem("stored")
        stats, moments, std_ok, rstd_ok, xn_ok, xt_ps, xc_ok = map(
            sem, ("stats", "moments", "std_ok", "rstd_ok", "xn_ok", "xt_ps", "xc_ok"))
        beta_ps, z_ok, ez_ok, ez1_ok, beta_ok = map(sem, ("beta_ps", "z_ok", "ez_ok", "ez1_ok", "beta_ok"))
        k_ps, sq_ok, ss_ok, ssc_ok, kn_ok, rkn_ok, k_ok = map(
            sem, ("k_ps", "sq_ok", "ss_ok", "ssc_ok", "kn_ok", "rkn_ok", "k_ok"))
        v_ps, v_ok, q_ps, q_ok, kt_ps, kt_ok = map(sem, ("v_ps", "v_ok", "q_ps", "q_ok", "kt_ps", "kt_ok"))
        g_ps, g_ok, p_ps, p_ok, bt_ok = map(sem, ("g_ps", "g_ok", "p_ps", "p_ok", "bt_ok"))
        x_ps, xx_ok, tx_ps, t_ok, xt2_ps, tt_ok = map(sem, ("x_ps", "xx_ok", "tx_ps", "t_ok", "xt2_ps", "tt_ok"))
        r_ps, r_ok, u_ps, u_ok, o_ps, o_ok, n_ps, n_ok = map(
            sem, ("r_ps", "r_ok", "u_ps", "u_ok", "o_ps", "o_ok", "n_ps", "n_ok"))
        y_ps, y_ok = sem("y_ps"), sem("y_ok")

        ident = cst[:, C_ID:C_ID + P]
        ident2 = cst[:, C_ID2:C_ID2 + C]
        N_WEIGHTS = 8

        def over_pairs(m):
            return m.unsqueeze(1).broadcast_to([P, HP, C])

        def over_cols(v):
            return v.unsqueeze(2).broadcast_to([P, HP, C])

        def grid(b):
            return bank[b][:].rearrange("p (a c) -> p a c", a=HP)

        block = ctx.enter_context(nc.Block())

        @block.sync
        def _(sp):
            sp.dma_start(cst[:], consts[:, 0:C_TRI]).then_inc(weights, 16)
            sp.dma_start(wk[:], Wk.rearrange("(k p) n -> p k n", p=P)).then_inc(weights, 16)
            sp.dma_start(wbeta[:], Wbeta.rearrange("(k p) n -> p k n", p=P)).then_inc(weights, 16)
            for h in range(2):
                sp.dma_start(bbeta[C * h:C * h + C, :], b_beta.rearrange("(a h) -> h a", h=2)[h:h + 1, :]
                             .broadcast_to([C, HP]), allow_slow_non_contiguous=True).then_inc(weights, 16)
            sp.dma_start(wv[:], Wv.rearrange("(k p) n -> p k n", p=P)).then_inc(weights, 16)
            sp.dma_start(wq[:], Wq.rearrange("(k p) n -> p k n", p=P)).then_inc(weights, 16)
            sp.dma_start(wout[:], Wout.rearrange("(a p) n -> p a n", p=P)).then_inc(weights, 16)
            with sp.Fori(0, NCH) as c:
                sp.wait_ge(xn_ok, c * 2)
                for h in range(2):
                    sp.dma_start(x_ln[C * h:C * h + C],
                                 x[h::2, bass.ts(c, C), :].rearrange("b t d -> t b d")).then_inc(x_in, 16)
                sp.wait_ge(y_ok, c)
                for h in range(2):
                    sp.dma_start(x_res[C * h:C * h + C],
                                 x[h::2, bass.ts(c, C), :].rearrange("b t d -> t b d")).then_inc(r_in, 16)

        @block.gpsimd
        def _(pool):
            pool.wait_ge(weights, 16 * N_WEIGHTS)
            with pool.Fori(0, NCH) as c:
                for b in range(B):
                    j = b % 2
                    pool.wait_ge(g_ok, c * 4 + b + 1)
                    pool.wait_ge(x_ps, (c * 4 + max(b - 2, 0)) * LEVELS + (LEVELS if b >= 2 else 0))
                    for l in range(LEVELS):
                        m = cst[:, C_LVL + l * C:C_LVL + (l + 1) * C]
                        pool.tensor_tensor(BT[:, j, l], G[:, j], over_pairs(m), ALU.mult).then_inc(bt_ok, 1)
                pool.wait_ge(y_ok, c + 1)
                for h in range(2):
                    pool.dma_start(x1[h::2, bass.ts(c, C), :].rearrange("b t d -> t b d"),
                                   y[C * h:C * h + C]).then_inc(stored, 16)
            pool.wait_ge(stored, NCH * 32)

        @block.scalar
        def _(act):
            counts = Counts(act, "dl")
            with act.Fori(0, NCH) as c:
                act.wait_ge(moments, c * 2 + 2)
                act.activation(std[:], mv[:, :, 1], ACT.Sqrt, bias=eps[:, 0:1]).then_inc(std_ok, 1)
                act.wait_ge(xt_ps, c + 1)
                act.activation(xc[:].rearrange("p k t -> p (k t)"), bank[1][:], ACT.Copy).then_inc(xc_ok, 1)
                act.wait_ge(z_ok, c + 1)
                act.activation(ez[:], z[:], ACT.Exp, scale=-1.0).then_inc(ez_ok, 1)
                for b in range(B):
                    act.wait_ge(k_ps, c * 4 + b + 1)
                    if b >= 2:
                        act.wait_ge(ss_ok, c * 4 + b - 1)
                    act.activation(sq[:, b % 2], grid(b), ACT.Square).then_inc(sq_ok, 1)
                act.wait_ge(ssc_ok, c + 1)
                act.activation(kn[:], ssc[:], ACT.Sqrt).then_inc(kn_ok, 1)
                for b in range(B):
                    act.wait_ge(v_ps, c * 4 + b + 1)
                    act.activation(V[:, b], grid(4 + b), ACT.Copy).then_inc(v_ok, 1)
                for q in range(4):
                    act.wait_ge(q_ps, c * 4 + q + 1)
                    act.activation(QT[:, 2 * q:2 * q + 2].rearrange("p a b t -> p (a b t)"), bank[4 + q][:],
                                   ACT.Copy, scale=-1.0).then_inc(q_ok, 1)
                for b in range(B):
                    act.wait_ge(kt_ps, c * 4 + b + 1)
                    act.activation(KT[:, b], grid(b), ACT.Copy).then_inc(kt_ok, 1)
                for lanes in ((0, 1), (2, 3)):
                    for l in range(1, LEVELS):
                        for b in lanes:
                            act.wait_ge(x_ps, (c * 4 + lanes[0]) * LEVELS + 2 * l + b % 2 + 1)
                            act.activation(X[:, b % 2], grid(b % 2), ACT.Copy).then_inc(xx_ok, 1)
                for b in range(B):
                    act.wait_ge(o_ps, c * 4 + b + 1)
                    act.activation(OT[:, :, b], grid(b), ACT.Copy).then_inc(o_ok, 1)

        @block.vector
        def _(dve):
            counts = Counts(dve, "dl")
            dve.memset(N[:], 0.0).then_inc(state0, 1)
            dve.memset(eps[:], LN_EPS).then_inc(state0, 1)
            dve.wait_ge(weights, 16 * N_WEIGHTS)
            with dve.Fori(0, NCH) as c:
                dve.wait_ge(x_in, c * 32 + 32)
                for u in range(2):
                    dve.bn_stats(bn[:, u], x_ln[:, u]).then_inc(stats, 1)
                for u in range(2):
                    at = counts(c * 2 + u + 1)
                    dve.wait_ge(weights, 16 * N_WEIGHTS)
                    dve.wait_ge(stats, at[0])
                    dve.bn_aggr(mv[:, u], bn[:, u]).then_inc(moments, 1)
                dve.wait_ge(std_ok, c + 1)
                dve.reciprocal(rstd[:], std[:]).then_inc(rstd_ok, 1)
                dve.wait_ge(rstd_ok, c + 1)
                for u in range(2):
                    dve.tensor_scalar(xn[:, u], x_ln[:, u], mv[:, u, 0:1], rstd[:, u:u + 1],
                                      ALU.subtract, ALU.mult).then_inc(xn_ok, 1)
                dve.wait_ge(beta_ps, c + 1)
                dve.tensor_tensor(z[:], bank[7][:, 0:B * HP].rearrange("p (b a) -> p b a", b=B),
                                  bbeta[:].unsqueeze(1).broadcast_to([P, B, HP]), ALU.add).then_inc(z_ok, 1)
                dve.wait_ge(ez_ok, c + 1)
                dve.tensor_scalar(ez1[:], ez[:], 1.0, None, ALU.add).then_inc(ez1_ok, 1)
                dve.wait_ge(ez1_ok, c + 1)
                dve.reciprocal(beta[:], ez1[:]).then_inc(beta_ok, 1)
                for b in range(B):
                    dve.wait_ge(sq_ok, c * 4 + b + 1)
                    dve.tensor_reduce(ss[:, b], sq[:, b % 2], AX.X, ALU.add).then_inc(ss_ok, 1)
                dve.wait_ge(ss_ok, c * 4 + 4)
                dve.tensor_scalar(ssc[:], ss[:], SQ_EPS, None, ALU.max).then_inc(ssc_ok, 1)
                dve.wait_ge(kn_ok, c + 1)
                dve.reciprocal(rkn[:], kn[:]).then_inc(rkn_ok, 1)
                dve.wait_ge(rkn_ok, c + 1)
                for b in range(B):
                    dve.tensor_tensor(K[:, b], grid(b), over_cols(rkn[:, b]), ALU.mult).then_inc(k_ok, 1)
                dve.wait_ge(beta_ok, c + 1)
                for lanes in ((0, 1), (2, 3)):
                    for b in lanes:
                        j = b % 2
                        dve.wait_ge(g_ps, c * 4 + b + 1)
                        if b >= 2:
                            dve.wait_ge(bt_ok, (c * 4 + b - 1) * LEVELS)
                        dve.tensor_tensor(G[:, j], grid(j), over_cols(beta[:, b]), ALU.mult).then_inc(g_ok, 1)
                    for b in lanes:
                        j = b % 2
                        dve.wait_ge(p_ps, c * 4 + b + 1)
                        dve.tensor_tensor(PT[:, b], grid(6 + j), over_pairs(cst[:, C_CAUSAL:C_CAUSAL + C]),
                                          ALU.mult).then_inc(p_ok, 1)
                    for b in lanes:
                        j = b % 2
                        dve.wait_ge(bt_ok, (c * 4 + b) * LEVELS + 1)
                        dve.tensor_tensor(TT[:, b], over_pairs(ident2), BT[:, j, 0], ALU.subtract).then_inc(tt_ok, 1)
                        dve.wait_ge(x_ps, (c * 4 + lanes[0]) * LEVELS + j + 1)
                        dve.tensor_tensor(T[:, j], over_pairs(ident2), grid(j), ALU.subtract).then_inc(t_ok, 1)
                    for l in range(1, LEVELS):
                        for b in lanes:
                            j = b % 2
                            n = (c * 4 + lanes[0]) * LEVELS + 2 * l + j
                            if l < LEVELS - 1:
                                dve.wait_ge(tx_ps, (c * 4 + lanes[0]) * (LEVELS - 2) + 2 * (l - 1) + j + 1)
                                dve.wait_ge(t_ok, (c * 4 + lanes[0]) * (LEVELS - 1) + 2 * l + j - 1)
                                dve.tensor_tensor(T[:, j], T[:, j], grid(2 + j), ALU.subtract).then_inc(t_ok, 1)
                            dve.wait_ge(xt2_ps, (c * 4 + lanes[0]) * (LEVELS - 1) + 2 * (l - 1) + j + 1)
                            dve.wait_ge(tt_ok, n - 1)
                            dve.tensor_tensor(TT[:, b], TT[:, b], grid(4 + j), ALU.subtract).then_inc(tt_ok, 1)
                for b in range(B):
                    dve.wait_ge(r_ps, c * 4 + b + 1)
                    dve.tensor_tensor(R[:, b], grid(b), V[:, b], ALU.add).then_inc(r_ok, 1)
                for b in range(B):
                    dve.wait_ge(u_ps, c * 4 + b + 1)
                    dve.tensor_tensor(U[:, b], grid(4 + b), over_cols(beta[:, b]), ALU.mult).then_inc(u_ok, 1)
                for b in range(B):
                    dve.wait_ge(n_ps, c * 4 + b + 1)
                    dve.tensor_tensor(N[:, b], N[:, b], grid(4 + b), ALU.subtract).then_inc(n_ok, 1)
                dve.wait_ge(y_ps, c + 1)
                dve.wait_ge(r_in, c * 32 + 32)
                dve.wait_ge(stored, c * 32)
                dve.tensor_tensor(y[:].rearrange("p u d -> p (u d)"), bank[0][:],
                                  x_res[:].rearrange("p u d -> p (u d)"), ALU.add).then_inc(y_ok, 1)

        @block.tensor
        def _(pe):
            counts = Counts(pe, "dl")
            def pairs(out, lhsT, rhs):
                for a in range(HP):
                    for h in range(2):
                        rows = slice(C * h, C * h + C)
                        last = pe.matmul(out[rows, a], lhsT(rows, a), rhs(rows, a), start=True, stop=True)
                return last

            def natural(out, w, b):
                wh = w[:].rearrange("p k (a h d) -> p k h a d", h=2, d=DH)
                for k in range(KD):
                    for h in range(2):
                        last = pe.matmul(out[C * h:C * h + C], xc[:, k, C * b:C * b + C], wh[:, k, h],
                                         start=(k == 0), stop=(k == KD - 1))
                return last

            pe.wait_ge(weights, 16 * N_WEIGHTS)
            pe.wait_ge(state0, 2)
            with pe.Fori(0, NCH) as c:
                for u in range(2):
                    pe.wait_ge(xn_ok, c * 2 + u + 1)
                    for k in range(KD):
                        last = pe.transpose(bank[1][:, k * 256 + u * P:k * 256 + u * P + P],
                                            xn[:, u, k * P:k * P + P], ident)
                last.then_inc(xt_ps, 1)
                pe.wait_ge(xc_ok, c + 1)
                pe.wait_ge(n_ok, c * 4)
                pe.wait_ge(y_ok, c)
                wbh = wbeta[:].rearrange("p k (a h) -> p k h a", h=2)
                for b in range(B):
                    for h in range(2):
                        for k in range(KD):
                            last = pe.matmul(bank[7][C * h:C * h + C, b * HP:(b + 1) * HP],
                                             xc[:, k, C * b:C * b + C], wbh[:, k, h],
                                             start=(k == 0), stop=(k == KD - 1))
                last.then_inc(beta_ps, 1)
                for b in range(B):
                    natural(grid(b), wk, b).then_inc(k_ps, 1)
                for b in range(B):
                    if b == 3:
                        pe.wait_ge(z_ok, c + 1)
                    natural(grid(4 + b), wv, b).then_inc(v_ps, 1)
                for q in range(4):
                    pe.wait_ge(v_ok, c * 4 + q + 1)
                    for a in (0, 1):
                        for k in range(KD):
                            m = (2 * q + a) * P
                            last = pe.matmul(bank[4 + q][:, a * 256:a * 256 + 256], wq[:, k, m:m + P], xc[:, k],
                                             start=(k == 0), stop=(k == KD - 1))
                    last.then_inc(q_ps, 1)
                for b in range(B):
                    at = counts(c * 4 + b + 1)
                    pe.wait_ge(weights, 16 * N_WEIGHTS)
                    pe.wait_ge(k_ok, at[0])
                    pairs(grid(b), lambda r, a: K[r, b, a], lambda r, a: ident2[r]).then_inc(kt_ps, 1)
                for lanes in ((0, 1), (2, 3)):
                    for b in lanes:
                        j = b % 2
                        at = counts(c * 4 + max(b, 1) + 1)
                        pe.wait_ge(weights, 16 * N_WEIGHTS)
                        pe.wait_ge(kt_ok, at[0])
                        pairs(grid(j), lambda r, a: KT[r, b, a], lambda r, a: KT[r, b, a]).then_inc(g_ps, 1)
                    for b in lanes:
                        j = b % 2
                        at = counts(c * 4 + 4, c * 4 + max(b - 1, 0))
                        pe.wait_ge(weights, 16 * N_WEIGHTS)
                        pe.wait_ge(q_ok, at[0])
                        pe.wait_ge(p_ok, at[1])
                        pairs(grid(6 + j), lambda r, a: KT[r, b, a], lambda r, a: QT[r, a, b]).then_inc(p_ps, 1)
                    for l in range(LEVELS):
                        for b in lanes:
                            j = b % 2
                            if l == 0:
                                at = counts((c * 4 + b) * LEVELS + 1, c * 4 + b + 1)
                                pe.wait_ge(weights, 16 * N_WEIGHTS)
                                pe.wait_ge(bt_ok, at[0])
                                pe.wait_ge(g_ok, at[1])
                            else:
                                first = c * 4 + lanes[0]
                                at = counts((c * 4 + b) * LEVELS + l + 1, first * (LEVELS - 1) + 2 * (l - 1) + j + 1,
                                            first * (LEVELS - 1) + max(2 * (l - 2) + j + 1, 0))
                                pe.wait_ge(weights, 16 * N_WEIGHTS)
                                pe.wait_ge(bt_ok, at[0])
                                pe.wait_ge(t_ok, at[1])
                                pe.wait_ge(xx_ok, at[2])
                            src = (lambda r, a: T[r, j, a]) if l else (lambda r, a: ident2[r])
                            pairs(grid(j), lambda r, a: BT[r, j, l, a], src).then_inc(x_ps, 1)
                        if l == 0:
                            continue
                        for b in lanes:
                            j = b % 2
                            at = counts((c * 4 + lanes[0]) * (LEVELS - 1) + 2 * (l - 1) + j + 1,
                                        (c * 4 + lanes[0]) * LEVELS + 2 * (l - 1) + j + 1)
                            pe.wait_ge(weights, 16 * N_WEIGHTS)
                            pe.wait_ge(xx_ok, at[0])
                            pe.wait_ge(tt_ok, at[1])
                            if l < LEVELS - 1:
                                pairs(grid(2 + j), lambda r, a: TT[r, b, a], lambda r, a: X[r, j, a]).then_inc(tx_ps, 1)
                            pairs(grid(4 + j), lambda r, a: X[r, j, a], lambda r, a: TT[r, b, a]).then_inc(xt2_ps, 1)
                at = counts(c * 4 * LEVELS + 4 * LEVELS, c * 4 + 4)
                pe.wait_ge(weights, 16 * N_WEIGHTS)
                pe.wait_ge(tt_ok, at[0])
                pe.wait_ge(p_ok, at[1])
                for b in range(B):
                    pairs(grid(b), lambda r, a: KT[r, b, a], lambda r, a: N[r, b, a]).then_inc(r_ps, 1)
                for b in range(B):
                    at = counts(c * 4 + b + 1)
                    pe.wait_ge(weights, 16 * N_WEIGHTS)
                    pe.wait_ge(r_ok, at[0])
                    pairs(grid(4 + b), lambda r, a: TT[r, b, a], lambda r, a: R[r, b, a]).then_inc(u_ps, 1)
                for b in range(B):
                    at = counts(c * 4 + b + 1)
                    pe.wait_ge(weights, 16 * N_WEIGHTS)
                    pe.wait_ge(u_ok, at[0])
                    for a in range(HP):
                        for h in range(2):
                            r = slice(C * h, C * h + C)
                            pe.matmul(grid(b)[r, a], N[r, b, a], QT[r, a, b], start=True, stop=False)
                            last = pe.matmul(grid(b)[r, a], U[r, b, a], PT[r, b, a], start=False, stop=True)
                    last.then_inc(o_ps, 1)
                    pairs(grid(4 + b), lambda r, a: K[r, b, a], lambda r, a: U[r, b, a]).then_inc(n_ps, 1)
                pe.wait_ge(o_ok, c * 4 + 4)
                for u in range(2):
                    for a in range(HP):
                        last = pe.matmul(bank[0][:, u * D:(u + 1) * D],
                                         OT[:, a, 2 * u:2 * u + 2].rearrange("p b t -> p (b t)"), wout[:, a],
                                         start=(a == 0), stop=(a == HP - 1))
                last.then_inc(y_ps, 1)
    clear(nc, held)


E_N = 8
F = 1024
NT = B * S // P
GT = 4


def expert_layer(nc, name, consts, x, Wr, br, W1, b1, W2, b2, cap, keeps_dropped, out, slots, answers):
    nrow = cap // P if cap % P == 0 else 2
    rp = cap // nrow
    nhalf = 2 if cap > 512 else 1
    half = cap // nhalf
    FT = F // P
    biased = b1 is not None
    last_slot = E_N * cap - 1

    held = []
    with ExitStack() as ctx:
        def sb(n, shape, dt=F32):
            return ctx.enter_context(nc.sbuf_tensor(f"{name}_{n}", shape, dt))

        def sem(n):
            held.append(nc.alloc_semaphore(name=f"{name}_{n}"))
            return held[-1]

        bank = [ctx.enter_context(nc.psum_tensor(f"{name}_bank{i}", [P, 512], F32)) for i in range(8)]

        cst = sb("cst", [P, C_ALL])
        wr = sb("wr", [P, KD, E_N])
        bias_r = sb("bias_r", [P, E_N])
        x_all = sb("x_all", [P, NT, D])
        xn_all = sb("xn_all", [P, NT, D])
        xn = sb("xn", [P, GT, D])
        bn = sb("bn", [P, GT, 6])
        mv = sb("mv", [P, GT, 2])
        eps = sb("eps", [P, 1])
        std = sb("std", [P, GT])
        rstd = sb("rstd", [P, GT])
        xT = sb("xT", [P, GT, KD, P])
        logit = sb("logit", [P, NT, E_N])
        route = [sb(f"route{i}", [P, NT, E_N]) for i in range(3)]
        per_token = [sb(f"token{i}", [P, NT]) for i in range(12)]
        reset = sb("reset", [P, E_N, NT])
        total = sb("total", [P, E_N, NT])
        running = sb("running", [P, E_N, NT])
        slot_in = sb("slot_in", [P, NT], I32)
        slot_out = sb("slot_out", [P, NT], I32)
        zero = sb("zero", [P, 4 * D])
        w1 = sb("w1", [P, 2, KD, F])
        w2 = sb("w2", [P, 2, FT, D])
        rows = sb("rows", [rp, 2, nrow, D])
        rowsT = sb("rowsT", [P, KD, cap])
        hid = sb("hid", [P, FT, cap])
        ans = sb("ans", [rp, nrow, D])
        if biased:
            b1_sb = sb("b1", [P, E_N, FT])
            b2_sb = sb("b2", [1, E_N, D])
        got = sb("got", [P, NT, D])

        const_in, x_in, zeroed, zero_ok, eps_ok = map(sem, ("const_in", "x_in", "zeroed", "zero_ok", "eps_ok"))
        w_in = [sem("w_in0"), sem("w_in1")]
        stats, moments, std_ok, rstd_ok, xn_ok, xn_kept, xT_ps, xT_ok, lg_ps, lg_ok = map(
            sem, ("stats", "moments", "std_ok", "rstd_ok", "xn_ok", "xn_kept", "xT_ps", "xT_ok", "lg_ps", "lg_ok"))
        chain, ex_ok, once_ok, count_ps, slot_ok = map(sem, ("chain", "ex_ok", "once_ok", "count_ps", "slot_ok"))
        sent = sem("sent")
        rows_in, rT_ps, rT_ok, h_ps, h_act, h_dve, a_ps, a_ok, a_out = map(
            sem, ("rows_in", "rT_ps", "rT_ok", "h_ps", "h_act", "h_dve", "a_ps", "a_ok", "a_out"))
        mixed, out_ok, stored = map(sem, ("mixed", "out_ok", "stored"))
        fetched = [sem(f"fetched{g}") for g in range(NT // GT)]

        ident = cst[:, C_ID:C_ID + P]
        N_CONST = 2 + (3 if biased else 0)
        x_t = x.rearrange("b s d -> (b s) d").rearrange("(n p) d -> p n d", p=P)
        out_t = out.rearrange("b s d -> (b s) d").rearrange("(n p) d -> p n d", p=P)
        slots_t = slots.rearrange("(e j p) d -> e p j d", j=nrow, p=rp)
        answers_t = answers.rearrange("(e j p) d -> e p j d", j=nrow, p=rp)
        blocks = [(f, q) for f in range(FT) for q in range(nhalf)]
        NB = len(blocks)
        on_act = NB if biased else NB // 2

        def over_experts(v):
            return v.unsqueeze(2).broadcast_to([P, NT, E_N])

        block = ctx.enter_context(nc.Block())

        @block.sync
        def _(sp):
            sp.dma_start(cst[:], consts).then_inc(const_in, 16)
            sp.dma_start(wr[:], Wr.rearrange("(k p) n -> p k n", p=P)).then_inc(const_in, 16)
            if biased:
                sp.dma_start(bias_r[:], br.unsqueeze(0).broadcast_to([P, E_N])).then_inc(const_in, 16)
                sp.dma_start(b2_sb[:], b2.unsqueeze(0)).then_inc(const_in, 16)
                sp.dma_start(b1_sb[:], b1.rearrange("e (f p) -> p e f", p=P),
                             allow_slow_non_contiguous=True).then_inc(const_in, 16)
            with sp.Fori(0, NT // GT) as g:
                sp.wait_ge(x_in, g * 16)
                sp.dma_start(x_all[:, bass.ts(g, GT)], x_t[:, bass.ts(g, GT)]).then_inc(x_in, 16)
            sp.wait_ge(zero_ok, 1)
            per = E_N * cap // P // 10 * D * 2
            zrow = slots.rearrange("(p r) d -> p (r d)", p=P)
            step = 4 * D if zrow.shape[1] % (4 * D) == 0 else 2 * D
            for i in range(zrow.shape[1] // step):
                sp.dma_start(zrow[:, i * step:(i + 1) * step], zero[:, 0:step]).then_inc(zeroed, 16)
            sp.wait_ge(sent, 16 * NT)
            with sp.Fori(0, E_N // 2) as i:
                for u in range(2):
                    e = i * 2 + u
                    sp.wait_ge(a_ps, (i * 2 + u) * nrow if u == 0 else i * 2 * nrow)
                    sp.dma_start(rows[:, u], slots_t[e]).then_inc(rows_in, 16)
                    sp.wait_ge(a_ok, (i * 2 + u + 1) * nrow)
                    sp.dma_start(answers_t[e], ans[:]).then_inc(a_out, 16)
            for g in range(NT // GT):
                sp.wait_ge(out_ok, GT * (g + 1))
                sp.dma_start(out_t[:, g * GT:(g + 1) * GT], got[:, g * GT:(g + 1) * GT]).then_inc(stored, 16)
            sp.wait_ge(stored, 16 * (NT // GT))

        @block.gpsimd
        def _(pool):
            pool.memset(zero[:], 0.0).then_inc(zero_ok, 1)
            n_zero = slots.shape[0] // P * D // (4 * D if slots.shape[0] // P * D % (4 * D) == 0 else 2 * D)
            pool.wait_ge(slot_ok, 2)
            pool.wait_ge(xn_kept, NT // GT)
            pool.wait_ge(zeroed, 16 * n_zero)
            for t in range(NT):
                pool.indirect_dma_start(out=slots, out_offset=bass.IndirectOffsetOnAxis(ap=slot_in[:, t:t + 1], axis=0),
                                        in_=xn_all[:, t], in_offset=None, bounds_check=last_slot,
                                        oob_is_err=False).then_inc(sent, 16)
            pool.wait_ge(a_out, 16 * E_N)
            for t in range(NT):
                pool.indirect_dma_start(out=got[:, t], out_offset=None, in_=answers,
                                        in_offset=bass.IndirectOffsetOnAxis(ap=slot_out[:, t:t + 1], axis=0),
                                        bounds_check=last_slot, oob_is_err=False).then_inc(fetched[t // GT], 16)

        @block.scalar
        def _(act):
            counts = Counts(act, name)
            act.wait_ge(eps_ok, 1)
            with act.Fori(0, NT // GT) as g:
                act.wait_ge(moments, g * GT + GT)
                act.activation(std[:], mv[:, :, 1], ACT.Sqrt, bias=eps[:, 0:1]).then_inc(std_ok, 1)
                at = counts(g * GT + GT)
                act.wait_ge(eps_ok, 1)
                act.wait_ge(xn_ok, at[0])
                act.activation(xn_all[:, bass.ts(g, GT)], xn[:], ACT.Copy).then_inc(xn_kept, 1)
                for u in range(2):
                    act.wait_ge(xT_ps, g * 2 + u + 1)
                    act.activation(xT[:, 2 * u:2 * u + 2].rearrange("p j k t -> p (j k t)"), bank[u][:],
                                   ACT.Copy).then_inc(xT_ok, 1)
            act.wait_ge(chain, 2)
            act.activation(route[1][:], route[0][:], ACT.Exp).then_inc(ex_ok, 1)
            with act.Fori(0, E_N // 2) as i:
                for u in range(2):
                    e = i * 2 + u
                    act.wait_ge(a_ps, i * 2 * nrow)
                    act.dma_start(w1[:, u], W1[e].rearrange("(k p) f -> p k f", p=P)).then_inc(w_in[u], 16)
                    act.dma_start(w2[:, u], W2[e].rearrange("(f p) d -> p f d", p=P)).then_inc(w_in[u], 16)
                for u in range(2):
                    e = i * 2 + u
                    for n, (f, q) in enumerate(blocks):
                        if not biased and n % 2:
                            continue
                        act.wait_ge(h_ps, e * NB + n + 1)
                        dst = hid[:, f, q * half:(q + 1) * half]
                        if biased:
                            act.activation(dst, bank[2 + n % 4][:, 0:half], ACT.Gelu_apprx_tanh,
                                           bias=b1_sb[:, e, f:f + 1]).then_inc(h_act, 1)
                        else:
                            act.activation(dst, bank[2 + n % 4][:, 0:half], ACT.Relu).then_inc(h_act, 1)

        @block.vector
        def _(dve):
            counts = Counts(dve, name)
            dve.memset(eps[:], LN_EPS).then_inc(eps_ok, 1)
            dve.memset(reset[:], 1.0).then_inc(once_ok, 1)
            dve.wait_ge(once_ok, 1)
            dve.memset(reset[:, :, 0:1], 0.0).then_inc(once_ok, 1)
            dve.wait_ge(const_in, 16 * N_CONST)
            with dve.Fori(0, NT // GT) as g:
                dve.wait_ge(x_in, g * 16 + 16)
                for j in range(GT):
                    dve.bn_stats(bn[:, j], x_all[:, g * GT + j]).then_inc(stats, 1)
                for j in range(GT):
                    at = counts(g * GT + j + 1)
                    dve.wait_ge(const_in, 16 * N_CONST)
                    dve.wait_ge(stats, at[0])
                    dve.bn_aggr(mv[:, j], bn[:, j]).then_inc(moments, 1)
                dve.wait_ge(std_ok, g + 1)
                dve.reciprocal(rstd[:], std[:]).then_inc(rstd_ok, 1)
                dve.wait_ge(rstd_ok, g + 1)
                dve.wait_ge(xn_kept, g)
                dve.wait_ge(xT_ps, g * 2)
                for j in range(GT):
                    dve.tensor_scalar(xn[:, j], x_all[:, g * GT + j], mv[:, j, 0:1], rstd[:, j:j + 1],
                                      ALU.subtract, ALU.mult).then_inc(xn_ok, 1)
                dve.wait_ge(lg_ps, g + 1)
                if biased:
                    dve.tensor_tensor(logit[:, bass.ts(g, GT)],
                                      bank[6][:, 0:GT * E_N].rearrange("p (j e) -> p j e", j=GT),
                                      bias_r[:].unsqueeze(1).broadcast_to([P, GT, E_N]), ALU.add).then_inc(lg_ok, 1)
                else:
                    dve.tensor_copy(logit[:, bass.ts(g, GT)],
                                    bank[6][:, 0:GT * E_N].rearrange("p (j e) -> p j e", j=GT)).then_inc(lg_ok, 1)
            n = [0]

            def step(ins):
                n[0] += 1
                ins.then_inc(chain, 1)
                dve.wait_ge(chain, n[0])

            top, esum, prob, rank, pos, kept, factor, dropped, slot, sin, sout, _ = (v[:] for v in per_token)
            shifted, mask, work = (r[:] for r in route)
            dve.wait_ge(lg_ok, NT // GT)
            step(dve.tensor_reduce(top, logit[:], AX.X, ALU.max))
            step(dve.tensor_tensor(shifted, logit[:], over_experts(top), ALU.subtract))
            dve.wait_ge(ex_ok, 1)
            step(dve.tensor_reduce(esum, mask, AX.X, ALU.add))
            step(dve.reciprocal(prob, esum))
            step(dve.tensor_tensor(work, logit[:], over_experts(top), ALU.is_equal))
            step(dve.tensor_tensor(mask, work, cst[:, C_RANK:C_RANK + E_N].unsqueeze(1).broadcast_to([P, NT, E_N]),
                                   ALU.mult))
            step(dve.tensor_reduce(rank, mask, AX.X, ALU.max))
            step(dve.tensor_tensor(work, mask, over_experts(rank), ALU.is_equal))
            dve.wait_ge(count_ps, 2)
            step(dve.tensor_copy(total[:], bank[1][:, 0:NT * E_N].rearrange("p (t e) -> p e t", e=E_N)))
            step(dve.tensor_tensor_scan(running[:].rearrange("p e t -> p (e t)"), reset[:].rearrange("p e t -> p (e t)"),
                                        total[:].rearrange("p e t -> p (e t)"), 0.0, ALU.mult, ALU.add))
            step(dve.tensor_tensor(running[:], running[:], total[:], ALU.subtract))
            step(dve.tensor_tensor(shifted, bank[0][:, 0:NT * E_N].rearrange("p (t e) -> p t e", e=E_N),
                                   running[:].rearrange("p e t -> p t e"), ALU.add))
            step(dve.tensor_tensor(mask, shifted, work, ALU.mult))
            step(dve.tensor_reduce(pos, mask, AX.X, ALU.add))
            step(dve.tensor_scalar(kept, pos, float(cap), None, ALU.is_le))
            step(dve.tensor_scalar(dropped, kept, -1.0, 1.0, ALU.mult, ALU.add))
            step(dve.tensor_tensor(factor, kept, prob, ALU.mult))
            step(dve.tensor_scalar(slot, rank, -float(cap), float(E_N * cap - 1), ALU.mult, ALU.add))
            step(dve.tensor_tensor(slot, slot, pos, ALU.add))
            step(dve.tensor_scalar(sin, dropped, float(2 * E_N * cap), None, ALU.mult))
            step(dve.tensor_tensor(sin, sin, slot, ALU.add))
            step(dve.tensor_scalar(sout, slot, float(last_slot), None, ALU.min))
            dve.tensor_copy(slot_in[:], sin).then_inc(slot_ok, 1)
            dve.tensor_copy(slot_out[:], sout).then_inc(slot_ok, 1)

            with dve.Fori(0, E_N // 2) as i:
                for u in range(2):
                    e = i * 2 + u
                    for j in range(nrow):
                        dve.wait_ge(rT_ps, e * nrow + j + 1)
                        dve.tensor_copy(rowsT[:, :, j * rp:(j + 1) * rp],
                                        bank[j % 2][:, 0:KD * rp].rearrange("p (k t) -> p k t", k=KD)).then_inc(rT_ok, 1)
                    if not biased:
                        for n_, (f, q) in enumerate(blocks):
                            if n_ % 2 == 0:
                                continue
                            dve.wait_ge(h_ps, e * NB + n_ + 1)
                            dve.tensor_scalar(hid[:, f, q * half:(q + 1) * half], bank[2 + n_ % 4][:, 0:half],
                                              0.0, None, ALU.max).then_inc(h_dve, 1)
                    dve.wait_ge(a_out, e * 16)
                    for j in range(nrow):
                        dve.wait_ge(a_ps, e * nrow + j + 1)
                        dve.tensor_copy(ans[:, j], bank[6 + j % 2][0:rp, 0:D]).then_inc(a_ok, 1)
            for t in range(NT):
                if t % GT == 0:
                    dve.wait_ge(fetched[t // GT], 16 * GT)
                if keeps_dropped:
                    dve.scalar_tensor_tensor(got[:, t], got[:, t], factor[:, t:t + 1], x_all[:, t],
                                             ALU.mult, ALU.add).then_inc(mixed, 1)
                    dve.wait_ge(mixed, t + 1)
                    dve.scalar_tensor_tensor(got[:, t], xn_all[:, t], dropped[:, t:t + 1], got[:, t],
                                             ALU.mult, ALU.add).then_inc(out_ok, 1)
                else:
                    dve.scalar_tensor_tensor(got[:, t], got[:, t], factor[:, t:t + 1], x_all[:, t],
                                             ALU.mult, ALU.add).then_inc(out_ok, 1)

        @block.tensor
        def _(pe):
            counts = Counts(pe, name)
            pe.wait_ge(const_in, 16 * N_CONST)
            with pe.Fori(0, NT // GT) as g:
                for u in range(2):
                    pe.wait_ge(xn_ok, g * GT + 2 * u + 2)
                    pe.wait_ge(xT_ok, g * 2)
                    for j in range(2):
                        for k in range(KD):
                            last = pe.transpose(bank[u][:, (j * KD + k) * P:(j * KD + k + 1) * P],
                                                xn[:, 2 * u + j, k * P:(k + 1) * P], ident)
                    last.then_inc(xT_ps, 1)
                pe.wait_ge(xT_ok, g * 2 + 2)
                pe.wait_ge(lg_ok, g)
                for j in range(GT):
                    for k in range(KD):
                        last = pe.matmul(bank[6][:, j * E_N:(j + 1) * E_N], xT[:, j, k], wr[:, k],
                                         start=(k == 0), stop=(k == KD - 1))
                last.then_inc(lg_ps, 1)
            pe.wait_ge(chain, 8)
            oh = route[2][:].rearrange("p t e -> p (t e)")
            pe.matmul(bank[0][:, 0:NT * E_N], cst[:, C_TRI:C_TRI + P], oh, start=True, stop=True).then_inc(count_ps, 1)
            pe.matmul(bank[1][:, 0:NT * E_N], cst[:, C_ONE:C_ONE + P], oh, start=True, stop=True).then_inc(count_ps, 1)
            pe.wait_ge(slot_ok, 2)
            with pe.Fori(0, E_N // 2) as i:
                for u in range(2):
                    e = i * 2 + u
                    pe.wait_ge(rows_in, e * 16 + 16)
                    for j in range(nrow):
                        pe.wait_ge(rT_ok, e * nrow + j - 1 if j >= 2 else e * nrow)
                        for k in range(KD):
                            last = pe.transpose(bank[j % 2][:, k * rp:(k + 1) * rp],
                                                rows[:, u, j, k * P:(k + 1) * P], ident[0:rp, 0:rp])
                        last.then_inc(rT_ps, 1)
                    pe.wait_ge(rT_ok, (e + 1) * nrow)
                    pe.wait_ge(w_in[u], i * 32 + 32)
                    for n, (f, q) in enumerate(blocks):
                        if biased:
                            pe.wait_ge(h_act, e * NB + max(n - 3, 0))
                        elif n % 2 == 0:
                            pe.wait_ge(h_act, e * (NB // 2) + max(n // 2 - 1, 0))
                        else:
                            pe.wait_ge(h_dve, e * (NB // 2) + max(n // 2 - 1, 0))
                        for k in range(KD):
                            last = pe.matmul(bank[2 + n % 4][:, 0:half], w1[:, u, k, f * P:(f + 1) * P],
                                             rowsT[:, k, q * half:(q + 1) * half],
                                             start=(k == 0), stop=(k == KD - 1))
                        last.then_inc(h_ps, 1)
                    for j in range(nrow):
                        at = counts(e * nrow + max(j - 1, 0), (e + 1) * on_act, (e + 1) * (NB - on_act))
                        pe.wait_ge(const_in, 16 * N_CONST)
                        pe.wait_ge(a_ok, at[0])
                        if j == 0:
                            pe.wait_ge(h_act, at[1])
                            pe.wait_ge(h_dve, at[2])
                        if biased:
                            pe.matmul(bank[6 + j % 2][0:rp, 0:D], cst[0:1, C_ONE:C_ONE + rp], b2_sb[:, e],
                                      start=True, stop=False)
                        for f in range(FT):
                            last = pe.matmul(bank[6 + j % 2][0:rp, 0:D], hid[:, f, j * rp:(j + 1) * rp],
                                             w2[:, u, f], start=(f == 0 and not biased), stop=(f == FT - 1))
                        last.then_inc(a_ps, 1)
    clear(nc, held)


TB = S // P


def attention_layer(nc, consts, x, WqT, WkT, WvT, bq, bk, bv, WoT, bo, out):
    QH = S // 512
    UNITS = 2 * TB
    held = []
    with ExitStack() as ctx:
        def sb(n, shape, dt=F32):
            return ctx.enter_context(nc.sbuf_tensor(f"at_{n}", shape, dt))

        def sem(n):
            held.append(nc.alloc_semaphore(name=f"at_{n}"))
            return held[-1]

        score = [ctx.enter_context(nc.psum_tensor(f"at_score{i}", [P, S], F32)) for i in range(2)]
        mix = ctx.enter_context(nc.psum_tensor("at_mix", [P, S], F32))
        bank = [ctx.enter_context(nc.psum_tensor(f"at_bank{i}", [P, 512], F32)) for i in range(2)]

        cst = sb("cst", [P, C_ONE + P])
        w = sb("w", [P, 2, 3, KD, P])
        wo = sb("wo", [P, HP, D])
        b_q, b_k = sb("b_q", [P, HP]), sb("b_k", [P, HP])
        b_v = sb("b_v", [P, H * DH])
        b_o = sb("b_o", [1, D])
        x_all = sb("x_all", [P, TB, D])
        xn = sb("xn", [P, TB, D])
        bn = sb("bn", [P, TB, 6])
        mv = sb("mv", [P, TB, 2])
        eps = sb("eps", [P, 1])
        std = sb("std", [P, TB])
        rstd = sb("rstd", [P, TB])
        xT = sb("xT", [P, KD, S])
        Q = sb("Q", [P, 2, S])
        K = sb("K", [P, S])
        V = sb("V", [P, TB, P])
        E = sb("E", [P, 4, S])
        top, ntop, esum, rsum = (sb(n, [P, 4]) for n in ("top", "ntop", "esum", "rsum"))
        Vs = sb("Vs", [P, 4, DH])
        CT = sb("CT", [P, HP, S])
        y = sb("y", [P, TB, D])

        const_in, zero_ok, x_in = map(sem, ("const_in", "zero_ok", "x_in"))
        y_out = sem("y_out")
        w_in = [sem("w_in0"), sem("w_in1")]
        stats, moments, std_ok, rstd_ok, xn_ok, xT_ps, xT_ok = map(
            sem, ("stats", "moments", "std_ok", "rstd_ok", "xn_ok", "xT_ps", "xT_ok"))
        q_ps, q_ok, k_ps, k_ok, v_ps, v_ok = map(sem, ("q_ps", "q_ok", "k_ps", "k_ok", "v_ps", "v_ok"))
        s_ps, top_ok, ntop_ok, e_ok, rsum_ok, vs_ok, c_ps, ct_ok = map(
            sem, ("s_ps", "top_ok", "ntop_ok", "e_ok", "rsum_ok", "vs_ok", "c_ps", "ct_ok"))
        o_ps, y_ok = sem("o_ps"), sem("y_ok")

        ident = cst[:, C_ID:C_ID + P]
        N_CONST = 6
        x_t = x.rearrange("b (n p) d -> b p n d", p=P)
        out_t = out.rearrange("b (n p) d -> b p n d", p=P)

        block = ctx.enter_context(nc.Block())

        @block.sync
        def _(sp):
            sp.dma_start(cst[:], consts[:, 0:C_ONE + P]).then_inc(const_in, 16)
            sp.dma_start(b_q[:], bq.rearrange("(a p) -> p a", p=P), allow_slow_non_contiguous=True).then_inc(const_in, 16)
            sp.dma_start(b_k[:], bk.rearrange("(a p) -> p a", p=P), allow_slow_non_contiguous=True).then_inc(const_in, 16)
            sp.dma_start(b_v[:], bv.unsqueeze(0).broadcast_to([P, H * DH])).then_inc(const_in, 16)
            sp.dma_start(b_o[:], bo.unsqueeze(0)).then_inc(const_in, 16)
            sp.dma_start(wo[:], WoT.rearrange("(a p) d -> p a d", p=P)).then_inc(const_in, 16)
            with sp.Fori(0, B) as b:
                sp.wait_ge(y_ok, b * TB)
                sp.dma_start(x_all[:], x_t[b]).then_inc(x_in, 16)
                with sp.Fori(0, HP // 2) as a2:
                    for u in range(2):
                        a = a2 * 2 + u
                        sp.wait_ge(v_ps, (b * HP + a2 * 2) * 2)
                        for i, wt in enumerate((WqT, WkT, WvT)):
                            sp.dma_start(w[:, u, i], wt.rearrange("(k p) n -> p k n", p=P)[:, :, bass.ts(a, P)]
                                         ).then_inc(w_in[u], 16)

        @block.gpsimd
        def _(pool):
            pool.memset(Q[:], 0.0).then_inc(zero_ok, 1)
            with pool.Fori(0, B) as b:
                pool.wait_ge(y_ok, b * TB + TB)
                pool.dma_start(out_t[b], y[:]).then_inc(y_out, 16)
            pool.wait_ge(y_out, 16 * B)

        @block.scalar
        def _(act):
            counts = Counts(act, "at")
            act.wait_ge(const_in, 16 * N_CONST)
            act.wait_ge(zero_ok, 2)
            with act.Fori(0, B) as b:
                act.wait_ge(moments, b * TB + TB)
                act.activation(std[:], mv[:, :, 1], ACT.Sqrt, bias=eps[:, 0:1]).then_inc(std_ok, 1)
                for u in range(TB // 2):
                    act.wait_ge(xT_ps, b * 4 + u + 1)
                    act.activation(xT[:, :, 2 * u * P:(2 * u + 2) * P].rearrange("p k (j t) -> p k j t", j=2),
                                   bank[u % 2][:].rearrange("p (k j t) -> p k j t", k=KD, j=2),
                                   ACT.Copy).then_inc(xT_ok, 1)
                with act.Fori(0, HP) as a:
                    n = b * HP + a
                    for q in range(QH):
                        at = counts(n * 2 + q + 1)
                        act.wait_ge(zero_ok, 2)
                        act.wait_ge(q_ps, at[0])
                        for h in range(2):
                            r = slice(DH * h, DH * h + DH)
                            act.activation(Q[r, h, q * 512:(q + 1) * 512], bank[q][r], ACT.Identity,
                                           bias=b_q[r, bass.ds(a, 1)]).then_inc(q_ok, 1)
                    for i in range(UNITS):
                        act.wait_ge(ntop_ok, n * UNITS + i + 1)
                        if i >= 4:
                            act.wait_ge(c_ps, n * TB + i // 2 - 1)
                        act.activation(E[:, i % 4], score[i % 2][:], ACT.Exp, scale=1.0 / 8.0,
                                       bias=ntop[:, i % 4:i % 4 + 1], accum_out=esum[:, i % 4:i % 4 + 1]
                                       ).then_inc(e_ok, 1)
                    at = counts(n * TB + TB)
                    act.wait_ge(zero_ok, 2)
                    act.wait_ge(c_ps, at[0])
                    act.activation(CT[:, bass.ds(a, 1)].rearrange("p o s -> p (o s)"), mix[:], ACT.Copy).then_inc(ct_ok, 1)

        @block.vector
        def _(dve):
            counts = Counts(dve, "at")
            dve.memset(eps[:], LN_EPS).then_inc(zero_ok, 1)
            dve.wait_ge(const_in, 16 * N_CONST)
            with dve.Fori(0, B) as b:
                dve.wait_ge(x_in, b * 16 + 16)
                for j in range(TB):
                    dve.bn_stats(bn[:, j], x_all[:, j]).then_inc(stats, 1)
                for j in range(TB):
                    at = counts(b * TB + j + 1)
                    dve.wait_ge(const_in, 16 * N_CONST)
                    dve.wait_ge(stats, at[0])
                    dve.bn_aggr(mv[:, j], bn[:, j]).then_inc(moments, 1)
                dve.wait_ge(std_ok, b + 1)
                dve.reciprocal(rstd[:], std[:]).then_inc(rstd_ok, 1)
                dve.wait_ge(rstd_ok, b + 1)
                for j in range(TB):
                    dve.tensor_scalar(xn[:, j], x_all[:, j], mv[:, j, 0:1], rstd[:, j:j + 1],
                                      ALU.subtract, ALU.mult).then_inc(xn_ok, 1)
                with dve.Fori(0, HP) as a:
                    n = b * HP + a
                    for q in range(QH):
                        dve.wait_ge(k_ps, n * 2 + q + 1)
                        dve.tensor_scalar(K[:, q * 512:(q + 1) * 512], bank[q][:], b_k[:, bass.ds(a, 1)], None,
                                          ALU.add).then_inc(k_ok, 1)
                    for q in range(2):
                        dve.wait_ge(v_ps, n * 2 + q + 1)
                        dve.tensor_tensor(V[:, 4 * q:4 * q + 4], bank[q][:].rearrange("p (j d) -> p j d", j=4),
                                          b_v[:, bass.ts(a, P)].unsqueeze(1).broadcast_to([P, 4, P]),
                                          ALU.add).then_inc(v_ok, 1)
                    def scale_value(i):
                        dve.wait_ge(e_ok, n * UNITS + i + 1)
                        dve.reciprocal(rsum[:, i % 4:i % 4 + 1], esum[:, i % 4:i % 4 + 1]).then_inc(rsum_ok, 1)
                        dve.wait_ge(rsum_ok, n * UNITS + i + 1)
                        if i >= 4:
                            dve.wait_ge(c_ps, n * TB + i // 2 - 1)
                        if i == 0:
                            dve.wait_ge(v_ok, n * 2 + 2)
                        h = i % 2
                        dve.tensor_scalar(Vs[:, i % 4], V[:, i // 2, DH * h:DH * h + DH], rsum[:, i % 4:i % 4 + 1],
                                          None, ALU.mult).then_inc(vs_ok, 1)
                    for i in range(UNITS):
                        dve.wait_ge(s_ps, n * UNITS + i + 1)
                        if i == 0:
                            dve.wait_ge(e_ok, n * UNITS)
                        dve.tensor_reduce(top[:, i % 4:i % 4 + 1], score[i % 2][:], AX.X, ALU.max).then_inc(top_ok, 1)
                        dve.wait_ge(top_ok, n * UNITS + i + 1)
                        dve.tensor_scalar(ntop[:, i % 4:i % 4 + 1], top[:, i % 4:i % 4 + 1], -1.0 / 8.0, None,
                                          ALU.mult).then_inc(ntop_ok, 1)
                        if i >= 1:
                            scale_value(i - 1)
                    scale_value(UNITS - 1)
                dve.wait_ge(y_out, b * 16)
                for j in range(TB):
                    dve.wait_ge(o_ps, b * TB + j + 1)
                    dve.tensor_tensor(y[:, j], bank[j % 2][:, 0:D], x_all[:, j], ALU.add).then_inc(y_ok, 1)

        @block.tensor
        def _(pe):
            counts = Counts(pe, "at")
            pe.wait_ge(const_in, 16 * N_CONST)
            pe.wait_ge(zero_ok, 2)
            with pe.Fori(0, B) as b:
                for u in range(TB // 2):
                    pe.wait_ge(xn_ok, b * TB + 2 * u + 2)
                    if u >= 2:
                        pe.wait_ge(xT_ok, b * 4 + u - 1)
                    else:
                        pe.wait_ge(y_ok, b * TB)
                    for k in range(KD):
                        for j in range(2):
                            last = pe.transpose(bank[u % 2][:, (k * 2 + j) * P:(k * 2 + j + 1) * P],
                                                xn[:, 2 * u + j, k * P:(k + 1) * P], ident)
                    last.then_inc(xT_ps, 1)
                at = counts(b * 4 + 4)
                pe.wait_ge(const_in, 16 * N_CONST)
                pe.wait_ge(xT_ok, at[0])
                with pe.Fori(0, HP // 2) as a2:
                    for u in range(2):
                        n = b * HP + a2 * 2 + u
                        pe.wait_ge(w_in[u], (b * 4 + a2) * 48 + 48)
                        for q in range(QH):
                            for k in range(KD):
                                last = pe.matmul(bank[q][:], w[:, u, 0, k], xT[:, k, q * 512:(q + 1) * 512],
                                                 start=(k == 0), stop=(k == KD - 1))
                            last.then_inc(q_ps, 1)
                        for q in range(QH):
                            pe.wait_ge(q_ok, n * 4 + 2 * q + 2)
                            for k in range(KD):
                                last = pe.matmul(bank[q][:], w[:, u, 1, k], xT[:, k, q * 512:(q + 1) * 512],
                                                 start=(k == 0), stop=(k == KD - 1))
                            last.then_inc(k_ps, 1)
                        for q in range(2):
                            pe.wait_ge(k_ok, n * 2 + q + 1)
                            for j in range(4):
                                for k in range(KD):
                                    last = pe.matmul(bank[q][:, j * P:(j + 1) * P],
                                                     xT[:, k, (4 * q + j) * P:(4 * q + j + 1) * P], w[:, u, 2, k],
                                                     start=(k == 0), stop=(k == KD - 1))
                            last.then_inc(v_ps, 1)
                        pe.wait_ge(v_ok, n * 2 + 2)

                        def scores(i):
                            if i >= 2:
                                pe.wait_ge(e_ok, n * UNITS + i - 1)
                            for q in range(QH):
                                last = pe.matmul(score[i % 2][:, q * 512:(q + 1) * 512],
                                                 K[:, (i // 2) * P:(i // 2 + 1) * P],
                                                 Q[:, i % 2, q * 512:(q + 1) * 512], start=True, stop=True)
                            last.then_inc(s_ps, 1)

                        def context(t):
                            pe.wait_ge(vs_ok, n * UNITS + 2 * t + 2)
                            if t == 0:
                                pe.wait_ge(ct_ok, n)
                            for q in range(QH):
                                for h in range(2):
                                    i = (2 * t + h) % 4
                                    last = pe.matmul(mix[DH * h:DH * h + DH, q * 512:(q + 1) * 512], Vs[:, i],
                                                     E[:, i, q * 512:(q + 1) * 512],
                                                     start=(t == 0), stop=(t == TB - 1))
                            last.then_inc(c_ps, 1)

                        for t in range(TB):
                            scores(2 * t)
                            scores(2 * t + 1)
                            if t:
                                context(t - 1)
                        context(TB - 1)
                pe.wait_ge(ct_ok, b * HP + HP)
                for j in range(TB):
                    if j >= 2:
                        pe.wait_ge(y_ok, b * TB + j - 1)
                    pe.matmul(bank[j % 2][:, 0:D], cst[0:1, C_ONE:C_ONE + P], b_o[:], start=True, stop=False)
                    for a in range(HP):
                        last = pe.matmul(bank[j % 2][:, 0:D], CT[:, a, j * P:(j + 1) * P], wo[:, a],
                                         start=False, stop=(a == HP - 1))
                    last.then_inc(o_ps, 1)
    clear(nc, held)


def seq_kernel(nc, consts, x, Wq, Wk, Wv, Wbeta, b_beta, Wout, Wr, W1, W2,
               WqT, bq, WkT, bk, WvT, bv, WoT, bo, gate_w, gate_b, w1, b1, w2, b2, out):
    def scratch(name, shape):
        return nc.dram_tensor(name, shape, F32, kind="Internal").ap()

    x1, x2, x3 = (scratch(n, [B, S, D]) for n in ("x1", "x2", "x3"))
    cap0, cap1 = int(1.25 * B * S / E_N), 160
    slots0, answers0 = scratch("slots0", [E_N * cap0, D]), scratch("answers0", [E_N * cap0, D])
    slots1, answers1 = scratch("slots1", [E_N * cap1, D]), scratch("answers1", [E_N * cap1, D])
    delta_layer(nc, consts, x, Wq, Wk, Wv, Wbeta, b_beta, Wout, x1)
    expert_layer(nc, "m0", consts, x1, Wr, None, W1, None, W2, None, cap0, True, x2, slots0, answers0)
    attention_layer(nc, consts, x2, WqT, WkT, WvT, bq, bk, bv, WoT, bo, x3)
    expert_layer(nc, "m1", consts, x3, gate_w, gate_b, w1, b1, w2, b2, cap1, False, out, slots1, answers1)


def kernel(**inputs):
    import concourse.bacc as bacc
    from concourse.bass_utils import run_bass_kernel_spmd

    def rows(name):
        a = np.asarray(inputs[name])
        return np.ascontiguousarray(a.reshape(-1, a.shape[-1]).T)

    flat = lambda name: np.ascontiguousarray(np.asarray(inputs[name]).reshape(-1))
    plain = lambda name: np.ascontiguousarray(inputs[name])
    arrays = {"consts": shape_constants()}
    for n in ("x", "Wq", "Wk", "Wv", "Wbeta", "b_beta", "Wout"):
        arrays["L0_attn_" + n] = plain("L0_attn_" + n)
    for n in ("Wr", "W1", "W2"):
        arrays["L0_ffn_" + n] = plain("L0_ffn_" + n)
    for n in ("q", "k", "v", "l"):
        arrays[f"L1_attn_{n}_w"] = rows(f"L1_attn_{n}_w")
        arrays[f"L1_attn_{n}_b"] = flat(f"L1_attn_{n}_b")
    for n in ("gate_w", "gate_b", "w1", "b1", "w2", "b2"):
        arrays["L1_ffn_" + n] = plain("L1_ffn_" + n)

    nc = bacc.Bacc("TRN2", target_bir_lowering=False, num_devices=1)
    args = [nc.dram_tensor(n, a.shape, mybir.dt.from_np(a.dtype), kind="ExternalInput").ap() for n, a in arrays.items()]
    out = nc.dram_tensor("out", (B, S, D), F32, kind="ExternalOutput").ap()
    seq_kernel(nc, *args, out)
    r = run_bass_kernel_spmd(nc, [arrays], core_ids=[0])
    return r.results[0]["out"]
```

```python
import numpy as np
from contextlib import ExitStack

import concourse.bass as bass
from concourse import mybir

F32 = mybir.dt.float32
BF16 = mybir.dt.bfloat16
I32 = mybir.dt.int32
U32 = mybir.dt.uint32
ALU = mybir.AluOpType
ACT = mybir.ActivationFunctionType
AX = mybir.AxisListType

P = 128
B, S, D = 4, 1024, 256
H, DH = 16, 64
HP = H // 2
KD = D // P
C = 64
NCH = S // C
SUB = 16
LEVELS = 2
LN_EPS = 1e-5
NORM_EPS = 1e-12
SQ_EPS = NORM_EPS * NORM_EPS

C_ID = 0
C_ID2 = C_ID + P
C_LVL = C_ID2 + C
C_CAUSAL = C_LVL + LEVELS * C
C_OWN = C_CAUSAL + C
C_SEL = C_OWN + C
C_BLK = C_SEL + SUB
C_SAME = C_BLK + C // SUB
C_TRI = C_SAME + P
C_ONE = C_TRI + P
C_EXP = C_ONE + P
C_RANK = C_EXP + 8
C_ALL = C_RANK + 8


def shape_constants():
    c = np.zeros((P, C_ALL), np.float32)
    row = np.arange(P)[:, None]
    c[:, C_ID:C_ID + P] = row == np.arange(P)[None]
    s, t = row % C, np.arange(C)[None]
    c[:, C_ID2:C_ID2 + C] = s == t
    for l in range(LEVELS):
        size = SUB << l
        same = s // (2 * size) == t // (2 * size)
        c[:, C_LVL + l * C:C_LVL + (l + 1) * C] = same & (t // size % 2 == 1) & (s // size % 2 == 0)
    c[:, C_CAUSAL:C_CAUSAL + C] = -1.0 * (s <= t)
    c[:, C_OWN:C_OWN + C] = -1.0 * ((s // SUB == t // SUB) & (s < t))
    c[:, C_SEL:C_SEL + SUB] = row % SUB == np.arange(SUB)[None]
    c[:, C_BLK:C_BLK + C // SUB] = s // SUB == np.arange(C // SUB)[None]
    c[:, C_SAME:C_SAME + P] = row // SUB == np.arange(P)[None] // SUB
    c[:, C_TRI:C_TRI + P] = row <= np.arange(P)[None]
    c[:, C_ONE:C_ONE + P] = 1.0
    c[:, C_EXP:C_EXP + 8] = np.arange(8)[None]
    c[:, C_RANK:C_RANK + 8] = 8 - np.arange(8)[None]
    return c


def clear(nc, held):
    nc.clear_and_free_semaphores(held)
    nc.all_engine_barrier()


START = 1


def start_counts(nc, held):
    for s in held:
        nc.sync.sem_inc(s, START)
    nc.all_engine_barrier()


class Counts:

    def __init__(self, eng, name, n=3):
        self.eng, self.regs = eng, [eng.alloc_register(f"{name}_count{i}") for i in range(n)]

    def __call__(self, *values):
        for reg, value in zip(self.regs, values):
            self.eng.reg_mov(reg, value)
        return self.regs[:len(values)]


def delta_layer(nc, consts, x, Wq, Wk, Wv, Wbeta, b_beta, Wout, x1):
    held = []
    with ExitStack() as ctx:
        def sb(name, shape, dt=F32):
            return ctx.enter_context(nc.sbuf_tensor("dl_" + name, shape, dt))

        def sem(name):
            held.append(nc.alloc_semaphore(name="dl_" + name))
            return held[-1]

        bank = [ctx.enter_context(nc.psum_tensor(f"dl_bank{i}", [P, 512], F32)) for i in range(8)]
        BG, BP, BSP, BX, BTX, BXT = (0, 1), (2, 3), (4, 5), (0, 1), (2, 3), (4, 5)
        BXN, BBETA, BK, BV, BQ, BKT = 7, 7, (6, 7), (6, 7), (6, 7), (6, 7)
        BR, BU, BO, BN, BY = (6, 7), (6, 7), 6, 7, 6

        cst = sb("cst", [P, C_TRI])
        wq, wk, wv = (sb(n, [P, KD, H * DH]) for n in ("wq", "wk", "wv"))
        wout = sb("wout", [P, HP, D])
        wbeta = sb("wbeta", [P, KD, H])
        bbeta = sb("bbeta", [P, HP])
        x_ln = sb("x_ln", [P, 2, D])
        x_res = sb("x_res", [P, 2, D])
        y = sb("y", [P, 2, D])
        bn = sb("bn", [P, 2, 6])
        mv = sb("mv", [P, 2, 2])
        std = sb("std", [P, 2])
        eps = sb("eps", [P, 1])
        rstd = sb("rstd", [P, 2])
        xn = sb("xn", [P, 2, D])
        xc = sb("xc", [P, 2, KD, P])
        z = sb("z", [P, B, HP])
        ez = sb("ez", [P, B, HP])
        ez1 = sb("ez1", [P, B, HP])
        beta = sb("beta", [P, B, HP])
        sq = sb("sq", [P, 2, HP, DH])
        ss = sb("ss", [P, B, HP])
        ssc = sb("ssc", [P, B, HP])
        kn = sb("kn", [P, B, HP])
        rkn = sb("rkn", [P, B, HP])
        K = sb("K", [P, B, HP, DH])
        V = sb("V", [P, B, HP, DH])
        QT = sb("QT", [P, HP, B, C])
        KT = sb("KT", [P, B, HP, C])
        PT = sb("PT", [P, B, HP, C])
        G = sb("G", [P, 2, HP, C])
        Gm = sb("Gm", [P, 2, HP, C])
        own = sb("own", [P, 2, HP, SUB])
        spread = sb("spread", [P, 2, HP, SUB, SUB])
        coef = sb("coef", [P, 2 * HP, SUB, SUB])
        part = sb("part", [P, SUB, 2 * HP, SUB])
        TS = sb("TS", [P, 2 * HP, SUB])
        BT = sb("BT", [P, 2, LEVELS, HP, C])
        T = sb("T", [P, 2, HP, C])
        TT = sb("TT", [P, B, HP, C])
        X = sb("X", [P, 2, HP, C])
        N = sb("N", [P, B, HP, DH])
        R = sb("R", [P, B, HP, DH])
        U = sb("U", [P, B, HP, DH])
        OT = sb("OT", [P, HP, B, C])

        weights, state0 = sem("weights"), sem("state0")
        x_in, r_in, stored = ([sem(f"{n}{u}") for u in range(2)] for n in ("x_in", "r_in", "stored"))
        stats, moments, std_ok, rstd_ok, xn_ok, xt_ps, xc_ok = map(
            sem, ("stats", "moments", "std_ok", "rstd_ok", "xn_ok", "xt_ps", "xc_ok"))
        beta_ps, z_ok, ez_ok, ez1_ok, beta_ok = map(sem, ("beta_ps", "z_ok", "ez_ok", "ez1_ok", "beta_ok"))
        k_ps, sq_ok, ss_ok, ssc_ok, kn_ok, rkn_ok, k_ok = map(
            sem, ("k_ps", "sq_ok", "ss_ok", "ssc_ok", "kn_ok", "rkn_ok", "k_ok"))
        v_ps, v_ok, q_ps, q_ok, kt_ps, kt_ok = map(sem, ("v_ps", "v_ok", "q_ps", "q_ok", "kt_ps", "kt_ok"))
        g_ps, g_ok, p_ps, p_ok, bt_ok = map(sem, ("g_ps", "g_ok", "p_ps", "p_ok", "bt_ok"))
        gm_ok, own_ok, spread_ok, coef_ps, coef_ok, column, ts_ok, tn_ps, tn_ok = map(
            sem, ("gm_ok", "own_ok", "spread_ok", "coef_ps", "coef_ok", "column", "ts_ok", "tn_ps", "tn_ok"))
        x_ps, xx_ok, tx_ps, t_ok, xt2_ps, tt_ok = map(sem, ("x_ps", "xx_ok", "tx_ps", "t_ok", "xt2_ps", "tt_ok"))
        r_ps, r_ok, u_ps, u_ok, o_ps, o_ok, n_ps, n_ok = map(
            sem, ("r_ps", "r_ok", "u_ps", "u_ok", "o_ps", "o_ok", "n_ps", "n_ok"))
        y_ps, y_ok = sem("y_ps"), sem("y_ok")
        start_counts(nc, held)

        ident = cst[:, C_ID:C_ID + P]
        ident2 = cst[:, C_ID2:C_ID2 + C]
        N_WEIGHTS = 8
        ALL_WEIGHTS = 16 * N_WEIGHTS + START

        COLUMNS = 2 * (SUB - 1)
        CB = HP * SUB * SUB // 512

        def x_count(f, l, j):
            return f * (2 * LEVELS) + (2 * l + j + 1)

        def over_pairs(m):
            return m.unsqueeze(1).broadcast_to([P, HP, C])

        def over_cols(v):
            return v.unsqueeze(2).broadcast_to([P, HP, C])

        def grid(b):
            return bank[b][:].rearrange("p (a c) -> p a c", a=HP)

        SLOTS = 8 + 2 * LEVELS

        def whole(part):
            def run(c, u):
                for s in range(SLOTS):
                    part(c, u, s)
            return run

        def first(c, u):
            return isinstance(c, int) and (c, u) == (0, 0)

        def last(c, u):
            return isinstance(c, int) and (c, u) == (NCH - 1, 1)

        def steps(eng, front, pair_block, state):
            front(0, 0)
            pair_block(0, 0, state=False)
            with eng.Fori(0, NCH - 1) as c:
                pair_block(c, 1)
                pair_block(c + 1, 0)
            pair_block(NCH - 1, 1, front=False)
            state(NCH - 1, 1)

        block = ctx.enter_context(nc.Block())

        @block.sync
        def _(sp):
            def load(dst, c, u, done):
                for h in range(2):
                    sp.dma_start(dst[C * h:C * h + C, u], x[2 * u + h, bass.ts(c, C), :]).then_inc(done[u], 16)

            load(x_ln, 0, 0, x_in)
            load(x_ln, 0, 1, x_in)
            sp.dma_start(cst[:], consts[:, 0:C_TRI]).then_inc(weights, 16)
            sp.dma_start(wk[:], Wk.rearrange("(k p) n -> p k n", p=P)).then_inc(weights, 16)
            sp.dma_start(wbeta[:], Wbeta.rearrange("(k p) n -> p k n", p=P)).then_inc(weights, 16)
            for h in range(2):
                sp.dma_start(bbeta[C * h:C * h + C, :], b_beta.rearrange("(a h) -> h a", h=2)[h:h + 1, :]
                             .broadcast_to([C, HP]), allow_slow_non_contiguous=True).then_inc(weights, 16)
            sp.dma_start(wv[:], Wv.rearrange("(k p) n -> p k n", p=P)).then_inc(weights, 16)
            sp.dma_start(wq[:], Wq.rearrange("(k p) n -> p k n", p=P)).then_inc(weights, 16)
            sp.dma_start(wout[:], Wout.rearrange("(a p) n -> p a n", p=P)).then_inc(weights, 16)

            def store(c, u):
                sp.wait_ge(y_ok, c * 2 + (u + 1 + START))
                for h in range(2):
                    sp.dma_start(x1[2 * u + h, bass.ts(c, C), :], y[C * h:C * h + C, u]).then_inc(stored[u], 16)

            load(x_res, 0, 0, r_in)
            load(x_res, 0, 1, r_in)
            with sp.Fori(0, NCH - 1) as c:
                for u in range(2):
                    sp.wait_ge(xn_ok, c * 2 + (u + 1 + START))
                    load(x_ln, c + 1, u, x_in)
                    store(c, u)
                    load(x_res, c + 1, u, r_in)
            for u in range(2):
                store(NCH - 1, u)
                sp.wait_ge(stored[u], NCH * 32 + START)

        @block.gpsimd
        def _(pool):
            pool.wait_ge(weights, ALL_WEIGHTS)
            with pool.Fori(0, 2 * NCH) as f:
                for j in range(2):
                    pool.wait_ge(own_ok, f * 2 + (j + 1 + START))
                    pool.wait_ge(coef_ps, f * (2 * CB) + START)
                    pool.tensor_tensor(spread[:, j].rearrange("p a t s -> p (a t) s"),
                                       own[:, j].rearrange("p a t -> p (a t)").unsqueeze(2)
                                       .broadcast_to([P, HP * SUB, SUB]),
                                       cst[:, C_SEL:C_SEL + SUB].unsqueeze(1).broadcast_to([P, HP * SUB, SUB]),
                                       ALU.mult).then_inc(spread_ok, 1)
                pool.wait_ge(x_ps, f * (2 * LEVELS) + START)
                for l in range(LEVELS):
                    m = cst[:, C_LVL + l * C:C_LVL + (l + 1) * C]
                    for j in range(2):
                        pool.tensor_tensor(BT[:, j, l], G[:, j], over_pairs(m), ALU.mult).then_inc(bt_ok, 1)

        @block.scalar
        def _(act):
            def ln_std(c, u):
                act.wait_ge(moments, c * 2 + (u + 1 + START))
                act.activation(std[:, u:u + 1], mv[:, u, 1:2], ACT.Sqrt, bias=eps[:, 0:1]).then_inc(std_ok, 1)

            def keep_xc(c, u):
                act.wait_ge(xt_ps, c * 2 + (u + 1 + START))
                act.activation(xc[:, u].rearrange("p k t -> p (k t)"), bank[BXN][:, 0:KD * P], ACT.Copy
                               ).then_inc(xc_ok, 1)

            def exp_z(c, u):
                act.wait_ge(z_ok, c * 2 + (u + 1 + START))
                act.activation(ez[:, 2 * u:2 * u + 2], z[:, 2 * u:2 * u + 2], ACT.Exp, scale=-1.0).then_inc(ez_ok, 1)

            def square_k(c, u, j):
                b = 2 * u + j
                act.wait_ge(k_ps, c * 4 + (b + 1 + START))
                act.wait_ge(ss_ok, c * 4 + (2 * u + START))
                act.activation(sq[:, j], grid(BK[j]), ACT.Square).then_inc(sq_ok, 1)

            def sqrt_k(c, u):
                act.wait_ge(ssc_ok, c * 2 + (u + 1 + START))
                act.activation(kn[:, 2 * u:2 * u + 2], ssc[:, 2 * u:2 * u + 2], ACT.Sqrt).then_inc(kn_ok, 1)

            def keep_v(c, u, j):
                act.wait_ge(v_ps, c * 4 + (2 * u + j + 1 + START))
                act.activation(V[:, 2 * u + j], grid(BV[j]), ACT.Copy).then_inc(v_ok, 1)

            def keep_q(c, u, q):
                act.wait_ge(q_ps, c * 4 + (2 * u + q + 1 + START))
                act.activation(QT[:, 4 * q:4 * q + 4, 2 * u:2 * u + 2].rearrange("p a b t -> p a (b t)"),
                               bank[BQ[q]][:].rearrange("p (a t) -> p a t", a=4), ACT.Copy, scale=-1.0
                               ).then_inc(q_ok, 1)

            def keep_kt(c, u, j):
                act.wait_ge(kt_ps, c * 4 + (2 * u + j + 1 + START))
                act.activation(KT[:, 2 * u + j], grid(BKT[j]), ACT.Copy).then_inc(kt_ok, 1)

            def keep_o(c, u, j):
                act.wait_ge(o_ps, c * 4 + (2 * u + j + 1 + START))
                act.activation(OT[:, :, 2 * u + j], grid(BO), ACT.Copy).then_inc(o_ok, 1)

            def pair_block(c, u, state=True, front=True):
                f = c * 2 + u
                keep_v(c, u, 0)
                keep_v(c, u, 1)
                before, after = ((c - 1, 1), (c, 1)) if u == 0 else ((c, 0), (c + 1, 0))

                def slot(s):
                    if state:
                        state_part(*before, s)
                    if front:
                        front_part(*after, s)

                slot(0)
                slot(1)
                for j in range(2):
                    for i in range(CB):
                        act.wait_ge(coef_ps, f * (2 * CB) + (CB * j + i + 1 + START))
                        act.wait_ge(ts_ok, f + START)
                        act.activation(coef[:, HP * j + 2 * i:HP * j + 2 * i + 2].rearrange("p a t s -> p (a t s)"),
                                       bank[BSP[i % 2]][:], ACT.Copy).then_inc(coef_ok, 1)
                    slot(2 + j)
                for s in range(4, 8):
                    slot(s)
                for j in range(2):
                    act.wait_ge(tn_ps, f * 2 + (j + 1 + START))
                    act.activation(T[:, j], grid(BX[j]), ACT.Copy).then_inc(tn_ok, 1)
                for l in range(LEVELS):
                    for j in range(2):
                        act.wait_ge(x_ps, x_count(f, l, j) + START)
                        act.activation(X[:, j], grid(BX[j]), ACT.Copy).then_inc(xx_ok, 1)
                    slot(2 * l + 8)
                    slot(2 * l + 9)

            def state_part(c, u, s):
                if s == 2:
                    keep_o(c, u, 0)
                if s == 3:
                    keep_o(c, u, 1)

            def front_part(c, u, s):
                if s == 1:
                    ln_std(c, u)
                if s == 4:
                    keep_xc(c, u)
                if s == 5:
                    square_k(c, u, 0)
                if s == 6:
                    square_k(c, u, 1)
                    exp_z(c, u)
                if s == 7:
                    sqrt_k(c, u)
                if s == 8:
                    keep_q(c, u, 0)
                if s == 9:
                    keep_q(c, u, 1)
                if s == 10:
                    keep_kt(c, u, 0)
                if s == 11:
                    keep_kt(c, u, 1)

            act.wait_ge(state0, 2 + SUB + START)
            steps(act, whole(front_part), pair_block, whole(state_part))

        @block.vector
        def _(dve):
            counts = Counts(dve, "dl")

            def ln_stats(c, u):
                dve.wait_ge(x_in[u], c * 32 + (32 + START))
                dve.bn_stats(bn[:, u], x_ln[:, u]).then_inc(stats, 1)
                at = counts(c * 2 + (u + 1 + START))
                dve.wait_ge(weights, ALL_WEIGHTS)
                dve.wait_ge(stats, at[0])
                dve.bn_aggr(mv[:, u], bn[:, u]).then_inc(moments, 1)

            def ln_apply(c, u):
                dve.wait_ge(std_ok, c * 2 + (u + 1 + START))
                dve.reciprocal(rstd[:, u:u + 1], std[:, u:u + 1]).then_inc(rstd_ok, 1)
                dve.wait_ge(rstd_ok, c * 2 + (u + 1 + START))
                dve.tensor_scalar(xn[:, u], x_ln[:, u], mv[:, u, 0:1], rstd[:, u:u + 1],
                                  ALU.subtract, ALU.mult).then_inc(xn_ok, 1)

            def rates_z(c, u):
                dve.wait_ge(beta_ps, c * 2 + (u + 1 + START))
                dve.tensor_tensor(z[:, 2 * u:2 * u + 2],
                                  bank[BBETA][:, 0:2 * HP].rearrange("p (j a) -> p j a", j=2),
                                  bbeta[:].unsqueeze(1).broadcast_to([P, 2, HP]), ALU.add).then_inc(z_ok, 1)

            def rates(c, u):
                lanes = slice(2 * u, 2 * u + 2)
                dve.wait_ge(ez_ok, c * 2 + (u + 1 + START))
                dve.tensor_scalar(ez1[:, lanes], ez[:, lanes], 1.0, None, ALU.add).then_inc(ez1_ok, 1)
                dve.wait_ge(ez1_ok, c * 2 + (u + 1 + START))
                dve.reciprocal(beta[:, lanes], ez1[:, lanes]).then_inc(beta_ok, 1)

            def sum_squares(c, u, j):
                dve.wait_ge(sq_ok, c * 4 + (2 * u + j + 1 + START))
                dve.tensor_reduce(ss[:, 2 * u + j], sq[:, j], AX.X, ALU.add).then_inc(ss_ok, 1)

            def floor_squares(c, u):
                lanes = slice(2 * u, 2 * u + 2)
                dve.wait_ge(ss_ok, c * 4 + (2 * u + 2 + START))
                dve.tensor_scalar(ssc[:, lanes], ss[:, lanes], SQ_EPS, None, ALU.max).then_inc(ssc_ok, 1)

            def keys(c, u):
                lanes = slice(2 * u, 2 * u + 2)
                dve.wait_ge(kn_ok, c * 2 + (u + 1 + START))
                dve.reciprocal(rkn[:, lanes], kn[:, lanes]).then_inc(rkn_ok, 1)
                dve.wait_ge(rkn_ok, c * 2 + (u + 1 + START))
                for j in range(2):
                    b = 2 * u + j
                    dve.tensor_tensor(K[:, b], grid(BK[j]), over_cols(rkn[:, b]), ALU.mult).then_inc(k_ok, 1)

            def inverse(c, u, slot):
                f = c * 2 + u
                lanes = slice(2 * u, 2 * u + 2)
                dve.wait_ge(beta_ok, f + (1 + START))
                for j in range(2):
                    dve.wait_ge(g_ps, f * 2 + (j + 1 + START))
                    dve.wait_ge(bt_ok, f * (2 * LEVELS) + START)
                    dve.tensor_tensor(G[:, j], grid(BG[j]), over_cols(beta[:, 2 * u + j]), ALU.mult).then_inc(g_ok, 1)
                for j in range(2):
                    dve.wait_ge(g_ok, f * 2 + (j + 1 + START))
                    dve.tensor_tensor(Gm[:, j], G[:, j], over_pairs(cst[:, C_OWN:C_OWN + C]), ALU.mult
                                      ).then_inc(gm_ok, 1)
                for j in range(2):
                    dve.wait_ge(gm_ok, f * 2 + (j + 1 + START))
                    dve.wait_ge(spread_ok, f * 2 + START)
                    dve.tensor_reduce(own[:, j], Gm[:, j].rearrange("p a (q t) -> p a t q", t=SUB), AX.X, ALU.add
                                      ).then_inc(own_ok, 1)
                for j in range(2):
                    dve.wait_ge(p_ps, f * 2 + (j + 1 + START))
                    dve.tensor_tensor(PT[:, 2 * u + j], grid(BP[j]), over_pairs(cst[:, C_CAUSAL:C_CAUSAL + C]),
                                      ALU.mult).then_inc(p_ok, 1)
                for s in range(3):
                    slot(s)
                dve.wait_ge(coef_ok, f * (2 * CB) + (2 * CB + START))
                for t in range(1, SUB):
                    if t > 1:
                        dve.wait_ge(column, f * COLUMNS + (2 * t - 2 + START))
                    dve.tensor_tensor(part[:, t, :, 0:t], TS[:, :, 0:t], coef[:, :, t, 0:t], ALU.mult
                                      ).then_inc(column, 1)
                    dve.wait_ge(column, f * COLUMNS + (2 * t - 1 + START))
                    dve.tensor_reduce(TS[:, :, t], part[:, t, :, 0:t + 1], AX.X, ALU.add).then_inc(column, 1)
                    if t == SUB // 2:
                        slot(3)
                dve.wait_ge(column, f * COLUMNS + (COLUMNS + START))
                dve.tensor_tensor(TT[:, lanes].rearrange("p j a (q t) -> p (j a) q t", t=SUB),
                                  TS[:].unsqueeze(2).broadcast_to([P, 2 * HP, C // SUB, SUB]),
                                  cst[:, C_BLK:C_BLK + C // SUB].unsqueeze(1).unsqueeze(3)
                                  .broadcast_to([P, 2 * HP, C // SUB, SUB]), ALU.mult).then_inc(ts_ok, 1)
                for s in range(4, 8):
                    slot(s)
                for l in range(LEVELS):
                    slot(2 * l + 8)
                    for j in range(2):
                        b = 2 * u + j
                        if l < LEVELS - 1:
                            dve.wait_ge(tx_ps, f * 2 + (j + 1 + START))
                            dve.tensor_tensor(T[:, j], T[:, j], grid(BTX[j]), ALU.subtract).then_inc(t_ok, 1)
                        dve.wait_ge(xt2_ps, x_count(f, l, j) + START)
                        dve.wait_ge(*((ts_ok, f + (1 + START)) if l == 0 else (tt_ok, x_count(f, l - 1, j) + START)))
                        dve.tensor_tensor(TT[:, b], TT[:, b], grid(BXT[j]), ALU.subtract).then_inc(tt_ok, 1)
                    slot(2 * l + 9)

            def add_v(c, u, j):
                b = 2 * u + j
                dve.wait_ge(r_ps, c * 4 + (b + 1 + START))
                dve.tensor_tensor(R[:, b], grid(BR[j]), V[:, b], ALU.add).then_inc(r_ok, 1)

            def scale_u(c, u, j):
                b = 2 * u + j
                dve.wait_ge(u_ps, c * 4 + (b + 1 + START))
                dve.tensor_tensor(U[:, b], grid(BU[j]), over_cols(beta[:, b]), ALU.mult).then_inc(u_ok, 1)

            def new_state(c, u, j):
                b = 2 * u + j
                dve.wait_ge(n_ps, c * 4 + (b + 1 + START))
                dve.tensor_tensor(N[:, b], N[:, b], grid(BN), ALU.subtract).then_inc(n_ok, 1)

            def residual(c, u):
                dve.wait_ge(y_ps, c * 2 + (u + 1 + START))
                dve.wait_ge(r_in[u], c * 32 + (32 + START))
                dve.wait_ge(stored[u], c * 32 + START)
                dve.tensor_tensor(y[:, u], bank[BY][:, 0:D], x_res[:, u], ALU.add).then_inc(y_ok, 1)

            def state_part(c, u, s):
                if s == 0:
                    add_v(c, u, 0)
                    add_v(c, u, 1)
                if s == 1:
                    scale_u(c, u, 0)
                    scale_u(c, u, 1)
                if s == 2:
                    new_state(c, u, 0)
                if s == 3:
                    new_state(c, u, 1)
                if s == 4:
                    residual(c, u)

            def front_part(c, u, s):
                if s == 0:
                    ln_stats(c, u)
                if s == 2:
                    ln_apply(c, u)
                if s == 5:
                    rates_z(c, u)
                    sum_squares(c, u, 0)
                if s == 6:
                    sum_squares(c, u, 1)
                    floor_squares(c, u)
                    rates(c, u)
                if s == 7:
                    keys(c, u)

            def pair_block(c, u, state=True, front=True):
                before, after = ((c - 1, 1), (c, 1)) if u == 0 else ((c, 0), (c + 1, 0))

                def slot(s):
                    if state:
                        state_part(*before, s)
                    if front:
                        front_part(*after, s)

                inverse(c, u, slot)

            dve.memset(N[:], 0.0).then_inc(state0, 1)
            dve.memset(eps[:], LN_EPS).then_inc(state0, 1)
            dve.wait_ge(weights, ALL_WEIGHTS)
            sel = cst[:, C_SEL:C_SEL + SUB]
            for t in range(1, SUB):
                dve.tensor_copy(part[:, t, :, t], sel[:, t:t + 1].broadcast_to([P, 2 * HP])).then_inc(state0, 1)
            dve.tensor_copy(TS[:, :, 0], sel[:, 0:1].broadcast_to([P, 2 * HP])).then_inc(state0, 1)
            dve.wait_ge(state0, 2 + SUB + START)
            steps(dve, whole(front_part), pair_block, whole(state_part))

        @block.tensor
        def _(pe):
            counts = Counts(pe, "dl")

            def pairs(out, lhsT, rhs):
                for a in range(HP):
                    for h in range(2):
                        rows = slice(C * h, C * h + C)
                        last = pe.matmul(out[rows, a], lhsT(rows, a), rhs(rows, a), start=True, stop=True)
                return last

            def natural(out, w, u, j):
                wh = w[:].rearrange("p k (a h d) -> p k h a d", h=2, d=DH)
                for k in range(KD):
                    for h in range(2):
                        last = pe.matmul(out[C * h:C * h + C], xc[:, u, k, C * j:C * j + C], wh[:, k, h],
                                         start=(k == 0), stop=(k == KD - 1))
                return last

            def turn_x(c, u):
                at = counts(c * 2 + (u + 1 + START), c * 4 + (2 * u - 2 + START))
                pe.wait_ge(weights, ALL_WEIGHTS)
                pe.wait_ge(xn_ok, at[0])
                if not first(c, u):
                    pe.wait_ge(n_ok, at[1])
                for k in range(KD):
                    last = pe.transpose(bank[BXN][:, k * P:(k + 1) * P], xn[:, u, k * P:(k + 1) * P], ident)
                last.then_inc(xt_ps, 1)

            def rates(c, u):
                pe.wait_ge(xc_ok, c * 2 + (u + 1 + START))
                wbh = wbeta[:].rearrange("p k (a h) -> p k h a", h=2)
                for j in range(2):
                    for h in range(2):
                        for k in range(KD):
                            last = pe.matmul(bank[BBETA][C * h:C * h + C, j * HP:(j + 1) * HP],
                                             xc[:, u, k, C * j:C * j + C], wbh[:, k, h],
                                             start=(k == 0), stop=(k == KD - 1))
                last.then_inc(beta_ps, 1)

            def keys(c, u, j):
                pe.wait_ge(xc_ok, c * 2 + (u + 1 + START))
                if j == 1:
                    pe.wait_ge(z_ok, c * 2 + (u + 1 + START))
                elif not first(c, u):
                    pe.wait_ge(y_ok, c * 2 + (u - 1 + START))
                natural(grid(BK[j]), wk, u, j).then_inc(k_ps, 1)

            def values(c, u, j):
                pe.wait_ge(kt_ok, c * 4 + (2 * u + 2 + START))
                natural(grid(BV[j]), wv, u, j).then_inc(v_ps, 1)

            def queries(c, u, q):
                pe.wait_ge(k_ok, c * 4 + (2 * u + q + 1 + START))
                for a in range(4):
                    for k in range(KD):
                        m = (4 * q + a) * P
                        last = pe.matmul(bank[BQ[q]][:, a * P:(a + 1) * P], wq[:, k, m:m + P], xc[:, u, k],
                                         start=(k == 0), stop=(k == KD - 1))
                last.then_inc(q_ps, 1)

            def turn_keys(c, u, j):
                b = 2 * u + j
                at = counts(c * 4 + (b + 1 + START), c * 4 + (b + 1 + START))
                pe.wait_ge(weights, ALL_WEIGHTS)
                pe.wait_ge(k_ok, at[0])
                pe.wait_ge(q_ok, at[1])
                pairs(grid(BKT[j]), lambda r, a: K[r, b, a], lambda r, a: ident2[r]).then_inc(kt_ps, 1)

            def inverse(c, u, slot):
                f = c * 2 + u
                for j in range(2):
                    b = 2 * u + j
                    at = counts(c * 4 + (2 * u + 2 + START))
                    pe.wait_ge(weights, ALL_WEIGHTS)
                    pe.wait_ge(kt_ok, at[0])
                    pairs(grid(BG[j]), lambda r, a: KT[r, b, a], lambda r, a: KT[r, b, a]).then_inc(g_ps, 1)
                values(c, u, 0)
                values(c, u, 1)
                for j in range(2):
                    b = 2 * u + j
                    at = counts(c * 4 + (2 * u + 2 + START))
                    pe.wait_ge(weights, ALL_WEIGHTS)
                    pe.wait_ge(q_ok, at[0])
                    pairs(grid(BP[j]), lambda r, a: KT[r, b, a], lambda r, a: QT[r, a, b]).then_inc(p_ps, 1)
                slot(0)
                slot(1)
                for j in range(2):
                    for i in range(CB):
                        n = CB * j + i
                        at = counts(f * 2 + (j + 1 + START), f * (2 * CB) + (n - 1 + START))
                        pe.wait_ge(weights, ALL_WEIGHTS)
                        pe.wait_ge(spread_ok, at[0])
                        if n >= 2:
                            pe.wait_ge(coef_ok, at[1])
                        pe.matmul(bank[BSP[i % 2]][:], cst[:, C_SAME:C_SAME + P],
                                  spread[:, j, 2 * i:2 * i + 2].rearrange("p a t s -> p (a t s)"),
                                  start=True, stop=True).then_inc(coef_ps, 1)
                    slot(2 + j)
                for s in range(4, 8):
                    slot(s)
                for j in range(2):
                    b = 2 * u + j
                    at = counts(f + (1 + START), f * 2 + (2 + START))
                    pe.wait_ge(weights, ALL_WEIGHTS)
                    pe.wait_ge(ts_ok, at[0])
                    pe.wait_ge(g_ok, at[1])
                    pairs(grid(BX[j]), lambda r, a: TT[r, b, a], lambda r, a: ident2[r]).then_inc(tn_ps, 1)
                for l in range(LEVELS):
                    for j in range(2):
                        at = counts(x_count(f, l, j) + START, f * 2 + (j + 1 + START),
                                    x_count(f, max(l - 1, 0), j) + START)
                        pe.wait_ge(weights, ALL_WEIGHTS)
                        pe.wait_ge(bt_ok, at[0])
                        pe.wait_ge(t_ok if l else tn_ok, at[1])
                        if l:
                            pe.wait_ge(xx_ok, at[2])
                        pairs(grid(BX[j]), lambda r, a: BT[r, j, l, a], lambda r, a: T[r, j, a]).then_inc(x_ps, 1)
                    slot(2 * l + 8)
                    for j in range(2):
                        b = 2 * u + j
                        at = counts(x_count(f, l, j) + START, x_count(f, max(l - 1, 0), j) + START,
                                    f * 2 + (2 + START))
                        pe.wait_ge(weights, ALL_WEIGHTS)
                        pe.wait_ge(xx_ok, at[0])
                        if l:
                            pe.wait_ge(tt_ok, at[1])
                        else:
                            pe.wait_ge(p_ok, at[2])
                        if l < LEVELS - 1:
                            pairs(grid(BTX[j]), lambda r, a: TT[r, b, a], lambda r, a: X[r, j, a]).then_inc(tx_ps, 1)
                        pairs(grid(BXT[j]), lambda r, a: X[r, j, a], lambda r, a: TT[r, b, a]).then_inc(xt2_ps, 1)
                    slot(2 * l + 9)

            def recall(c, u, j):
                b = 2 * u + j
                at = counts(c * 4 + (2 * u + START), c * 4 + (2 * u + (2 if last(c, u) else 4) + START))
                pe.wait_ge(weights, ALL_WEIGHTS)
                pe.wait_ge(n_ok, at[0])
                pe.wait_ge(v_ok, at[1])
                pairs(grid(BR[j]), lambda r, a: KT[r, b, a], lambda r, a: N[r, b, a]).then_inc(r_ps, 1)

            def solve(c, u, j):
                b = 2 * u + j
                at = counts(c * 4 + (b + 1 + START), x_count(c * 2 + u, LEVELS - 1, j) + START)
                pe.wait_ge(weights, ALL_WEIGHTS)
                pe.wait_ge(r_ok, at[0])
                pe.wait_ge(tt_ok, at[1])
                pairs(grid(BU[j]), lambda r, a: TT[r, b, a], lambda r, a: R[r, b, a]).then_inc(u_ps, 1)

            def answer(c, u, j):
                b = 2 * u + j
                at = counts(c * 4 + (2 * u + 2 + START), c * 4 + (b + START), c * 4 + (2 * u + 2 + START))
                pe.wait_ge(weights, ALL_WEIGHTS)
                pe.wait_ge(u_ok, at[0])
                pe.wait_ge(o_ok, at[1])
                for a in range(HP):
                    for h in range(2):
                        r = slice(C * h, C * h + C)
                        pe.matmul(grid(BO)[r, a], N[r, b, a], QT[r, a, b], start=True, stop=False)
                        last = pe.matmul(grid(BO)[r, a], U[r, b, a], PT[r, b, a], start=False, stop=True)
                last.then_inc(o_ps, 1)
                at = counts(c * 4 + (b + START))
                pe.wait_ge(weights, ALL_WEIGHTS)
                pe.wait_ge(n_ok, at[0])
                pairs(grid(BN), lambda r, a: K[r, b, a], lambda r, a: U[r, b, a]).then_inc(n_ps, 1)

            def project(c, u):
                pe.wait_ge(o_ok, c * 4 + (2 * u + 2 + START))
                for a in range(HP):
                    last = pe.matmul(bank[BY][:, 0:D], OT[:, a, 2 * u:2 * u + 2].rearrange("p b t -> p (b t)"),
                                     wout[:, a], start=(a == 0), stop=(a == HP - 1))
                last.then_inc(y_ps, 1)

            def state_part(c, u, s):
                if s == 0:
                    recall(c, u, 0)
                    recall(c, u, 1)
                if s == 1:
                    solve(c, u, 0)
                    solve(c, u, 1)
                if s == 2:
                    answer(c, u, 0)
                if s == 3:
                    answer(c, u, 1)
                if s == 4:
                    project(c, u)

            def front_part(c, u, s):
                if s == 4:
                    turn_x(c, u)
                if s == 5:
                    rates(c, u)
                    keys(c, u, 0)
                if s == 6:
                    keys(c, u, 1)
                if s == 8:
                    queries(c, u, 0)
                if s == 9:
                    queries(c, u, 1)
                if s == 10:
                    turn_keys(c, u, 0)
                if s == 11:
                    turn_keys(c, u, 1)

            def pair_block(c, u, state=True, front=True):
                before, after = ((c - 1, 1), (c, 1)) if u == 0 else ((c, 0), (c + 1, 0))

                def slot(s):
                    if state:
                        state_part(*before, s)
                    if front:
                        front_part(*after, s)

                inverse(c, u, slot)

            pe.wait_ge(weights, ALL_WEIGHTS)
            pe.wait_ge(state0, 2 + SUB + START)
            steps(pe, whole(front_part), pair_block, whole(state_part))
    clear(nc, held)


E_N = 8
F = 1024
NT = B * S // P
GT = 4


def expert_layer(nc, name, consts, x, Wr, br, W1, b1, W2, b2, cap, keeps_dropped, out, slots, answers):
    nrow = cap // P if cap % P == 0 else 2
    rp = cap // nrow
    nhalf = 2 if cap > 512 else 1
    half = cap // nhalf
    FT = F // P
    biased = b1 is not None
    last_slot = E_N * cap - 1

    held = []
    with ExitStack() as ctx:
        def sb(n, shape, dt=F32):
            return ctx.enter_context(nc.sbuf_tensor(f"{name}_{n}", shape, dt))

        def sem(n):
            held.append(nc.alloc_semaphore(name=f"{name}_{n}"))
            return held[-1]

        bank = [ctx.enter_context(nc.psum_tensor(f"{name}_bank{i}", [P, 512], F32)) for i in range(8)]

        cst = sb("cst", [P, C_ALL])
        wr = sb("wr", [P, KD, E_N])
        bias_r = sb("bias_r", [P, E_N])
        x_all = sb("x_all", [P, NT, D])
        xn_all = sb("xn_all", [P, NT, D])
        xn = sb("xn", [P, GT, D])
        bn = sb("bn", [P, GT, 6])
        mv = sb("mv", [P, GT, 2])
        eps = sb("eps", [P, 1])
        std = sb("std", [P, GT])
        rstd = sb("rstd", [P, GT])
        xT = sb("xT", [P, GT, KD, P])
        logit = sb("logit", [P, NT, E_N])
        route = [sb(f"route{i}", [P, NT, E_N]) for i in range(3)]
        per_token = [sb(f"token{i}", [P, NT]) for i in range(12)]
        reset = sb("reset", [P, E_N, NT])
        total = sb("total", [P, E_N, NT])
        running = sb("running", [P, E_N, NT])
        slot_in = sb("slot_in", [P, NT], I32)
        slot_out = sb("slot_out", [P, NT], I32)
        zero = sb("zero", [P, 4 * D])
        w1 = sb("w1", [P, 2, KD, F])
        w2 = sb("w2", [P, 2, FT, D])
        rows = sb("rows", [rp, 2, nrow, D])
        rowsT = sb("rowsT", [P, KD, cap])
        hid = sb("hid", [P, FT, cap])
        ans = sb("ans", [rp, nrow, D])
        if biased:
            b1_sb = sb("b1", [P, E_N, FT])
            b2_sb = sb("b2", [1, E_N, D])
        got = sb("got", [P, NT, D])

        const_in, x_in, zeroed, zero_ok, eps_ok = map(sem, ("const_in", "x_in", "zeroed", "zero_ok", "eps_ok"))
        w_in = [sem("w_in0"), sem("w_in1")]
        stats, moments, std_ok, rstd_ok, xn_ok, xn_kept, xT_ps, xT_ok, lg_ps, lg_ok = map(
            sem, ("stats", "moments", "std_ok", "rstd_ok", "xn_ok", "xn_kept", "xT_ps", "xT_ok", "lg_ps", "lg_ok"))
        chain, ex_ok, once_ok, count_ps, slot_ok = map(sem, ("chain", "ex_ok", "once_ok", "count_ps", "slot_ok"))
        sent = sem("sent")
        rows_in, rT_ps, rT_ok, h_ps, h_act, h_dve, a_ps, a_ok, a_out = map(
            sem, ("rows_in", "rT_ps", "rT_ok", "h_ps", "h_act", "h_dve", "a_ps", "a_ok", "a_out"))
        mixed, out_ok, stored = map(sem, ("mixed", "out_ok", "stored"))
        fetched = [sem(f"fetched{g}") for g in range(NT // GT)]

        ident = cst[:, C_ID:C_ID + P]
        N_CONST = 2 + (3 if biased else 0)
        x_t = x.rearrange("b s d -> (b s) d").rearrange("(n p) d -> p n d", p=P)
        out_t = out.rearrange("b s d -> (b s) d").rearrange("(n p) d -> p n d", p=P)
        slots_t = slots.rearrange("(e j p) d -> e p j d", j=nrow, p=rp)
        answers_t = answers.rearrange("(e j p) d -> e p j d", j=nrow, p=rp)
        blocks = [(f, q) for f in range(FT) for q in range(nhalf)]
        NB = len(blocks)
        on_act = NB if biased else NB // 2

        def over_experts(v):
            return v.unsqueeze(2).broadcast_to([P, NT, E_N])

        block = ctx.enter_context(nc.Block())

        @block.sync
        def _(sp):
            sp.dma_start(cst[:], consts).then_inc(const_in, 16)
            sp.dma_start(wr[:], Wr.rearrange("(k p) n -> p k n", p=P)).then_inc(const_in, 16)
            if biased:
                sp.dma_start(bias_r[:], br.unsqueeze(0).broadcast_to([P, E_N])).then_inc(const_in, 16)
                sp.dma_start(b2_sb[:], b2.unsqueeze(0)).then_inc(const_in, 16)
                sp.dma_start(b1_sb[:], b1.rearrange("e (f p) -> p e f", p=P),
                             allow_slow_non_contiguous=True).then_inc(const_in, 16)
            with sp.Fori(0, NT // GT) as g:
                sp.wait_ge(x_in, g * 16)
                sp.dma_start(x_all[:, bass.ts(g, GT)], x_t[:, bass.ts(g, GT)]).then_inc(x_in, 16)
            sp.wait_ge(zero_ok, 1)
            per = E_N * cap // P // 10 * D * 2
            zrow = slots.rearrange("(p r) d -> p (r d)", p=P)
            step = 4 * D if zrow.shape[1] % (4 * D) == 0 else 2 * D
            for i in range(zrow.shape[1] // step):
                sp.dma_start(zrow[:, i * step:(i + 1) * step], zero[:, 0:step]).then_inc(zeroed, 16)
            sp.wait_ge(sent, 16 * NT)
            with sp.Fori(0, E_N // 2) as i:
                for u in range(2):
                    e = i * 2 + u
                    sp.wait_ge(a_ps, (i * 2 + u) * nrow if u == 0 else i * 2 * nrow)
                    sp.dma_start(rows[:, u], slots_t[e]).then_inc(rows_in, 16)
                    sp.wait_ge(a_ok, (i * 2 + u + 1) * nrow)
                    sp.dma_start(answers_t[e], ans[:]).then_inc(a_out, 16)
            for g in range(NT // GT):
                sp.wait_ge(out_ok, GT * (g + 1))
                sp.dma_start(out_t[:, g * GT:(g + 1) * GT], got[:, g * GT:(g + 1) * GT]).then_inc(stored, 16)
            sp.wait_ge(stored, 16 * (NT // GT))

        @block.gpsimd
        def _(pool):
            pool.memset(zero[:], 0.0).then_inc(zero_ok, 1)
            n_zero = slots.shape[0] // P * D // (4 * D if slots.shape[0] // P * D % (4 * D) == 0 else 2 * D)
            pool.wait_ge(slot_ok, 2)
            pool.wait_ge(xn_kept, NT // GT)
            pool.wait_ge(zeroed, 16 * n_zero)
            for t in range(NT):
                pool.indirect_dma_start(out=slots, out_offset=bass.IndirectOffsetOnAxis(ap=slot_in[:, t:t + 1], axis=0),
                                        in_=xn_all[:, t], in_offset=None, bounds_check=last_slot,
                                        oob_is_err=False).then_inc(sent, 16)
            pool.wait_ge(a_out, 16 * E_N)
            for t in range(NT):
                pool.indirect_dma_start(out=got[:, t], out_offset=None, in_=answers,
                                        in_offset=bass.IndirectOffsetOnAxis(ap=slot_out[:, t:t + 1], axis=0),
                                        bounds_check=last_slot, oob_is_err=False).then_inc(fetched[t // GT], 16)

        @block.scalar
        def _(act):
            counts = Counts(act, name)
            act.wait_ge(eps_ok, 1)
            with act.Fori(0, NT // GT) as g:
                act.wait_ge(moments, g * GT + GT)
                act.activation(std[:], mv[:, :, 1], ACT.Sqrt, bias=eps[:, 0:1]).then_inc(std_ok, 1)
                at = counts(g * GT + GT)
                act.wait_ge(eps_ok, 1)
                act.wait_ge(xn_ok, at[0])
                act.activation(xn_all[:, bass.ts(g, GT)], xn[:], ACT.Copy).then_inc(xn_kept, 1)
                for u in range(2):
                    act.wait_ge(xT_ps, g * 2 + u + 1)
                    act.activation(xT[:, 2 * u:2 * u + 2].rearrange("p j k t -> p (j k t)"), bank[u][:],
                                   ACT.Copy).then_inc(xT_ok, 1)
            act.wait_ge(chain, 2)
            act.activation(route[1][:], route[0][:], ACT.Exp).then_inc(ex_ok, 1)
            with act.Fori(0, E_N // 2) as i:
                for u in range(2):
                    e = i * 2 + u
                    act.wait_ge(a_ps, i * 2 * nrow)
                    act.dma_start(w1[:, u], W1[e].rearrange("(k p) f -> p k f", p=P)).then_inc(w_in[u], 16)
                    act.dma_start(w2[:, u], W2[e].rearrange("(f p) d -> p f d", p=P)).then_inc(w_in[u], 16)
                for u in range(2):
                    e = i * 2 + u
                    for n, (f, q) in enumerate(blocks):
                        if not biased and n % 2:
                            continue
                        act.wait_ge(h_ps, e * NB + n + 1)
                        dst = hid[:, f, q * half:(q + 1) * half]
                        if biased:
                            act.activation(dst, bank[2 + n % 4][:, 0:half], ACT.Gelu_apprx_tanh,
                                           bias=b1_sb[:, e, f:f + 1]).then_inc(h_act, 1)
                        else:
                            act.activation(dst, bank[2 + n % 4][:, 0:half], ACT.Relu).then_inc(h_act, 1)

        @block.vector
        def _(dve):
            counts = Counts(dve, name)
            dve.memset(eps[:], LN_EPS).then_inc(eps_ok, 1)
            dve.memset(reset[:], 1.0).then_inc(once_ok, 1)
            dve.wait_ge(once_ok, 1)
            dve.memset(reset[:, :, 0:1], 0.0).then_inc(once_ok, 1)
            dve.wait_ge(const_in, 16 * N_CONST)
            with dve.Fori(0, NT // GT) as g:
                dve.wait_ge(x_in, g * 16 + 16)
                for j in range(GT):
                    dve.bn_stats(bn[:, j], x_all[:, g * GT + j]).then_inc(stats, 1)
                for j in range(GT):
                    at = counts(g * GT + j + 1)
                    dve.wait_ge(const_in, 16 * N_CONST)
                    dve.wait_ge(stats, at[0])
                    dve.bn_aggr(mv[:, j], bn[:, j]).then_inc(moments, 1)
                dve.wait_ge(std_ok, g + 1)
                dve.reciprocal(rstd[:], std[:]).then_inc(rstd_ok, 1)
                dve.wait_ge(rstd_ok, g + 1)
                dve.wait_ge(xn_kept, g)
                dve.wait_ge(xT_ps, g * 2)
                for j in range(GT):
                    dve.tensor_scalar(xn[:, j], x_all[:, g * GT + j], mv[:, j, 0:1], rstd[:, j:j + 1],
                                      ALU.subtract, ALU.mult).then_inc(xn_ok, 1)
                dve.wait_ge(lg_ps, g + 1)
                if biased:
                    dve.tensor_tensor(logit[:, bass.ts(g, GT)],
                                      bank[6][:, 0:GT * E_N].rearrange("p (j e) -> p j e", j=GT),
                                      bias_r[:].unsqueeze(1).broadcast_to([P, GT, E_N]), ALU.add).then_inc(lg_ok, 1)
                else:
                    dve.tensor_copy(logit[:, bass.ts(g, GT)],
                                    bank[6][:, 0:GT * E_N].rearrange("p (j e) -> p j e", j=GT)).then_inc(lg_ok, 1)
            n = [0]

            def step(ins):
                n[0] += 1
                ins.then_inc(chain, 1)
                dve.wait_ge(chain, n[0])

            top, esum, prob, rank, pos, kept, factor, dropped, slot, sin, sout, _ = (v[:] for v in per_token)
            shifted, mask, work = (r[:] for r in route)
            dve.wait_ge(lg_ok, NT // GT)
            step(dve.tensor_reduce(top, logit[:], AX.X, ALU.max))
            step(dve.tensor_tensor(shifted, logit[:], over_experts(top), ALU.subtract))
            dve.wait_ge(ex_ok, 1)
            step(dve.tensor_reduce(esum, mask, AX.X, ALU.add))
            step(dve.reciprocal(prob, esum))
            step(dve.tensor_tensor(work, logit[:], over_experts(top), ALU.is_equal))
            step(dve.tensor_tensor(mask, work, cst[:, C_RANK:C_RANK + E_N].unsqueeze(1).broadcast_to([P, NT, E_N]),
                                   ALU.mult))
            step(dve.tensor_reduce(rank, mask, AX.X, ALU.max))
            step(dve.tensor_tensor(work, mask, over_experts(rank), ALU.is_equal))
            dve.wait_ge(count_ps, 2)
            step(dve.tensor_copy(total[:], bank[1][:, 0:NT * E_N].rearrange("p (t e) -> p e t", e=E_N)))
            step(dve.tensor_tensor_scan(running[:].rearrange("p e t -> p (e t)"), reset[:].rearrange("p e t -> p (e t)"),
                                        total[:].rearrange("p e t -> p (e t)"), 0.0, ALU.mult, ALU.add))
            step(dve.tensor_tensor(running[:], running[:], total[:], ALU.subtract))
            step(dve.tensor_tensor(shifted, bank[0][:, 0:NT * E_N].rearrange("p (t e) -> p t e", e=E_N),
                                   running[:].rearrange("p e t -> p t e"), ALU.add))
            step(dve.tensor_tensor(mask, shifted, work, ALU.mult))
            step(dve.tensor_reduce(pos, mask, AX.X, ALU.add))
            step(dve.tensor_scalar(kept, pos, float(cap), None, ALU.is_le))
            step(dve.tensor_scalar(dropped, kept, -1.0, 1.0, ALU.mult, ALU.add))
            step(dve.tensor_tensor(factor, kept, prob, ALU.mult))
            step(dve.tensor_scalar(slot, rank, -float(cap), float(E_N * cap - 1), ALU.mult, ALU.add))
            step(dve.tensor_tensor(slot, slot, pos, ALU.add))
            step(dve.tensor_scalar(sin, dropped, float(2 * E_N * cap), None, ALU.mult))
            step(dve.tensor_tensor(sin, sin, slot, ALU.add))
            step(dve.tensor_scalar(sout, slot, float(last_slot), None, ALU.min))
            dve.tensor_copy(slot_in[:], sin).then_inc(slot_ok, 1)
            dve.tensor_copy(slot_out[:], sout).then_inc(slot_ok, 1)

            with dve.Fori(0, E_N // 2) as i:
                for u in range(2):
                    e = i * 2 + u
                    for j in range(nrow):
                        dve.wait_ge(rT_ps, e * nrow + j + 1)
                        dve.tensor_copy(rowsT[:, :, j * rp:(j + 1) * rp],
                                        bank[j % 2][:, 0:KD * rp].rearrange("p (k t) -> p k t", k=KD)).then_inc(rT_ok, 1)
                    if not biased:
                        for n_, (f, q) in enumerate(blocks):
                            if n_ % 2 == 0:
                                continue
                            dve.wait_ge(h_ps, e * NB + n_ + 1)
                            dve.tensor_scalar(hid[:, f, q * half:(q + 1) * half], bank[2 + n_ % 4][:, 0:half],
                                              0.0, None, ALU.max).then_inc(h_dve, 1)
                    dve.wait_ge(a_out, e * 16)
                    for j in range(nrow):
                        dve.wait_ge(a_ps, e * nrow + j + 1)
                        dve.tensor_copy(ans[:, j], bank[6 + j % 2][0:rp, 0:D]).then_inc(a_ok, 1)
            for t in range(NT):
                if t % GT == 0:
                    dve.wait_ge(fetched[t // GT], 16 * GT)
                if keeps_dropped:
                    dve.scalar_tensor_tensor(got[:, t], got[:, t], factor[:, t:t + 1], x_all[:, t],
                                             ALU.mult, ALU.add).then_inc(mixed, 1)
                    dve.wait_ge(mixed, t + 1)
                    dve.scalar_tensor_tensor(got[:, t], xn_all[:, t], dropped[:, t:t + 1], got[:, t],
                                             ALU.mult, ALU.add).then_inc(out_ok, 1)
                else:
                    dve.scalar_tensor_tensor(got[:, t], got[:, t], factor[:, t:t + 1], x_all[:, t],
                                             ALU.mult, ALU.add).then_inc(out_ok, 1)

        @block.tensor
        def _(pe):
            counts = Counts(pe, name)
            pe.wait_ge(const_in, 16 * N_CONST)
            with pe.Fori(0, NT // GT) as g:
                for u in range(2):
                    pe.wait_ge(xn_ok, g * GT + 2 * u + 2)
                    pe.wait_ge(xT_ok, g * 2)
                    for j in range(2):
                        for k in range(KD):
                            last = pe.transpose(bank[u][:, (j * KD + k) * P:(j * KD + k + 1) * P],
                                                xn[:, 2 * u + j, k * P:(k + 1) * P], ident)
                    last.then_inc(xT_ps, 1)
                pe.wait_ge(xT_ok, g * 2 + 2)
                pe.wait_ge(lg_ok, g)
                for j in range(GT):
                    for k in range(KD):
                        last = pe.matmul(bank[6][:, j * E_N:(j + 1) * E_N], xT[:, j, k], wr[:, k],
                                         start=(k == 0), stop=(k == KD - 1))
                last.then_inc(lg_ps, 1)
            pe.wait_ge(chain, 8)
            oh = route[2][:].rearrange("p t e -> p (t e)")
            pe.matmul(bank[0][:, 0:NT * E_N], cst[:, C_TRI:C_TRI + P], oh, start=True, stop=True).then_inc(count_ps, 1)
            pe.matmul(bank[1][:, 0:NT * E_N], cst[:, C_ONE:C_ONE + P], oh, start=True, stop=True).then_inc(count_ps, 1)
            pe.wait_ge(slot_ok, 2)
            with pe.Fori(0, E_N // 2) as i:
                for u in range(2):
                    e = i * 2 + u
                    pe.wait_ge(rows_in, e * 16 + 16)
                    for j in range(nrow):
                        pe.wait_ge(rT_ok, e * nrow + j - 1 if j >= 2 else e * nrow)
                        for k in range(KD):
                            last = pe.transpose(bank[j % 2][:, k * rp:(k + 1) * rp],
                                                rows[:, u, j, k * P:(k + 1) * P], ident[0:rp, 0:rp])
                        last.then_inc(rT_ps, 1)
                    pe.wait_ge(rT_ok, (e + 1) * nrow)
                    pe.wait_ge(w_in[u], i * 32 + 32)
                    for n, (f, q) in enumerate(blocks):
                        if biased:
                            pe.wait_ge(h_act, e * NB + max(n - 3, 0))
                        elif n % 2 == 0:
                            pe.wait_ge(h_act, e * (NB // 2) + max(n // 2 - 1, 0))
                        else:
                            pe.wait_ge(h_dve, e * (NB // 2) + max(n // 2 - 1, 0))
                        for k in range(KD):
                            last = pe.matmul(bank[2 + n % 4][:, 0:half], w1[:, u, k, f * P:(f + 1) * P],
                                             rowsT[:, k, q * half:(q + 1) * half],
                                             start=(k == 0), stop=(k == KD - 1))
                        last.then_inc(h_ps, 1)
                    for j in range(nrow):
                        at = counts(e * nrow + max(j - 1, 0), (e + 1) * on_act, (e + 1) * (NB - on_act))
                        pe.wait_ge(const_in, 16 * N_CONST)
                        pe.wait_ge(a_ok, at[0])
                        if j == 0:
                            pe.wait_ge(h_act, at[1])
                            pe.wait_ge(h_dve, at[2])
                        if biased:
                            pe.matmul(bank[6 + j % 2][0:rp, 0:D], cst[0:1, C_ONE:C_ONE + rp], b2_sb[:, e],
                                      start=True, stop=False)
                        for f in range(FT):
                            last = pe.matmul(bank[6 + j % 2][0:rp, 0:D], hid[:, f, j * rp:(j + 1) * rp],
                                             w2[:, u, f], start=(f == 0 and not biased), stop=(f == FT - 1))
                        last.then_inc(a_ps, 1)
    clear(nc, held)


TB = S // P


def attention_layer(nc, consts, x, WqT, WkT, WvT, bq, bk, bv, WoT, bo, out):
    QH = S // 512
    UNITS = 2 * TB
    held = []
    with ExitStack() as ctx:
        def sb(n, shape, dt=F32):
            return ctx.enter_context(nc.sbuf_tensor(f"at_{n}", shape, dt))

        def sem(n):
            held.append(nc.alloc_semaphore(name=f"at_{n}"))
            return held[-1]

        score = [ctx.enter_context(nc.psum_tensor(f"at_score{i}", [P, S], F32)) for i in range(2)]
        mix = ctx.enter_context(nc.psum_tensor("at_mix", [P, S], F32))
        bank = [ctx.enter_context(nc.psum_tensor(f"at_bank{i}", [P, 512], F32)) for i in range(2)]

        cst = sb("cst", [P, C_ONE + P])
        w = sb("w", [P, 2, 3, KD, P])
        wo = sb("wo", [P, HP, D])
        b_q, b_k = sb("b_q", [P, HP]), sb("b_k", [P, HP])
        b_v = sb("b_v", [P, H * DH])
        b_o = sb("b_o", [1, D])
        x_all = sb("x_all", [P, TB, D])
        xn = sb("xn", [P, TB, D])
        bn = sb("bn", [P, TB, 6])
        mv = sb("mv", [P, TB, 2])
        eps = sb("eps", [P, 1])
        std = sb("std", [P, TB])
        rstd = sb("rstd", [P, TB])
        xT = sb("xT", [P, KD, S])
        Q = sb("Q", [P, 2, S])
        K = sb("K", [P, S])
        V = sb("V", [P, TB, P])
        E = sb("E", [P, 4, S])
        top, ntop, esum, rsum = (sb(n, [P, 4]) for n in ("top", "ntop", "esum", "rsum"))
        Vs = sb("Vs", [P, 4, DH])
        CT = sb("CT", [P, HP, S])
        y = sb("y", [P, TB, D])

        const_in, zero_ok, x_in = map(sem, ("const_in", "zero_ok", "x_in"))
        y_out = sem("y_out")
        w_in = [sem("w_in0"), sem("w_in1")]
        stats, moments, std_ok, rstd_ok, xn_ok, xT_ps, xT_ok = map(
            sem, ("stats", "moments", "std_ok", "rstd_ok", "xn_ok", "xT_ps", "xT_ok"))
        q_ps, q_ok, k_ps, k_ok, v_ps, v_ok = map(sem, ("q_ps", "q_ok", "k_ps", "k_ok", "v_ps", "v_ok"))
        s_ps, top_ok, ntop_ok, e_ok, rsum_ok, vs_ok, c_ps, ct_ok = map(
            sem, ("s_ps", "top_ok", "ntop_ok", "e_ok", "rsum_ok", "vs_ok", "c_ps", "ct_ok"))
        o_ps, y_ok = sem("o_ps"), sem("y_ok")

        ident = cst[:, C_ID:C_ID + P]
        N_CONST = 6
        x_t = x.rearrange("b (n p) d -> b p n d", p=P)
        out_t = out.rearrange("b (n p) d -> b p n d", p=P)

        block = ctx.enter_context(nc.Block())

        @block.sync
        def _(sp):
            sp.dma_start(cst[:], consts[:, 0:C_ONE + P]).then_inc(const_in, 16)
            sp.dma_start(b_q[:], bq.rearrange("(a p) -> p a", p=P), allow_slow_non_contiguous=True).then_inc(const_in, 16)
            sp.dma_start(b_k[:], bk.rearrange("(a p) -> p a", p=P), allow_slow_non_contiguous=True).then_inc(const_in, 16)
            sp.dma_start(b_v[:], bv.unsqueeze(0).broadcast_to([P, H * DH])).then_inc(const_in, 16)
            sp.dma_start(b_o[:], bo.unsqueeze(0)).then_inc(const_in, 16)
            sp.dma_start(wo[:], WoT.rearrange("(a p) d -> p a d", p=P)).then_inc(const_in, 16)
            with sp.Fori(0, B) as b:
                sp.wait_ge(y_ok, b * TB)
                sp.dma_start(x_all[:], x_t[b]).then_inc(x_in, 16)
                with sp.Fori(0, HP // 2) as a2:
                    for u in range(2):
                        a = a2 * 2 + u
                        sp.wait_ge(v_ps, (b * HP + a2 * 2) * 2)
                        for i, wt in enumerate((WqT, WkT, WvT)):
                            sp.dma_start(w[:, u, i], wt.rearrange("(k p) n -> p k n", p=P)[:, :, bass.ts(a, P)]
                                         ).then_inc(w_in[u], 16)

        @block.gpsimd
        def _(pool):
            pool.memset(Q[:], 0.0).then_inc(zero_ok, 1)
            with pool.Fori(0, B) as b:
                pool.wait_ge(y_ok, b * TB + TB)
                pool.dma_start(out_t[b], y[:]).then_inc(y_out, 16)
            pool.wait_ge(y_out, 16 * B)

        @block.scalar
        def _(act):
            counts = Counts(act, "at")
            act.wait_ge(const_in, 16 * N_CONST)
            act.wait_ge(zero_ok, 2)
            with act.Fori(0, B) as b:
                act.wait_ge(moments, b * TB + TB)
                act.activation(std[:], mv[:, :, 1], ACT.Sqrt, bias=eps[:, 0:1]).then_inc(std_ok, 1)
                for u in range(TB // 2):
                    act.wait_ge(xT_ps, b * 4 + u + 1)
                    act.activation(xT[:, :, 2 * u * P:(2 * u + 2) * P].rearrange("p k (j t) -> p k j t", j=2),
                                   bank[u % 2][:].rearrange("p (k j t) -> p k j t", k=KD, j=2),
                                   ACT.Copy).then_inc(xT_ok, 1)
                with act.Fori(0, HP) as a:
                    n = b * HP + a
                    for q in range(QH):
                        at = counts(n * 2 + q + 1)
                        act.wait_ge(zero_ok, 2)
                        act.wait_ge(q_ps, at[0])
                        for h in range(2):
                            r = slice(DH * h, DH * h + DH)
                            act.activation(Q[r, h, q * 512:(q + 1) * 512], bank[q][r], ACT.Identity,
                                           bias=b_q[r, bass.ds(a, 1)]).then_inc(q_ok, 1)
                    for i in range(UNITS):
                        act.wait_ge(ntop_ok, n * UNITS + i + 1)
                        if i >= 4:
                            act.wait_ge(c_ps, n * TB + i // 2 - 1)
                        act.activation(E[:, i % 4], score[i % 2][:], ACT.Exp, scale=1.0 / 8.0,
                                       bias=ntop[:, i % 4:i % 4 + 1], accum_out=esum[:, i % 4:i % 4 + 1]
                                       ).then_inc(e_ok, 1)
                    at = counts(n * TB + TB)
                    act.wait_ge(zero_ok, 2)
                    act.wait_ge(c_ps, at[0])
                    act.activation(CT[:, bass.ds(a, 1)].rearrange("p o s -> p (o s)"), mix[:], ACT.Copy).then_inc(ct_ok, 1)

        @block.vector
        def _(dve):
            counts = Counts(dve, "at")
            dve.memset(eps[:], LN_EPS).then_inc(zero_ok, 1)
            dve.wait_ge(const_in, 16 * N_CONST)
            with dve.Fori(0, B) as b:
                dve.wait_ge(x_in, b * 16 + 16)
                for j in range(TB):
                    dve.bn_stats(bn[:, j], x_all[:, j]).then_inc(stats, 1)
                for j in range(TB):
                    at = counts(b * TB + j + 1)
                    dve.wait_ge(const_in, 16 * N_CONST)
                    dve.wait_ge(stats, at[0])
                    dve.bn_aggr(mv[:, j], bn[:, j]).then_inc(moments, 1)
                dve.wait_ge(std_ok, b + 1)
                dve.reciprocal(rstd[:], std[:]).then_inc(rstd_ok, 1)
                dve.wait_ge(rstd_ok, b + 1)
                for j in range(TB):
                    dve.tensor_scalar(xn[:, j], x_all[:, j], mv[:, j, 0:1], rstd[:, j:j + 1],
                                      ALU.subtract, ALU.mult).then_inc(xn_ok, 1)
                with dve.Fori(0, HP) as a:
                    n = b * HP + a
                    for q in range(QH):
                        dve.wait_ge(k_ps, n * 2 + q + 1)
                        dve.tensor_scalar(K[:, q * 512:(q + 1) * 512], bank[q][:], b_k[:, bass.ds(a, 1)], None,
                                          ALU.add).then_inc(k_ok, 1)
                    for q in range(2):
                        dve.wait_ge(v_ps, n * 2 + q + 1)
                        dve.tensor_tensor(V[:, 4 * q:4 * q + 4], bank[q][:].rearrange("p (j d) -> p j d", j=4),
                                          b_v[:, bass.ts(a, P)].unsqueeze(1).broadcast_to([P, 4, P]),
                                          ALU.add).then_inc(v_ok, 1)
                    def scale_value(i):
                        dve.wait_ge(e_ok, n * UNITS + i + 1)
                        dve.reciprocal(rsum[:, i % 4:i % 4 + 1], esum[:, i % 4:i % 4 + 1]).then_inc(rsum_ok, 1)
                        dve.wait_ge(rsum_ok, n * UNITS + i + 1)
                        if i >= 4:
                            dve.wait_ge(c_ps, n * TB + i // 2 - 1)
                        if i == 0:
                            dve.wait_ge(v_ok, n * 2 + 2)
                        h = i % 2
                        dve.tensor_scalar(Vs[:, i % 4], V[:, i // 2, DH * h:DH * h + DH], rsum[:, i % 4:i % 4 + 1],
                                          None, ALU.mult).then_inc(vs_ok, 1)
                    for i in range(UNITS):
                        dve.wait_ge(s_ps, n * UNITS + i + 1)
                        if i == 0:
                            dve.wait_ge(e_ok, n * UNITS)
                        dve.tensor_reduce(top[:, i % 4:i % 4 + 1], score[i % 2][:], AX.X, ALU.max).then_inc(top_ok, 1)
                        dve.wait_ge(top_ok, n * UNITS + i + 1)
                        dve.tensor_scalar(ntop[:, i % 4:i % 4 + 1], top[:, i % 4:i % 4 + 1], -1.0 / 8.0, None,
                                          ALU.mult).then_inc(ntop_ok, 1)
                        if i >= 1:
                            scale_value(i - 1)
                    scale_value(UNITS - 1)
                dve.wait_ge(y_out, b * 16)
                for j in range(TB):
                    dve.wait_ge(o_ps, b * TB + j + 1)
                    dve.tensor_tensor(y[:, j], bank[j % 2][:, 0:D], x_all[:, j], ALU.add).then_inc(y_ok, 1)

        @block.tensor
        def _(pe):
            counts = Counts(pe, "at")
            pe.wait_ge(const_in, 16 * N_CONST)
            pe.wait_ge(zero_ok, 2)
            with pe.Fori(0, B) as b:
                for u in range(TB // 2):
                    pe.wait_ge(xn_ok, b * TB + 2 * u + 2)
                    if u >= 2:
                        pe.wait_ge(xT_ok, b * 4 + u - 1)
                    else:
                        pe.wait_ge(y_ok, b * TB)
                    for k in range(KD):
                        for j in range(2):
                            last = pe.transpose(bank[u % 2][:, (k * 2 + j) * P:(k * 2 + j + 1) * P],
                                                xn[:, 2 * u + j, k * P:(k + 1) * P], ident)
                    last.then_inc(xT_ps, 1)
                at = counts(b * 4 + 4)
                pe.wait_ge(const_in, 16 * N_CONST)
                pe.wait_ge(xT_ok, at[0])
                with pe.Fori(0, HP // 2) as a2:
                    for u in range(2):
                        n = b * HP + a2 * 2 + u
                        pe.wait_ge(w_in[u], (b * 4 + a2) * 48 + 48)
                        for q in range(QH):
                            for k in range(KD):
                                last = pe.matmul(bank[q][:], w[:, u, 0, k], xT[:, k, q * 512:(q + 1) * 512],
                                                 start=(k == 0), stop=(k == KD - 1))
                            last.then_inc(q_ps, 1)
                        for q in range(QH):
                            pe.wait_ge(q_ok, n * 4 + 2 * q + 2)
                            for k in range(KD):
                                last = pe.matmul(bank[q][:], w[:, u, 1, k], xT[:, k, q * 512:(q + 1) * 512],
                                                 start=(k == 0), stop=(k == KD - 1))
                            last.then_inc(k_ps, 1)
                        for q in range(2):
                            pe.wait_ge(k_ok, n * 2 + q + 1)
                            for j in range(4):
                                for k in range(KD):
                                    last = pe.matmul(bank[q][:, j * P:(j + 1) * P],
                                                     xT[:, k, (4 * q + j) * P:(4 * q + j + 1) * P], w[:, u, 2, k],
                                                     start=(k == 0), stop=(k == KD - 1))
                            last.then_inc(v_ps, 1)
                        pe.wait_ge(v_ok, n * 2 + 2)

                        def scores(i):
                            if i >= 2:
                                pe.wait_ge(e_ok, n * UNITS + i - 1)
                            for q in range(QH):
                                last = pe.matmul(score[i % 2][:, q * 512:(q + 1) * 512],
                                                 K[:, (i // 2) * P:(i // 2 + 1) * P],
                                                 Q[:, i % 2, q * 512:(q + 1) * 512], start=True, stop=True)
                            last.then_inc(s_ps, 1)

                        def context(t):
                            pe.wait_ge(vs_ok, n * UNITS + 2 * t + 2)
                            if t == 0:
                                pe.wait_ge(ct_ok, n)
                            for q in range(QH):
                                for h in range(2):
                                    i = (2 * t + h) % 4
                                    last = pe.matmul(mix[DH * h:DH * h + DH, q * 512:(q + 1) * 512], Vs[:, i],
                                                     E[:, i, q * 512:(q + 1) * 512],
                                                     start=(t == 0), stop=(t == TB - 1))
                            last.then_inc(c_ps, 1)

                        for t in range(TB):
                            scores(2 * t)
                            scores(2 * t + 1)
                            if t:
                                context(t - 1)
                        context(TB - 1)
                pe.wait_ge(ct_ok, b * HP + HP)
                for j in range(TB):
                    if j >= 2:
                        pe.wait_ge(y_ok, b * TB + j - 1)
                    pe.matmul(bank[j % 2][:, 0:D], cst[0:1, C_ONE:C_ONE + P], b_o[:], start=True, stop=False)
                    for a in range(HP):
                        last = pe.matmul(bank[j % 2][:, 0:D], CT[:, a, j * P:(j + 1) * P], wo[:, a],
                                         start=False, stop=(a == HP - 1))
                    last.then_inc(o_ps, 1)
    clear(nc, held)


def seq_kernel(nc, consts, x, Wq, Wk, Wv, Wbeta, b_beta, Wout, Wr, W1, W2,
               WqT, bq, WkT, bk, WvT, bv, WoT, bo, gate_w, gate_b, w1, b1, w2, b2, out):
    def scratch(name, shape):
        return nc.dram_tensor(name, shape, F32, kind="Internal").ap()

    x1, x2, x3 = (scratch(n, [B, S, D]) for n in ("x1", "x2", "x3"))
    cap0, cap1 = int(1.25 * B * S / E_N), 160
    slots0, answers0 = scratch("slots0", [E_N * cap0, D]), scratch("answers0", [E_N * cap0, D])
    slots1, answers1 = scratch("slots1", [E_N * cap1, D]), scratch("answers1", [E_N * cap1, D])
    delta_layer(nc, consts, x, Wq, Wk, Wv, Wbeta, b_beta, Wout, x1)
    expert_layer(nc, "m0", consts, x1, Wr, None, W1, None, W2, None, cap0, True, x2, slots0, answers0)
    attention_layer(nc, consts, x2, WqT, WkT, WvT, bq, bk, bv, WoT, bo, x3)
    expert_layer(nc, "m1", consts, x3, gate_w, gate_b, w1, b1, w2, b2, cap1, False, out, slots1, answers1)


def kernel(**inputs):
    import concourse.bacc as bacc
    from concourse.bass_utils import run_bass_kernel_spmd

    def rows(name):
        a = np.asarray(inputs[name])
        return np.ascontiguousarray(a.reshape(-1, a.shape[-1]).T)

    flat = lambda name: np.ascontiguousarray(np.asarray(inputs[name]).reshape(-1))
    plain = lambda name: np.ascontiguousarray(inputs[name])
    arrays = {"consts": shape_constants()}
    for n in ("x", "Wq", "Wk", "Wv", "Wbeta", "b_beta", "Wout"):
        arrays["L0_attn_" + n] = plain("L0_attn_" + n)
    for n in ("Wr", "W1", "W2"):
        arrays["L0_ffn_" + n] = plain("L0_ffn_" + n)
    for n in ("q", "k", "v", "l"):
        arrays[f"L1_attn_{n}_w"] = rows(f"L1_attn_{n}_w")
        arrays[f"L1_attn_{n}_b"] = flat(f"L1_attn_{n}_b")
    for n in ("gate_w", "gate_b", "w1", "b1", "w2", "b2"):
        arrays["L1_ffn_" + n] = plain("L1_ffn_" + n)

    nc = bacc.Bacc("TRN2", target_bir_lowering=False, num_devices=1)
    args = [nc.dram_tensor(n, a.shape, mybir.dt.from_np(a.dtype), kind="ExternalInput").ap() for n, a in arrays.items()]
    out = nc.dram_tensor("out", (B, S, D), F32, kind="ExternalOutput").ap()
    seq_kernel(nc, *args, out)
    r = run_bass_kernel_spmd(nc, [arrays], core_ids=[0])
    return r.results[0]["out"]
```

```python
import numpy as np
from contextlib import ExitStack

import concourse.bass as bass
from concourse import mybir

F32 = mybir.dt.float32
F32R = mybir.dt.float32r
BF16 = mybir.dt.bfloat16
I32 = mybir.dt.int32
U32 = mybir.dt.uint32
ALU = mybir.AluOpType
ACT = mybir.ActivationFunctionType
AX = mybir.AxisListType

P = 128
B, S, D = 4, 1024, 256
H, DH = 16, 64
HP = H // 2
KD = D // P
C = 64
NCH = S // C
SUB = 16
LEVELS = 2
LN_EPS = 1e-5
NORM_EPS = 1e-12
SQ_EPS = NORM_EPS * NORM_EPS

C_ID = 0
C_ID2 = C_ID + P
C_LVL = C_ID2 + C
C_CAUSAL = C_LVL + LEVELS * C
C_OWN = C_CAUSAL + C
C_SEL = C_OWN + C
C_BLK = C_SEL + SUB
C_SAME = C_BLK + C // SUB
C_TRI = C_SAME + P
C_ONE = C_TRI + P
C_EXP = C_ONE + P
C_RANK = C_EXP + 8
C_ALL = C_RANK + 8


def shape_constants():
    c = np.zeros((P, C_ALL), np.float32)
    row = np.arange(P)[:, None]
    c[:, C_ID:C_ID + P] = row == np.arange(P)[None]
    s, t = row % C, np.arange(C)[None]
    c[:, C_ID2:C_ID2 + C] = s == t
    for l in range(LEVELS):
        size = SUB << l
        same = s // (2 * size) == t // (2 * size)
        c[:, C_LVL + l * C:C_LVL + (l + 1) * C] = same & (t // size % 2 == 1) & (s // size % 2 == 0)
    c[:, C_CAUSAL:C_CAUSAL + C] = -1.0 * (s <= t)
    c[:, C_OWN:C_OWN + C] = -1.0 * ((s // SUB == t // SUB) & (s < t))
    c[:, C_SEL:C_SEL + SUB] = row % SUB == np.arange(SUB)[None]
    c[:, C_BLK:C_BLK + C // SUB] = s // SUB == np.arange(C // SUB)[None]
    c[:, C_SAME:C_SAME + P] = row // SUB == np.arange(P)[None] // SUB
    c[:, C_TRI:C_TRI + P] = row <= np.arange(P)[None]
    c[:, C_ONE:C_ONE + P] = 1.0
    c[:, C_EXP:C_EXP + 8] = np.arange(8)[None]
    c[:, C_RANK:C_RANK + 8] = 8 - np.arange(8)[None]
    return c


def clear(nc, held):
    nc.clear_and_free_semaphores(held)
    nc.all_engine_barrier()


START = 2


def start_counts(nc, held):
    for s in held:
        nc.sync.sem_inc(s, START)
    nc.all_engine_barrier()


class Counts:

    def __init__(self, eng, name, n=3):
        self.eng, self.regs = eng, [eng.alloc_register(f"{name}_count{i}") for i in range(n)]

    def __call__(self, *values):
        for reg, value in zip(self.regs, values):
            self.eng.reg_mov(reg, value)
        return self.regs[:len(values)]


def delta_layer(nc, consts, x, Wq, Wk, Wv, Wbeta, b_beta, Wout, x1):
    held = []
    with ExitStack() as ctx:
        def sb(name, shape, dt=F32):
            return ctx.enter_context(nc.sbuf_tensor("dl_" + name, shape, dt))

        def sem(name):
            held.append(nc.alloc_semaphore(name="dl_" + name))
            return held[-1]

        low = ctx.enter_context(nc.psum_tensor("dl_low", [P, 4, 512], F32))
        bank = [low[:, i] for i in range(4)]
        bank += [ctx.enter_context(nc.psum_tensor(f"dl_bank{i}", [P, 512], F32))[:] for i in range(4, 8)]
        BSP, BX, BXT = (4, 5), (0, 1), (4, 5)
        BXN, BBETA, BK, BV, BQ = 7, 7, (6, 7), (2, 3), (6, 7)
        BR, BU, BO, BN, BY = (6, 7), (6, 7), 6, 7, 6

        cst = sb("cst", [P, C_TRI])
        wq, wk, wv = (sb(n, [P, KD, H * DH]) for n in ("wq", "wk", "wv"))
        wout = sb("wout", [P, HP, D])
        wbeta = sb("wbeta", [P, KD, H])
        bbeta = sb("bbeta", [P, HP])
        x_ln = sb("x_ln", [P, 2, D])
        x_res = sb("x_res", [P, 2, D])
        y = sb("y", [P, 2, D])
        bn = sb("bn", [P, 2, 6])
        mv = sb("mv", [P, 2, 2])
        std = sb("std", [P, 2])
        eps = sb("eps", [P, 1])
        rstd = sb("rstd", [P, 2])
        xn = sb("xn", [P, 2, D])
        xc = sb("xc", [P, 2, KD, P])
        z = sb("z", [P, B, HP])
        ez = sb("ez", [P, B, HP])
        ez1 = sb("ez1", [P, B, HP])
        beta = sb("beta", [P, B, HP])
        sq = sb("sq", [P, 2, HP, DH])
        ss = sb("ss", [P, B, HP])
        ssc = sb("ssc", [P, B, HP])
        kn = sb("kn", [P, B, HP])
        rkn = sb("rkn", [P, B, HP])
        K = sb("K", [P, B, HP, DH])
        V = sb("V", [P, B, HP, DH])
        KQ = sb("KQ", [P, B, HP, 2, C])
        PT = sb("PT", [P, B, HP, C])
        G = sb("G", [P, 2, HP, C])
        Gm = sb("Gm", [P, 2, HP, C])
        own = sb("own", [P, 2, HP, SUB])
        spread = sb("spread", [P, 2, HP, SUB, SUB])
        coef = sb("coef", [P, 2 * HP, SUB, SUB])
        part = sb("part", [P, SUB, 2 * HP, SUB])
        TS = sb("TS", [P, 2 * HP, SUB])
        BT = sb("BT", [P, 2, LEVELS, HP, C])
        T = sb("T", [P, 2, HP, C])
        TT = sb("TT", [P, B, HP, C])
        X = sb("X", [P, 2, HP, C])
        N = sb("N", [P, B, HP, DH])
        R = sb("R", [P, B, HP, DH])
        U = sb("U", [P, B, HP, DH])
        OT = sb("OT", [P, HP, B, C])

        weights, state0 = sem("weights"), sem("state0")
        x_in, r_in, stored = ([sem(f"{n}{u}") for u in range(2)] for n in ("x_in", "r_in", "stored"))
        stats, moments, std_ok, rstd_ok, xn_ok, xt_ps, xc_ok = map(
            sem, ("stats", "moments", "std_ok", "rstd_ok", "xn_ok", "xt_ps", "xc_ok"))
        beta_ps, z_ok, ez_ok, ez1_ok, beta_ok = map(sem, ("beta_ps", "z_ok", "ez_ok", "ez1_ok", "beta_ok"))
        k_ps, sq_ok, ss_ok, ssc_ok, kn_ok, rkn_ok, k_ok = map(
            sem, ("k_ps", "sq_ok", "ss_ok", "ssc_ok", "kn_ok", "rkn_ok", "k_ok"))
        v_ps, v_ok, q_ps, q_ok, kt_ok = map(sem, ("v_ps", "v_ok", "q_ps", "q_ok", "kt_ok"))
        g_ps, g_ok, p_ok, bt_ok = map(sem, ("g_ps", "g_ok", "p_ok", "bt_ok"))
        gm_ok, own_ok, spread_ok, coef_ps, coef_ok, column, ts_ok, tn_ok = map(
            sem, ("gm_ok", "own_ok", "spread_ok", "coef_ps", "coef_ok", "column", "ts_ok", "tn_ok"))
        x_ps, xx_ok, t_ok, xt2_ps, tt_ok = map(sem, ("x_ps", "xx_ok", "t_ok", "xt2_ps", "tt_ok"))
        r_ps, r_ok, u_ps, u_ok, o_ps, o_ok, n_ps, n_ok = map(
            sem, ("r_ps", "r_ok", "u_ps", "u_ok", "o_ps", "o_ok", "n_ps", "n_ok"))
        y_ps, y_ok = sem("y_ps"), sem("y_ok")
        start_counts(nc, held)

        ident = cst[:, C_ID:C_ID + P]
        ident2 = cst[:, C_ID2:C_ID2 + C]
        N_WEIGHTS = 8
        ALL_WEIGHTS = 16 * N_WEIGHTS + START

        COLUMNS = 2 * (SUB - 1)
        CB = HP * SUB * SUB // 512

        def x_count(f, l, j):
            return f * (2 * LEVELS) + (2 * l + j + 1)

        def over_pairs(m):
            return m.unsqueeze(1).broadcast_to([P, HP, C])

        def over_cols(v):
            return v.unsqueeze(2).broadcast_to([P, HP, C])

        def keys_by(j):
            return low[:, 2 * j:2 * j + 2].rearrange("p q (a o c) -> p (q a) o c", o=2, c=C)

        def grid(b):
            return bank[b][:].rearrange("p (a c) -> p a c", a=HP)

        SLOTS = 8 + 2 * LEVELS

        def whole(part):
            def run(c, u):
                for s in range(SLOTS):
                    part(c, u, s)
            return run

        def first(c, u):
            return isinstance(c, int) and (c, u) == (0, 0)

        def last(c, u):
            return isinstance(c, int) and (c, u) == (NCH - 1, 1)

        def steps(eng, front, pair_block, state):
            front(0, 0)
            pair_block(0, 0, state=False)
            with eng.Fori(0, NCH - 1) as c:
                pair_block(c, 1)
                pair_block(c + 1, 0)
            pair_block(NCH - 1, 1, front=False)
            state(NCH - 1, 1)

        block = ctx.enter_context(nc.Block())

        @block.sync
        def _(sp):
            def load(dst, c, u, done):
                for h in range(2):
                    sp.dma_start(dst[C * h:C * h + C, u], x[2 * u + h, bass.ts(c, C), :]).then_inc(done[u], 16)

            load(x_ln, 0, 0, x_in)
            load(x_ln, 0, 1, x_in)
            sp.dma_start(cst[:], consts[:, 0:C_TRI]).then_inc(weights, 16)
            sp.dma_start(wk[:], Wk.rearrange("(k p) n -> p k n", p=P)).then_inc(weights, 16)
            sp.dma_start(wbeta[:], Wbeta.rearrange("(k p) n -> p k n", p=P)).then_inc(weights, 16)
            for h in range(2):
                sp.dma_start(bbeta[C * h:C * h + C, :], b_beta.rearrange("(a h) -> h a", h=2)[h:h + 1, :]
                             .broadcast_to([C, HP]), allow_slow_non_contiguous=True).then_inc(weights, 16)
            sp.dma_start(wv[:], Wv.rearrange("(k p) n -> p k n", p=P)).then_inc(weights, 16)
            sp.dma_start(wq[:], Wq.rearrange("(k p) n -> p k n", p=P)).then_inc(weights, 16)
            sp.dma_start(wout[:], Wout.rearrange("(a p) n -> p a n", p=P)).then_inc(weights, 16)

            def store(c, u):
                sp.wait_ge(y_ok, c * 2 + (u + 1 + START))
                for h in range(2):
                    sp.dma_start(x1[2 * u + h, bass.ts(c, C), :], y[C * h:C * h + C, u]).then_inc(stored[u], 16)

            load(x_res, 0, 0, r_in)
            load(x_res, 0, 1, r_in)
            with sp.Fori(0, NCH - 1) as c:
                for u in range(2):
                    sp.wait_ge(xn_ok, c * 2 + (u + 1 + START))
                    load(x_ln, c + 1, u, x_in)
                    store(c, u)
                    load(x_res, c + 1, u, r_in)
            for u in range(2):
                store(NCH - 1, u)
                sp.wait_ge(stored[u], NCH * 32 + START)

        @block.gpsimd
        def _(pool):
            pool.wait_ge(weights, ALL_WEIGHTS)
            with pool.Fori(0, 2 * NCH) as f:
                for j in range(2):
                    pool.wait_ge(own_ok, f * 2 + (j + 1 + START))
                    pool.wait_ge(coef_ps, f * (2 * CB) + START)
                    pool.tensor_tensor(spread[:, j].rearrange("p a t s -> p (a t) s"),
                                       own[:, j].rearrange("p a t -> p (a t)").unsqueeze(2)
                                       .broadcast_to([P, HP * SUB, SUB]),
                                       cst[:, C_SEL:C_SEL + SUB].unsqueeze(1).broadcast_to([P, HP * SUB, SUB]),
                                       ALU.mult).then_inc(spread_ok, 1)
                pool.wait_ge(x_ps, f * (2 * LEVELS) + START)
                for l in range(LEVELS):
                    m = cst[:, C_LVL + l * C:C_LVL + (l + 1) * C]
                    for j in range(2):
                        pool.tensor_tensor(BT[:, j, l], G[:, j], over_pairs(m), ALU.mult).then_inc(bt_ok, 1)

        @block.scalar
        def _(act):
            def ln_std(c, u):
                act.wait_ge(moments, c * 2 + (u + 1 + START))
                act.activation(std[:, u:u + 1], mv[:, u, 1:2], ACT.Sqrt, bias=eps[:, 0:1]).then_inc(std_ok, 1)

            def keep_xc(c, u):
                act.wait_ge(xt_ps, c * 2 + (u + 1 + START))
                act.activation(xc[:, u].rearrange("p k t -> p (k t)"), bank[BXN][:, 0:KD * P], ACT.Copy
                               ).then_inc(xc_ok, 1)

            def exp_z(c, u):
                act.wait_ge(z_ok, c * 2 + (u + 1 + START))
                act.activation(ez[:, 2 * u:2 * u + 2], z[:, 2 * u:2 * u + 2], ACT.Exp, scale=-1.0).then_inc(ez_ok, 1)

            def square_k(c, u, j):
                b = 2 * u + j
                act.wait_ge(k_ps, c * 4 + (b + 1 + START))
                act.wait_ge(ss_ok, c * 4 + (2 * u + START))
                act.activation(sq[:, j], grid(BK[j]), ACT.Square).then_inc(sq_ok, 1)

            def sqrt_k(c, u):
                act.wait_ge(ssc_ok, c * 2 + (u + 1 + START))
                act.activation(kn[:, 2 * u:2 * u + 2], ssc[:, 2 * u:2 * u + 2], ACT.Sqrt).then_inc(kn_ok, 1)

            def keep_v(c, u, j):
                act.wait_ge(v_ps, c * 4 + (2 * u + j + 1 + START))
                act.activation(V[:, 2 * u + j], grid(BV[j]), ACT.Copy).then_inc(v_ok, 1)

            def keep_q(c, u, q):
                act.wait_ge(q_ps, c * 4 + (2 * u + q + 1 + START))
                act.activation(KQ[:, 2 * u:2 * u + 2, 4 * q:4 * q + 4, 1].rearrange("p b a t -> p a b t"),
                               bank[BQ[q]][:].rearrange("p (a b t) -> p a b t", a=4, b=2), ACT.Copy, scale=-1.0
                               ).then_inc(q_ok, 1)

            def keep_o(c, u, j):
                act.wait_ge(o_ps, c * 4 + (2 * u + j + 1 + START))
                act.activation(OT[:, :, 2 * u + j], grid(BO), ACT.Copy).then_inc(o_ok, 1)

            def pair_block(c, u, state=True, front=True):
                f = c * 2 + u
                before, after = ((c - 1, 1), (c, 1)) if u == 0 else ((c, 0), (c + 1, 0))

                def slot(s):
                    if state:
                        state_part(*before, s)
                    if front:
                        front_part(*after, s)

                slot(0)
                slot(1)
                for j in range(2):
                    for i in range(CB):
                        act.wait_ge(coef_ps, f * (2 * CB) + (CB * j + i + 1 + START))
                        act.wait_ge(ts_ok, f + START)
                        act.activation(coef[:, HP * j + 2 * i:HP * j + 2 * i + 2].rearrange("p a t s -> p (a t s)"),
                                       bank[BSP[i % 2]][:], ACT.Copy).then_inc(coef_ok, 1)
                slot(2)
                keep_v(c, u, 0)
                slot(3)
                keep_v(c, u, 1)
                slot(4)
                for s in range(5, 8):
                    slot(s)
                for l in range(LEVELS):
                    for j in range(2):
                        act.wait_ge(x_ps, x_count(f, l, j) + START)
                        act.activation(X[:, j], grid(BX[j]), ACT.Copy).then_inc(xx_ok, 1)
                    slot(2 * l + 8)
                    slot(2 * l + 9)

            def state_part(c, u, s):
                if s == 2:
                    keep_o(c, u, 0)
                if s == 3:
                    keep_o(c, u, 1)

            def front_part(c, u, s):
                if s == 1:
                    ln_std(c, u)
                if s == 4:
                    keep_xc(c, u)
                if s == 5:
                    square_k(c, u, 0)
                if s == 6:
                    square_k(c, u, 1)
                if s == 7:
                    sqrt_k(c, u)
                if s == 9:
                    keep_q(c, u, 0)
                    exp_z(c, u)
                if s == 10:
                    keep_q(c, u, 1)

            act.wait_ge(state0, 2 + SUB + START)
            steps(act, whole(front_part), pair_block, whole(state_part))

        @block.vector
        def _(dve):
            counts = Counts(dve, "dl")

            def ln_stats(c, u):
                dve.wait_ge(x_in[u], c * 32 + (32 + START))
                dve.bn_stats(bn[:, u], x_ln[:, u]).then_inc(stats, 1)
                at = counts(c * 2 + (u + 1 + START))
                dve.wait_ge(weights, ALL_WEIGHTS)
                dve.wait_ge(stats, at[0])
                dve.bn_aggr(mv[:, u], bn[:, u]).then_inc(moments, 1)

            def ln_apply(c, u):
                dve.wait_ge(std_ok, c * 2 + (u + 1 + START))
                dve.reciprocal(rstd[:, u:u + 1], std[:, u:u + 1]).then_inc(rstd_ok, 1)
                dve.wait_ge(rstd_ok, c * 2 + (u + 1 + START))
                dve.tensor_scalar(xn[:, u], x_ln[:, u], mv[:, u, 0:1], rstd[:, u:u + 1],
                                  ALU.subtract, ALU.mult).then_inc(xn_ok, 1)

            def rates_z(c, u):
                dve.wait_ge(beta_ps, c * 2 + (u + 1 + START))
                dve.tensor_tensor(z[:, 2 * u:2 * u + 2],
                                  bank[BBETA][:, 0:2 * HP].rearrange("p (j a) -> p j a", j=2),
                                  bbeta[:].unsqueeze(1).broadcast_to([P, 2, HP]), ALU.add).then_inc(z_ok, 1)

            def rates(c, u):
                lanes = slice(2 * u, 2 * u + 2)
                dve.wait_ge(ez_ok, c * 2 + (u + 1 + START))
                dve.tensor_scalar(ez1[:, lanes], ez[:, lanes], 1.0, None, ALU.add).then_inc(ez1_ok, 1)
                dve.wait_ge(ez1_ok, c * 2 + (u + 1 + START))
                dve.reciprocal(beta[:, lanes], ez1[:, lanes]).then_inc(beta_ok, 1)

            def sum_squares(c, u, j):
                dve.wait_ge(sq_ok, c * 4 + (2 * u + j + 1 + START))
                dve.tensor_reduce(ss[:, 2 * u + j], sq[:, j], AX.X, ALU.add).then_inc(ss_ok, 1)

            def floor_squares(c, u):
                lanes = slice(2 * u, 2 * u + 2)
                dve.wait_ge(ss_ok, c * 4 + (2 * u + 2 + START))
                dve.tensor_scalar(ssc[:, lanes], ss[:, lanes], SQ_EPS, None, ALU.max).then_inc(ssc_ok, 1)

            def keys(c, u):
                lanes = slice(2 * u, 2 * u + 2)
                dve.wait_ge(kn_ok, c * 2 + (u + 1 + START))
                dve.reciprocal(rkn[:, lanes], kn[:, lanes]).then_inc(rkn_ok, 1)
                dve.wait_ge(rkn_ok, c * 2 + (u + 1 + START))
                for j in range(2):
                    b = 2 * u + j
                    dve.tensor_tensor(K[:, b], grid(BK[j]), over_cols(rkn[:, b]), ALU.mult).then_inc(k_ok, 1)

            def turn_keys(c, u, j):
                b = 2 * u + j
                dve.wait_ge(k_ok, c * 4 + (b + 1 + START))
                for h in range(2):
                    for r in range(2):
                        for k in range(2):
                            done = dve.transpose(KQ[C * h + 32 * k:C * h + 32 * k + 32, b, :, 0, 32 * r:32 * r + 32],
                                                 K[C * h + 32 * r:C * h + 32 * r + 32, b, :, 32 * k:32 * k + 32])
                done.then_inc(kt_ok, 1)

            def turn_blocks(u, j):
                return dve.transpose(T[:, j].rearrange("p a s -> p (a s)"),
                                     TT[:, 2 * u + j].rearrange("p a s -> p (a s)"))

            def inverse(c, u, slot):
                f = c * 2 + u
                lanes = slice(2 * u, 2 * u + 2)
                dve.wait_ge(beta_ok, f + (1 + START))
                for j in range(2):
                    dve.wait_ge(g_ps, f * 2 + (j + 1 + START))
                    dve.wait_ge(bt_ok, f * (2 * LEVELS) + START)
                    dve.tensor_tensor(G[:, j], keys_by(j)[:, :, 0], over_cols(beta[:, 2 * u + j]), ALU.mult).then_inc(g_ok, 1)
                for j in range(2):
                    dve.wait_ge(g_ok, f * 2 + (j + 1 + START))
                    dve.tensor_tensor(Gm[:, j], G[:, j], over_pairs(cst[:, C_OWN:C_OWN + C]), ALU.mult
                                      ).then_inc(gm_ok, 1)
                for j in range(2):
                    dve.wait_ge(gm_ok, f * 2 + (j + 1 + START))
                    dve.wait_ge(spread_ok, f * 2 + START)
                    dve.tensor_reduce(own[:, j], Gm[:, j].rearrange("p a (q t) -> p a t q", t=SUB), AX.X, ALU.add
                                      ).then_inc(own_ok, 1)
                slot(0)
                for j in range(2):
                    dve.tensor_tensor(PT[:, 2 * u + j], keys_by(j)[:, :, 1], over_pairs(cst[:, C_CAUSAL:C_CAUSAL + C]),
                                      ALU.mult).then_inc(p_ok, 1)
                slot(1)
                dve.wait_ge(coef_ok, f * (2 * CB) + (2 * CB + START))
                for t in range(1, SUB):
                    if t > 1:
                        dve.wait_ge(column, f * COLUMNS + (2 * t - 2 + START))
                    dve.tensor_tensor(part[:, t, :, 0:t], TS[:, :, 0:t], coef[:, :, t, 0:t], ALU.mult
                                      ).then_inc(column, 1)
                    dve.wait_ge(column, f * COLUMNS + (2 * t - 1 + START))
                    dve.tensor_reduce(TS[:, :, t], part[:, t, :, 0:t + 1], AX.X, ALU.add).then_inc(column, 1)
                    if t == 10:
                        slot(2)
                dve.wait_ge(column, f * COLUMNS + (COLUMNS + START))
                dve.tensor_tensor(TT[:, lanes].rearrange("p j a (q t) -> p (j a) q t", t=SUB),
                                  TS[:].unsqueeze(2).broadcast_to([P, 2 * HP, C // SUB, SUB]),
                                  cst[:, C_BLK:C_BLK + C // SUB].unsqueeze(1).unsqueeze(3)
                                  .broadcast_to([P, 2 * HP, C // SUB, SUB]), ALU.mult).then_inc(ts_ok, 1)
                dve.wait_ge(ts_ok, f + (1 + START))
                for j in range(2):
                    turn_blocks(u, j).then_inc(tn_ok, 1)
                for s in range(3, 8):
                    slot(s)
                for l in range(LEVELS):
                    slot(2 * l + 8)
                    for j in range(2):
                        b = 2 * u + j
                        dve.wait_ge(xt2_ps, x_count(f, l, j) + START)
                        dve.wait_ge(*((ts_ok, f + (1 + START)) if l == 0 else (tt_ok, x_count(f, l - 1, j) + START)))
                        dve.tensor_tensor(TT[:, b], TT[:, b], grid(BXT[j]), ALU.subtract).then_inc(tt_ok, 1)
                        if l == 0:
                            dve.wait_ge(tt_ok, x_count(f, l, j) + START)
                            turn_blocks(u, j).then_inc(t_ok, 1)
                    slot(2 * l + 9)

            def add_v(c, u, j):
                b = 2 * u + j
                dve.wait_ge(r_ps, c * 4 + (b + 1 + START))
                dve.tensor_tensor(R[:, b], grid(BR[j]), V[:, b], ALU.add).then_inc(r_ok, 1)

            def scale_u(c, u, j):
                b = 2 * u + j
                dve.wait_ge(u_ps, c * 4 + (b + 1 + START))
                dve.tensor_tensor(U[:, b], grid(BU[j]), over_cols(beta[:, b]), ALU.mult).then_inc(u_ok, 1)

            def new_state(c, u, j):
                b = 2 * u + j
                dve.wait_ge(n_ps, c * 4 + (b + 1 + START))
                dve.tensor_tensor(N[:, b], N[:, b], grid(BN), ALU.subtract).then_inc(n_ok, 1)

            def residual(c, u):
                dve.wait_ge(y_ps, c * 2 + (u + 1 + START))
                dve.wait_ge(r_in[u], c * 32 + (32 + START))
                dve.wait_ge(stored[u], c * 32 + START)
                dve.tensor_tensor(y[:, u], bank[BY][:, 0:D], x_res[:, u], ALU.add).then_inc(y_ok, 1)

            def state_part(c, u, s):
                if s == 0:
                    add_v(c, u, 0)
                    add_v(c, u, 1)
                if s == 1:
                    scale_u(c, u, 0)
                    scale_u(c, u, 1)
                if s == 2:
                    new_state(c, u, 0)
                if s == 3:
                    new_state(c, u, 1)
                if s == 4:
                    residual(c, u)

            def front_part(c, u, s):
                if s == 0:
                    ln_stats(c, u)
                if s == 2:
                    ln_apply(c, u)
                if s == 5:
                    rates_z(c, u)
                    sum_squares(c, u, 0)
                if s == 6:
                    sum_squares(c, u, 1)
                    floor_squares(c, u)
                if s == 7:
                    keys(c, u)
                if s == 9:
                    turn_keys(c, u, 0)
                    turn_keys(c, u, 1)
                if s == 10:
                    rates(c, u)

            def pair_block(c, u, state=True, front=True):
                before, after = ((c - 1, 1), (c, 1)) if u == 0 else ((c, 0), (c + 1, 0))

                def slot(s):
                    if state:
                        state_part(*before, s)
                    if front:
                        front_part(*after, s)

                inverse(c, u, slot)

            dve.memset(N[:], 0.0).then_inc(state0, 1)
            dve.memset(eps[:], LN_EPS).then_inc(state0, 1)
            dve.wait_ge(weights, ALL_WEIGHTS)
            sel = cst[:, C_SEL:C_SEL + SUB]
            for t in range(1, SUB):
                dve.tensor_copy(part[:, t, :, t], sel[:, t:t + 1].broadcast_to([P, 2 * HP])).then_inc(state0, 1)
            dve.tensor_copy(TS[:, :, 0], sel[:, 0:1].broadcast_to([P, 2 * HP])).then_inc(state0, 1)
            dve.wait_ge(state0, 2 + SUB + START)
            steps(dve, whole(front_part), pair_block, whole(state_part))

        @block.tensor
        def _(pe):
            counts = Counts(pe, "dl")

            def pairs(out, lhsT, rhs):
                for a in range(HP):
                    for h in range(2):
                        rows = slice(C * h, C * h + C)
                        last = pe.matmul(out[rows, a], lhsT(rows, a), rhs(rows, a), start=True, stop=True)
                return last

            def natural(out, w, u, j):
                wh = w[:].rearrange("p k (a h d) -> p k h a d", h=2, d=DH)
                for k in range(KD):
                    for h in range(2):
                        last = pe.matmul(out[C * h:C * h + C], xc[:, u, k, C * j:C * j + C], wh[:, k, h],
                                         start=(k == 0), stop=(k == KD - 1))
                return last

            def turn_x(c, u):
                at = counts(c * 2 + (u + 1 + START), c * 4 + (2 * u - 2 + START))
                pe.wait_ge(weights, ALL_WEIGHTS)
                pe.wait_ge(xn_ok, at[0])
                if not first(c, u):
                    pe.wait_ge(n_ok, at[1])
                for k in range(KD):
                    last = pe.transpose(bank[BXN][:, k * P:(k + 1) * P], xn[:, u, k * P:(k + 1) * P], ident)
                last.then_inc(xt_ps, 1)

            def rates(c, u):
                pe.wait_ge(xc_ok, c * 2 + (u + 1 + START))
                wbh = wbeta[:].rearrange("p k (a h) -> p k h a", h=2)
                for j in range(2):
                    for h in range(2):
                        for k in range(KD):
                            last = pe.matmul(bank[BBETA][C * h:C * h + C, j * HP:(j + 1) * HP],
                                             xc[:, u, k, C * j:C * j + C], wbh[:, k, h],
                                             start=(k == 0), stop=(k == KD - 1))
                last.then_inc(beta_ps, 1)

            def keys(c, u, j):
                pe.wait_ge(xc_ok, c * 2 + (u + 1 + START))
                if j == 1:
                    pe.wait_ge(z_ok, c * 2 + (u + 1 + START))
                elif not first(c, u):
                    pe.wait_ge(y_ok, c * 2 + (u - 1 + START))
                natural(grid(BK[j]), wk, u, j).then_inc(k_ps, 1)

            def values(c, u, j):
                if j == 0:
                    pe.wait_ge(p_ok, c * 4 + (2 * u + 2 + START))
                natural(grid(BV[j]), wv, u, j).then_inc(v_ps, 1)

            def queries(c, u, q, part):
                pe.wait_ge(k_ok, c * 4 + (2 * u + q + 1 + START))
                for a in range(2 * part, 2 * part + 2):
                    for k in range(KD):
                        m = (4 * q + a) * P
                        last = pe.matmul(bank[BQ[q]][:, a * P:(a + 1) * P], wq[:, k, m:m + P], xc[:, u, k],
                                         start=(k == 0), stop=(k == KD - 1))
                if part == 1:
                    last.then_inc(q_ps, 1)

            def inverse(c, u, slot):
                f = c * 2 + u
                for j in range(2):
                    b = 2 * u + j
                    at = counts(c * 4 + (b + 1 + START), c * 4 + (2 * u + 2 + START), c * 4 + (2 * u + START))
                    pe.wait_ge(weights, ALL_WEIGHTS)
                    pe.wait_ge(kt_ok, at[0])
                    pe.wait_ge(q_ok, at[1])
                    pe.wait_ge(v_ok, at[2])
                    pairs(keys_by(j), lambda r, a: KQ[r, b, a, 0], lambda r, a: KQ[r, b, a]).then_inc(g_ps, 1)
                slot(0)
                slot(1)
                for j in range(2):
                    for i in range(CB):
                        n = CB * j + i
                        at = counts(f * 2 + (j + 1 + START), f * (2 * CB) + (n - 1 + START))
                        pe.wait_ge(weights, ALL_WEIGHTS)
                        pe.wait_ge(spread_ok, at[0])
                        if n >= 2:
                            pe.wait_ge(coef_ok, at[1])
                        pe.matmul(bank[BSP[i % 2]][:], cst[:, C_SAME:C_SAME + P],
                                  spread[:, j, 2 * i:2 * i + 2].rearrange("p a t s -> p (a t s)"),
                                  start=True, stop=True).then_inc(coef_ps, 1)
                slot(2)
                values(c, u, 0)
                slot(3)
                values(c, u, 1)
                slot(4)
                for s in range(5, 8):
                    slot(s)
                for l in range(LEVELS):
                    for j in range(2):
                        at = counts(x_count(f, l, j) + START, f * 2 + (j + 1 + START),
                                    x_count(f, max(l - 1, 0), j) + START)
                        pe.wait_ge(weights, ALL_WEIGHTS)
                        pe.wait_ge(bt_ok, at[0])
                        pe.wait_ge(t_ok if l else tn_ok, at[1])
                        if l:
                            pe.wait_ge(xx_ok, at[2])
                        pairs(grid(BX[j]), lambda r, a: BT[r, j, l, a], lambda r, a: T[r, j, a]).then_inc(x_ps, 1)
                    slot(2 * l + 8)
                    for j in range(2):
                        b = 2 * u + j
                        at = counts(x_count(f, l, j) + START, x_count(f, max(l - 1, 0), j) + START)
                        pe.wait_ge(weights, ALL_WEIGHTS)
                        pe.wait_ge(xx_ok, at[0])
                        if l:
                            pe.wait_ge(tt_ok, at[1])
                        pairs(grid(BXT[j]), lambda r, a: X[r, j, a], lambda r, a: TT[r, b, a]).then_inc(xt2_ps, 1)
                    slot(2 * l + 9)

            def recall(c, u, j):
                b = 2 * u + j
                at = counts(c * 4 + (2 * u + START), c * 4 + (b + 1 + START))
                pe.wait_ge(weights, ALL_WEIGHTS)
                pe.wait_ge(n_ok, at[0])
                pe.wait_ge(v_ok, at[1])
                pairs(grid(BR[j]), lambda r, a: KQ[r, b, a, 0], lambda r, a: N[r, b, a]).then_inc(r_ps, 1)

            def solve(c, u, j):
                b = 2 * u + j
                at = counts(c * 4 + (b + 1 + START), x_count(c * 2 + u, LEVELS - 1, j) + START)
                pe.wait_ge(weights, ALL_WEIGHTS)
                pe.wait_ge(r_ok, at[0])
                pe.wait_ge(tt_ok, at[1])
                pairs(grid(BU[j]), lambda r, a: TT[r, b, a], lambda r, a: R[r, b, a]).then_inc(u_ps, 1)

            def answer(c, u, j):
                b = 2 * u + j
                at = counts(c * 4 + (b + 1 + START), c * 4 + (b + START))
                pe.wait_ge(weights, ALL_WEIGHTS)
                pe.wait_ge(u_ok, at[0])
                pe.wait_ge(o_ok, at[1])
                for a in range(HP):
                    for h in range(2):
                        r = slice(C * h, C * h + C)
                        pe.matmul(grid(BO)[r, a], N[r, b, a], KQ[r, b, a, 1], start=True, stop=False)
                        last = pe.matmul(grid(BO)[r, a], U[r, b, a], PT[r, b, a], start=False, stop=True)
                last.then_inc(o_ps, 1)
                at = counts(c * 4 + (b + START), c * 4 + (2 * u + 2 + START))
                pe.wait_ge(weights, ALL_WEIGHTS)
                pe.wait_ge(n_ok, at[0])
                pe.wait_ge(u_ok, at[1])
                pairs(grid(BN), lambda r, a: K[r, b, a], lambda r, a: U[r, b, a]).then_inc(n_ps, 1)

            def project(c, u):
                pe.wait_ge(o_ok, c * 4 + (2 * u + 2 + START))
                for a in range(HP):
                    last = pe.matmul(bank[BY][:, 0:D], OT[:, a, 2 * u:2 * u + 2].rearrange("p b t -> p (b t)"),
                                     wout[:, a], start=(a == 0), stop=(a == HP - 1))
                last.then_inc(y_ps, 1)

            def state_part(c, u, s):
                if s == 0:
                    recall(c, u, 0)
                    recall(c, u, 1)
                if s == 1:
                    solve(c, u, 0)
                    solve(c, u, 1)
                if s == 2:
                    answer(c, u, 0)
                if s == 3:
                    answer(c, u, 1)
                if s == 4:
                    project(c, u)

            def front_part(c, u, s):
                if s == 4:
                    turn_x(c, u)
                if s == 5:
                    rates(c, u)
                    keys(c, u, 0)
                if s == 6:
                    keys(c, u, 1)
                if s == 8:
                    queries(c, u, 0, 0)
                if s == 9:
                    queries(c, u, 0, 1)
                    queries(c, u, 1, 0)
                if s == 10:
                    queries(c, u, 1, 1)

            def pair_block(c, u, state=True, front=True):
                before, after = ((c - 1, 1), (c, 1)) if u == 0 else ((c, 0), (c + 1, 0))

                def slot(s):
                    if state:
                        state_part(*before, s)
                    if front:
                        front_part(*after, s)

                inverse(c, u, slot)

            pe.wait_ge(weights, ALL_WEIGHTS)
            pe.wait_ge(state0, 2 + SUB + START)
            steps(pe, whole(front_part), pair_block, whole(state_part))
    clear(nc, held)


E_N = 8
F = 1024
NT = B * S // P
GT = 4


def expert_layer(nc, name, consts, x, Wr, br, W1, b1, W2, b2, cap, keeps_dropped, out, slots, answers):
    nrow = cap // P if cap % P == 0 else 2
    rp = cap // nrow
    nhalf = 2 if cap > 512 else 1
    half = cap // nhalf
    FT = F // P
    biased = b1 is not None
    last_slot = E_N * cap - 1

    held = []
    with ExitStack() as ctx:
        def sb(n, shape, dt=F32):
            return ctx.enter_context(nc.sbuf_tensor(f"{name}_{n}", shape, dt))

        def sem(n):
            held.append(nc.alloc_semaphore(name=f"{name}_{n}"))
            return held[-1]

        bank = [ctx.enter_context(nc.psum_tensor(f"{name}_bank{i}", [P, 512], F32)) for i in range(8)]

        cst = sb("cst", [P, C_ALL])
        wr = sb("wr", [P, KD, E_N])
        bias_r = sb("bias_r", [P, E_N])
        x_all = sb("x_all", [P, NT, D])
        xn_all = sb("xn_all", [P, NT, D])
        xn = sb("xn", [P, 2, GT, D])
        bn = sb("bn", [P, 2, GT, 6])
        mv = sb("mv", [P, 2, GT, 2])
        eps = sb("eps", [P, 1])
        std = sb("std", [P, 2, GT])
        rstd = sb("rstd", [P, 2, GT])
        xT = sb("xT", [P, 2, GT, KD, P])
        logit = sb("logit", [P, NT, E_N])
        route = [sb(f"route{i}", [P, NT, E_N]) for i in range(3)]
        per_token = [sb(f"token{i}", [P, NT]) for i in range(12)]
        reset = sb("reset", [P, E_N, NT])
        total = sb("total", [P, E_N, NT])
        running = sb("running", [P, E_N, NT])
        slot_in = sb("slot_in", [P, NT], I32)
        slot_out = sb("slot_out", [P, NT], I32)
        zero = sb("zero", [P, 4 * D])
        w1 = sb("w1", [P, 2, KD, F])
        w2 = sb("w2", [P, 2, FT, D])
        rows = sb("rows", [rp, 2, nrow, D])
        rowsT = sb("rowsT", [P, KD, cap])
        hid = sb("hid", [P, FT, cap])
        ans = sb("ans", [rp, nrow, D])
        if biased:
            b1_sb = sb("b1", [P, E_N, FT])
            b2_sb = sb("b2", [1, E_N, D])
        got = sb("got", [P, NT, D])

        const_in, zeroed, zero_ok, eps_ok = map(sem, ("const_in", "zeroed", "zero_ok", "eps_ok"))
        x_in, w_in, rows_in = ([sem(f"{n}{u}") for u in range(2)] for n in ("x_in", "w_in", "rows_in"))
        stats, moments, std_ok, rstd_ok, xn_ok, xn_kept, xT_ps, xT_ok, lg_ps, lg_ok = map(
            sem, ("stats", "moments", "std_ok", "rstd_ok", "xn_ok", "xn_kept", "xT_ps", "xT_ok", "lg_ps", "lg_ok"))
        chain, ex_ok, once_ok, count_ps, slot_ok = map(sem, ("chain", "ex_ok", "once_ok", "count_ps", "slot_ok"))
        rT_ps, rT_ok, h_ps, h_act, h_dve, a_ps, a_ok, a_out = map(
            sem, ("rT_ps", "rT_ok", "h_ps", "h_act", "h_dve", "a_ps", "a_ok", "a_out"))
        mixed, out_ok, stored = map(sem, ("mixed", "out_ok", "stored"))
        start_counts(nc, held)
        sent = sem("sent")
        fetched = [sem(f"fetched{g}") for g in range(NT // GT)]

        ident = cst[:, C_ID:C_ID + P]
        ALL_CONST = 16 * (2 + (3 if biased else 0)) + START
        G = NT // GT
        x_t = x.rearrange("b s d -> (b s) d").rearrange("(n p) d -> p n d", p=P)
        out_t = out.rearrange("b s d -> (b s) d").rearrange("(n p) d -> p n d", p=P)
        slots_t = slots.rearrange("(e j p) d -> e p j d", j=nrow, p=rp)
        answers_t = answers.rearrange("(e j p) d -> e p j d", j=nrow, p=rp)
        blocks = [(f, q) for f in range(FT) for q in range(nhalf)]
        NB = len(blocks)
        on_act = NB if biased else NB // 2

        def over_experts_in_order(eng, expert):
            with eng.Fori(0, E_N // 2 - 1) as i:
                for u in range(2):
                    expert(i * 2 + u, u, False)
            expert(E_N - 2, 0, False)
            expert(E_N - 1, 1, True)

        def over_groups(eng, group):
            with eng.Fori(0, G // 2 - 1) as i:
                for u in range(2):
                    group(i * 2 + u, u, i, False)
            group(G - 2, 0, G // 2 - 1, False)
            group(G - 1, 1, G // 2 - 1, True)

        def over_experts(v):
            return v.unsqueeze(2).broadcast_to([P, NT, E_N])

        block = ctx.enter_context(nc.Block())

        @block.sync
        def _(sp):
            sp.dma_start(cst[:], consts).then_inc(const_in, 16)
            sp.dma_start(wr[:], Wr.rearrange("(k p) n -> p k n", p=P)).then_inc(const_in, 16)
            if biased:
                sp.dma_start(bias_r[:], br.unsqueeze(0).broadcast_to([P, E_N])).then_inc(const_in, 16)
                sp.dma_start(b2_sb[:], b2.unsqueeze(0)).then_inc(const_in, 16)
                sp.dma_start(b1_sb[:], b1.rearrange("e (f p) -> p e f", p=P),
                             allow_slow_non_contiguous=True).then_inc(const_in, 16)
            with sp.Fori(0, G // 2) as i:
                for u in range(2):
                    sp.wait_ge(x_in[u], i * 16 + START)
                    sp.dma_start(x_all[:, bass.ts(i * 2 + u, GT)], x_t[:, bass.ts(i * 2 + u, GT)]).then_inc(x_in[u], 16)
            sp.wait_ge(zero_ok, 1 + START)
            zrow = slots.rearrange("(p r) d -> p (r d)", p=P)
            step = 4 * D if zrow.shape[1] % (4 * D) == 0 else 2 * D
            for i in range(zrow.shape[1] // step):
                sp.dma_start(zrow[:, i * step:(i + 1) * step], zero[:, 0:step]).then_inc(zeroed, 16)
            sp.wait_ge(sent, 16 * NT)

            def rows_of(e, u):
                sp.dma_start(rows[:, u], slots_t[e]).then_inc(rows_in[u], 16)

            def answer_of(e):
                sp.wait_ge(a_ok, (e + 1) * nrow + START)
                sp.dma_start(answers_t[e], ans[:]).then_inc(a_out, 16)

            rows_of(0, 0)
            rows_of(1, 1)
            with sp.Fori(0, E_N // 2 - 1) as i:
                for u in range(2):
                    sp.wait_ge(rT_ps, (i * 2 + u + 1) * nrow + START)
                    rows_of(i * 2 + u + 2, u)
                    answer_of(i * 2 + u)
            answer_of(E_N - 2)
            answer_of(E_N - 1)
            for g in range(NT // GT):
                sp.wait_ge(out_ok, GT * (g + 1) + START)
                sp.dma_start(out_t[:, g * GT:(g + 1) * GT], got[:, g * GT:(g + 1) * GT]).then_inc(stored, 16)
            sp.wait_ge(stored, 16 * G + START)

        @block.gpsimd
        def _(pool):
            pool.memset(zero[:], 0.0).then_inc(zero_ok, 1)
            n_zero = slots.shape[0] // P * D // (4 * D if slots.shape[0] // P * D % (4 * D) == 0 else 2 * D)
            pool.wait_ge(slot_ok, 2 + START)
            pool.wait_ge(xn_kept, G + START)
            pool.wait_ge(zeroed, 16 * n_zero + START)
            for t in range(NT):
                pool.indirect_dma_start(out=slots, out_offset=bass.IndirectOffsetOnAxis(ap=slot_in[:, t:t + 1], axis=0),
                                        in_=xn_all[:, t], in_offset=None, bounds_check=last_slot,
                                        oob_is_err=False).then_inc(sent, 16)
            pool.wait_ge(a_out, 16 * E_N + START)
            for t in range(NT):
                pool.indirect_dma_start(out=got[:, t], out_offset=None, in_=answers,
                                        in_offset=bass.IndirectOffsetOnAxis(ap=slot_out[:, t:t + 1], axis=0),
                                        bounds_check=last_slot, oob_is_err=False).then_inc(fetched[t // GT], 16)

        @block.scalar
        def _(act):
            counts = Counts(act, name)

            def root(g, u):
                act.wait_ge(moments, g * GT + GT + START)
                act.activation(std[:, u], mv[:, u, :, 1], ACT.Sqrt, bias=eps[:, 0:1]).then_inc(std_ok, 1)

            def group(g, u, i, last):
                if not last:
                    root(g + 1, 1 - u)
                at = counts(g * GT + GT + START)
                act.wait_ge(eps_ok, 1 + START)
                act.wait_ge(xn_ok, at[0])
                act.activation(xn_all[:, bass.ts(g, GT)], xn[:, u], ACT.Copy).then_inc(xn_kept, 1)
                for v in range(2):
                    act.wait_ge(xT_ps, g * 2 + v + 1 + START)
                    act.activation(xT[:, u, 2 * v:2 * v + 2].rearrange("p j k t -> p (j k t)"), bank[2 * u + v][:],
                                   ACT.Copy).then_inc(xT_ok, 1)

            def weights_of(e, u):
                act.dma_start(w1[:, u], W1[e].rearrange("(k p) f -> p k f", p=P)).then_inc(w_in[u], 16)
                act.dma_start(w2[:, u], W2[e].rearrange("(f p) d -> p f d", p=P)).then_inc(w_in[u], 16)

            def expert(e, u, last):
                if not last:
                    act.wait_ge(a_ps, e * nrow + START)
                    weights_of(e + 1, 1 - u)
                for n, (f, q) in enumerate(blocks):
                    if not biased and n % 2:
                        continue
                    act.wait_ge(h_ps, e * NB + n + 1 + START)
                    dst = hid[:, f, q * half:(q + 1) * half]
                    if biased:
                        act.activation(dst, bank[2 + n % 4][:, 0:half], ACT.Gelu_apprx_tanh,
                                       bias=b1_sb[:, e, f:f + 1]).then_inc(h_act, 1)
                    else:
                        act.activation(dst, bank[2 + n % 4][:, 0:half], ACT.Relu).then_inc(h_act, 1)

            act.wait_ge(eps_ok, 1 + START)
            root(0, 0)
            over_groups(act, group)
            weights_of(0, 0)
            act.wait_ge(chain, 2 + START)
            act.activation(route[1][:], route[0][:], ACT.Exp).then_inc(ex_ok, 1)
            over_experts_in_order(act, expert)

        @block.vector
        def _(dve):
            counts = Counts(dve, name)
            dve.memset(eps[:], LN_EPS).then_inc(eps_ok, 1)
            dve.memset(reset[:], 1.0).then_inc(once_ok, 1)
            dve.wait_ge(once_ok, 1 + START)
            dve.memset(reset[:, :, 0:1], 0.0).then_inc(once_ok, 1)
            dve.wait_ge(const_in, ALL_CONST)

            def statistics(g, u, i):
                dve.wait_ge(x_in[u], i * 16 + 16 + START)
                for j in range(GT):
                    dve.bn_stats(bn[:, u, j], x_all[:, g * GT + j]).then_inc(stats, 1)
                for j in range(GT):
                    at = counts(g * GT + j + 1 + START)
                    dve.wait_ge(const_in, ALL_CONST)
                    dve.wait_ge(stats, at[0])
                    dve.bn_aggr(mv[:, u, j], bn[:, u, j]).then_inc(moments, 1)

            def group(g, u, i, last):
                if not last:
                    statistics(g + 1, 1 - u, i + u)
                dve.wait_ge(std_ok, g + 1 + START)
                dve.reciprocal(rstd[:, u], std[:, u]).then_inc(rstd_ok, 1)
                dve.wait_ge(rstd_ok, g + 1 + START)
                dve.wait_ge(xn_kept, g - 1 + START)
                dve.wait_ge(xT_ps, g * 2 - 2 + START)
                for j in range(GT):
                    dve.tensor_scalar(xn[:, u, j], x_all[:, g * GT + j], mv[:, u, j, 0:1], rstd[:, u, j:j + 1],
                                      ALU.subtract, ALU.mult).then_inc(xn_ok, 1)

            statistics(0, 0, 0)
            over_groups(dve, group)
            dve.wait_ge(lg_ps, G + START)
            logits_ps = bank[6][:, 0:NT * E_N].rearrange("p (t e) -> p t e", e=E_N)
            if biased:
                dve.tensor_tensor(logit[:], logits_ps, bias_r[:].unsqueeze(1).broadcast_to([P, NT, E_N]),
                                  ALU.add).then_inc(lg_ok, 1)
            else:
                dve.tensor_copy(logit[:], logits_ps).then_inc(lg_ok, 1)
            n = [0]

            def step(ins):
                n[0] += 1
                ins.then_inc(chain, 1)
                dve.wait_ge(chain, n[0] + START)

            top, esum, prob, rank, pos, kept, factor, dropped, slot, sin, sout, _ = (v[:] for v in per_token)
            shifted, mask, work = (r[:] for r in route)
            dve.wait_ge(lg_ok, 1 + START)
            step(dve.tensor_reduce(top, logit[:], AX.X, ALU.max))
            step(dve.tensor_tensor(shifted, logit[:], over_experts(top), ALU.subtract))
            dve.wait_ge(ex_ok, 1 + START)
            step(dve.tensor_reduce(esum, mask, AX.X, ALU.add))
            step(dve.reciprocal(prob, esum))
            step(dve.tensor_tensor(work, logit[:], over_experts(top), ALU.is_equal))
            step(dve.tensor_tensor(mask, work, cst[:, C_RANK:C_RANK + E_N].unsqueeze(1).broadcast_to([P, NT, E_N]),
                                   ALU.mult))
            step(dve.tensor_reduce(rank, mask, AX.X, ALU.max))
            step(dve.tensor_tensor(work, mask, over_experts(rank), ALU.is_equal))
            dve.wait_ge(count_ps, 2 + START)
            step(dve.tensor_copy(total[:], bank[1][:, 0:NT * E_N].rearrange("p (t e) -> p e t", e=E_N)))
            step(dve.tensor_tensor_scan(running[:].rearrange("p e t -> p (e t)"), reset[:].rearrange("p e t -> p (e t)"),
                                        total[:].rearrange("p e t -> p (e t)"), 0.0, ALU.mult, ALU.add))
            step(dve.tensor_tensor(running[:], running[:], total[:], ALU.subtract))
            step(dve.tensor_tensor(shifted, bank[0][:, 0:NT * E_N].rearrange("p (t e) -> p t e", e=E_N),
                                   running[:].rearrange("p e t -> p t e"), ALU.add))
            step(dve.tensor_tensor(mask, shifted, work, ALU.mult))
            step(dve.tensor_reduce(pos, mask, AX.X, ALU.add))
            step(dve.tensor_scalar(kept, pos, float(cap), None, ALU.is_le))
            step(dve.tensor_scalar(dropped, kept, -1.0, 1.0, ALU.mult, ALU.add))
            step(dve.tensor_tensor(factor, kept, prob, ALU.mult))
            step(dve.tensor_scalar(slot, rank, -float(cap), float(E_N * cap - 1), ALU.mult, ALU.add))
            step(dve.tensor_tensor(slot, slot, pos, ALU.add))
            step(dve.tensor_scalar(sin, dropped, float(2 * E_N * cap), None, ALU.mult))
            step(dve.tensor_tensor(sin, sin, slot, ALU.add))
            step(dve.tensor_scalar(sout, slot, float(last_slot), None, ALU.min))
            dve.tensor_copy(slot_in[:], sin).then_inc(slot_ok, 1)
            dve.tensor_copy(slot_out[:], sout).then_inc(slot_ok, 1)

            def turned(e):
                for j in range(nrow):
                    dve.wait_ge(rT_ps, e * nrow + j + 1 + START)
                    dve.tensor_copy(rowsT[:, :, j * rp:(j + 1) * rp],
                                    bank[j % 2][:, 0:KD * rp].rearrange("p (k t) -> p k t", k=KD)).then_inc(rT_ok, 1)

            def expert(e, u, last):
                if not biased:
                    for n_, (f, q) in enumerate(blocks):
                        if n_ % 2 == 0:
                            continue
                        dve.wait_ge(h_ps, e * NB + n_ + 1 + START)
                        dve.tensor_scalar(hid[:, f, q * half:(q + 1) * half], bank[2 + n_ % 4][:, 0:half],
                                          0.0, None, ALU.max).then_inc(h_dve, 1)
                if not last:
                    turned(e + 1)
                dve.wait_ge(a_out, e * 16 + START)
                for j in range(nrow):
                    dve.wait_ge(a_ps, e * nrow + j + 1 + START)
                    dve.tensor_copy(ans[:, j], bank[6 + j % 2][0:rp, 0:D]).then_inc(a_ok, 1)

            turned(0)
            over_experts_in_order(dve, expert)
            for t in range(NT):
                if t % GT == 0:
                    dve.wait_ge(fetched[t // GT], 16 * GT)
                if keeps_dropped:
                    dve.scalar_tensor_tensor(got[:, t], got[:, t], factor[:, t:t + 1], x_all[:, t],
                                             ALU.mult, ALU.add).then_inc(mixed, 1)
                    dve.wait_ge(mixed, t + 1 + START)
                    dve.scalar_tensor_tensor(got[:, t], xn_all[:, t], dropped[:, t:t + 1], got[:, t],
                                             ALU.mult, ALU.add).then_inc(out_ok, 1)
                else:
                    dve.scalar_tensor_tensor(got[:, t], got[:, t], factor[:, t:t + 1], x_all[:, t],
                                             ALU.mult, ALU.add).then_inc(out_ok, 1)

        @block.tensor
        def _(pe):
            counts = Counts(pe, name)
            pe.wait_ge(const_in, ALL_CONST)

            def turn_tokens(g, u):
                for v in range(2):
                    at = counts(g * 2 - 2 + START, g * GT + 2 * v + 2 + START)
                    pe.wait_ge(const_in, ALL_CONST)
                    pe.wait_ge(xT_ok, at[0])
                    pe.wait_ge(xn_ok, at[1])
                    for j in range(2):
                        for k in range(KD):
                            last = pe.transpose(bank[2 * u + v][:, (j * KD + k) * P:(j * KD + k + 1) * P],
                                                xn[:, u, 2 * v + j, k * P:(k + 1) * P], ident)
                    last.then_inc(xT_ps, 1)

            def group(g, u, i, last):
                if not last:
                    turn_tokens(g + 1, 1 - u)
                at = counts(g * 2 + 2 + START)
                pe.wait_ge(const_in, ALL_CONST)
                pe.wait_ge(xT_ok, at[0])
                for j in range(GT):
                    for k in range(KD):
                        last = pe.matmul(bank[6][:, bass.ts(g * GT + j, E_N)], xT[:, u, j, k], wr[:, k],
                                         start=(k == 0), stop=(k == KD - 1))
                last.then_inc(lg_ps, 1)

            turn_tokens(0, 0)
            over_groups(pe, group)
            pe.wait_ge(chain, 8 + START)
            oh = route[2][:].rearrange("p t e -> p (t e)")
            pe.matmul(bank[0][:, 0:NT * E_N], cst[:, C_TRI:C_TRI + P], oh, start=True, stop=True).then_inc(count_ps, 1)
            pe.matmul(bank[1][:, 0:NT * E_N], cst[:, C_ONE:C_ONE + P], oh, start=True, stop=True).then_inc(count_ps, 1)
            pe.wait_ge(slot_ok, 2 + START)

            def turn_rows(e, u, i):
                pe.wait_ge(rows_in[u], i * 16 + 16 + START)
                for j in range(nrow):
                    pe.wait_ge(rT_ok, e * nrow + max(j - 1, 0) + START)
                    for k in range(KD):
                        last = pe.transpose(bank[j % 2][:, k * rp:(k + 1) * rp],
                                            rows[:, u, j, k * P:(k + 1) * P], ident[0:rp, 0:rp])
                    last.then_inc(rT_ps, 1)

            def expert(e, u, i, last):
                pe.wait_ge(rT_ok, (e + 1) * nrow + START)
                pe.wait_ge(w_in[u], i * 32 + 32 + START)
                for n, (f, q) in enumerate(blocks):
                    if biased:
                        pe.wait_ge(h_act, e * NB + max(n - 3, 0) + START)
                    elif n % 2 == 0:
                        pe.wait_ge(h_act, e * (NB // 2) + max(n // 2 - 1, 0) + START)
                    else:
                        pe.wait_ge(h_dve, e * (NB // 2) + max(n // 2 - 1, 0) + START)
                    for k in range(KD):
                        product = pe.matmul(bank[2 + n % 4][:, 0:half], w1[:, u, k, f * P:(f + 1) * P],
                                            rowsT[:, k, q * half:(q + 1) * half],
                                            start=(k == 0), stop=(k == KD - 1))
                    product.then_inc(h_ps, 1)
                if not last:
                    turn_rows(e + 1, 1 - u, i + u)
                for j in range(nrow):
                    at = counts(e * nrow + max(j - 1, 0) + START, (e + 1) * on_act + START,
                                (e + 1) * (NB - on_act) + START)
                    pe.wait_ge(const_in, ALL_CONST)
                    pe.wait_ge(a_ok, at[0])
                    if j == 0:
                        pe.wait_ge(h_act, at[1])
                        pe.wait_ge(h_dve, at[2])
                    if biased:
                        pe.matmul(bank[6 + j % 2][0:rp, 0:D], cst[0:1, C_ONE:C_ONE + rp], b2_sb[:, e],
                                  start=True, stop=False)
                    for f in range(FT):
                        product = pe.matmul(bank[6 + j % 2][0:rp, 0:D], hid[:, f, j * rp:(j + 1) * rp],
                                            w2[:, u, f], start=(f == 0 and not biased), stop=(f == FT - 1))
                    product.then_inc(a_ps, 1)

            turn_rows(0, 0, 0)
            with pe.Fori(0, E_N // 2 - 1) as i:
                for u in range(2):
                    expert(i * 2 + u, u, i, False)
            expert(E_N - 2, 0, E_N // 2 - 1, False)
            expert(E_N - 1, 1, E_N // 2 - 1, True)
    clear(nc, held)


TB = S // P


def attention_layer(nc, consts, x, WqT, WkT, WvT, bq, bk, bv, WoT, bo, out):
    QH = S // 512
    UNITS = 2 * TB
    held = []
    with ExitStack() as ctx:
        def sb(n, shape, dt=F32):
            return ctx.enter_context(nc.sbuf_tensor(f"at_{n}", shape, dt))

        def sem(n):
            held.append(nc.alloc_semaphore(name=f"at_{n}"))
            return held[-1]

        score = [ctx.enter_context(nc.psum_tensor(f"at_score{i}", [P, S], F32)) for i in range(2)]
        mix = ctx.enter_context(nc.psum_tensor("at_mix", [P, S], F32))
        bank = [ctx.enter_context(nc.psum_tensor(f"at_bank{i}", [P, 512], F32)) for i in range(2)]

        ident = sb("ident", [P, P])
        wqk = sb("wqk", [P, 2, 2, KD, P])
        wv = sb("wv", [P, KD, H * DH])
        wo = sb("wo", [P, HP, D])
        b_q, b_k = sb("b_q", [P, HP]), sb("b_k", [P, HP])
        b_v = sb("b_v", [P, H * DH])
        b_o = sb("b_o", [P, D])
        x_ln = sb("x_ln", [P, TB, D])
        x_res = sb("x_res", [P, TB, D])
        xn = sb("xn", [P, TB, D])
        bn = sb("bn", [P, TB, 6])
        mv = sb("mv", [P, TB, 2])
        eps = sb("eps", [P, 1])
        std = sb("std", [P, TB])
        rstd = sb("rstd", [P, TB])
        xT = sb("xT", [P, KD, S])
        Q = sb("Q", [P, 2, 2, S], F32R)
        KH = sb("KH", [P, 2, 2, S], F32R)
        KL = sb("KL", [P, 2, 2, S], F32R)
        V = sb("V", [P, 2, TB, P])
        E = sb("E", [P, 4, S])
        top, ntop, esum, rsum = (sb(n, [P, 4]) for n in ("top", "ntop", "esum", "rsum"))
        Vs = sb("Vs", [P, 4, DH])
        CT = sb("CT", [P, HP, S])

        const_in, eps_ok, x_in, r_in, res_ok, stored = map(sem, ("const_in", "eps_ok", "x_in", "r_in", "res_ok", "stored"))
        stats, moments, std_ok, rstd_ok, xn_ok, xT_ps, xT_ok = map(
            sem, ("stats", "moments", "std_ok", "rstd_ok", "xn_ok", "xT_ps", "xT_ok"))
        q_ps, qh_ok, ql_ok, k_ps, kh_ok, kl_ok, v_ps, v_ok = map(
            sem, ("q_ps", "qh_ok", "ql_ok", "k_ps", "kh_ok", "kl_ok", "v_ps", "v_ok"))
        s_ps, top_ok, ntop_ok, e_ok, rsum_ok, vs_ok, c_ps, ct_ok = map(
            sem, ("s_ps", "top_ok", "ntop_ok", "e_ok", "rsum_ok", "vs_ok", "c_ps", "ct_ok"))
        o_ps, y_ok = sem("o_ps"), sem("y_ok")
        late_in = sem("late_in")
        w_in = [sem(f"w_in{u}") for u in range(2)]
        start_counts(nc, held)

        ALL_CONST = 16 * 3 + START
        ALL_LATE = 16 * 4 + START
        x_t = x.rearrange("b (n p) d -> b p n d", p=P)
        out_t = out.rearrange("b (n p) d -> b p n d", p=P)
        HEAD = [slice(0, DH), slice(DH, P)]

        def over_pairs(eng, body):
            def batch(b, last):
                with eng.Fori(0, HP // 2 - 1) as a2:
                    for u in range(2):
                        body(b, a2 * 2 + u, u, b * (HP // 2) + a2, False, False)
                body(b, HP - 2, 0, b * (HP // 2) + HP // 2 - 1, False, False)
                body(b, HP - 1, 1, b * (HP // 2) + HP // 2 - 1, not last, last)

            with eng.Fori(0, B - 1) as b:
                batch(b, False)
            batch(B - 1, True)

        def piece_of(t, turn, end):
            if end:
                return []
            if turn:
                return {3: [("q", 0), ("q", 1)], 5: [("k", 0), ("k", 1)], 7: [("v", 0), ("v", 1)]}.get(t, [])
            return {0: [("q", 0)], 1: [("q", 1)], 3: [("k", 0)], 4: [("k", 1)], 6: [("v", 0)], 7: [("v", 1)]}.get(t, [])

        block = ctx.enter_context(nc.Block())

        @block.sync
        def _(sp):
            def weights_of(a, parity):
                for i, wt in enumerate((WqT, WkT)):
                    sp.dma_start(wqk[:, parity, i], wt.rearrange("(k p) n -> p k n", p=P)[:, :, bass.ts(a, P)]
                                 ).then_inc(w_in[parity], 16)

            sp.dma_start(x_ln[:], x_t[0]).then_inc(x_in, 16)
            sp.dma_start(ident[:], consts[:, C_ID:C_ID + P]).then_inc(const_in, 16)
            weights_of(0, 0)
            sp.dma_start(b_q[:], bq.rearrange("(a p) -> p a", p=P), allow_slow_non_contiguous=True).then_inc(const_in, 16)
            sp.dma_start(b_k[:], bk.rearrange("(a p) -> p a", p=P), allow_slow_non_contiguous=True).then_inc(const_in, 16)
            sp.dma_start(wv[:], WvT.rearrange("(k p) n -> p k n", p=P)).then_inc(late_in, 16)
            sp.dma_start(b_v[:], bv.unsqueeze(0).broadcast_to([P, H * DH])).then_inc(late_in, 16)
            weights_of(1, 1)
            sp.dma_start(x_res[:], x_t[0]).then_inc(r_in, 16)
            sp.dma_start(b_o[:], bo.unsqueeze(0).broadcast_to([P, D])).then_inc(late_in, 16)
            sp.dma_start(wo[:], WoT.rearrange("(a p) d -> p a d", p=P)).then_inc(late_in, 16)

            def next_weights(n, a, parity):
                sp.wait_ge(k_ps, n * 2 + 2 + START)
                weights_of(a, parity)

            def batch(b, last):
                with sp.Fori(0, HP // 2 - 1) as a2:
                    for u in range(2):
                        next_weights(b * HP + a2 * 2 + u, a2 * 2 + u + 2, u)
                if not last:
                    for u in range(2):
                        next_weights(b * HP + HP - 2 + u, u, u)
                    sp.wait_ge(xn_ok, b * TB + TB + START)
                    sp.dma_start(x_ln[:], x_t[b + 1]).then_inc(x_in, 16)
                sp.wait_ge(y_ok, b * TB + TB + START)
                sp.dma_start(out_t[b], x_res[:]).then_inc(stored, 16)
                sp.wait_ge(stored, b * 16 + 16 + START)
                if not last:
                    sp.dma_start(x_res[:], x_t[b + 1]).then_inc(r_in, 16)

            with sp.Fori(0, B - 1) as b:
                batch(b, False)
            batch(B - 1, True)

        @block.gpsimd
        def _(pool):
            pool.wait_ge(late_in, ALL_LATE)
            with pool.Fori(0, B) as b:
                pool.wait_ge(r_in, b * 16 + 16 + START)
                pool.tensor_tensor(x_res[:], x_res[:], b_o[:].unsqueeze(1).broadcast_to([P, TB, D]),
                                   ALU.add).then_inc(res_ok, 1)

        @block.scalar
        def _(act):
            counts = Counts(act, "at")

            def root(b):
                act.wait_ge(moments, b * TB + TB + START)
                act.activation(std[:], mv[:, :, 1], ACT.Sqrt, bias=eps[:, 0:1]).then_inc(std_ok, 1)

            def transposed(b, u):
                act.wait_ge(xT_ps, b * 4 + u + 1 + START)
                act.activation(xT[:, :, 2 * u * P:(2 * u + 2) * P].rearrange("p k (j t) -> p k j t", j=2),
                               bank[u % 2][:].rearrange("p (k j t) -> p k j t", k=KD, j=2),
                               ACT.Copy).then_inc(xT_ok, 1)

            def high(kind, n, a, parity, q):
                cols = slice(q * 512, (q + 1) * 512)
                at = counts(n * 2 + q + 1 + START)
                act.wait_ge(const_in, ALL_CONST)
                if kind == "q":
                    act.wait_ge(q_ps, at[0])
                    for h in range(2):
                        act.activation(Q[HEAD[h], parity, h, cols], bank[q][HEAD[h]], ACT.Identity,
                                       bias=b_q[HEAD[h], bass.ds(a, 1)]).then_inc(qh_ok, 1)
                if kind == "k":
                    act.wait_ge(k_ps, at[0])
                    for h in range(2):
                        for to in range(2):
                            act.activation(KH[HEAD[to], parity, h, cols], bank[q][HEAD[h]], ACT.Identity,
                                           bias=b_k[HEAD[h], bass.ds(a, 1)]).then_inc(kh_ok, 1)

            def exponentials(n, t, h):
                i = 2 * t + h
                act.wait_ge(ntop_ok, n * UNITS + i + 1 + START)
                act.wait_ge(c_ps, n * TB + t - 1 + START)
                act.activation(E[:, i % 4], score[h][:], ACT.Exp, scale=1.0 / 8.0,
                               bias=ntop[:, i % 4:i % 4 + 1], accum_out=esum[:, i % 4:i % 4 + 1]).then_inc(e_ok, 1)

            def body(b, a, parity, twos, turn, end):
                n = b * HP + a
                for t in range(TB):
                    after = (n, t + 1) if t + 1 < TB else (n + 1, 0)
                    last = end and t == TB - 1
                    for kind, q in piece_of(t - 1, turn, end):
                        high(kind, n + 1, 0 if turn else a + 1, 1 - parity, q)
                    if not last:
                        exponentials(*after, 0)
                        exponentials(*after, 1)
                    if turn and t == 0:
                        root(b + 1)
                    if turn and t in (1, 2):
                        transposed(b + 1, 2 * t - 2)
                        transposed(b + 1, 2 * t - 1)
                at = counts(n * TB + TB + START)
                act.wait_ge(const_in, ALL_CONST)
                act.wait_ge(c_ps, at[0])
                act.activation(CT[:, bass.ds(a, 1)].rearrange("p o s -> p (o s)"), mix[:], ACT.Copy).then_inc(ct_ok, 1)

            act.wait_ge(eps_ok, 1 + START)
            root(0)
            for u in range(TB // 2):
                transposed(0, u)
            for q in range(QH):
                high("q", 0, 0, 0, q)
            for q in range(QH):
                high("k", 0, 0, 0, q)
            exponentials(0, 0, 0)
            exponentials(0, 0, 1)
            over_pairs(act, body)

        @block.vector
        def _(dve):
            counts = Counts(dve, "at")

            def statistics(b):
                dve.wait_ge(x_in, b * 16 + 16 + START)
                for j in range(TB):
                    dve.bn_stats(bn[:, j], x_ln[:, j]).then_inc(stats, 1)
                for j in range(TB):
                    at = counts(b * TB + j + 1 + START)
                    dve.wait_ge(const_in, ALL_CONST)
                    dve.wait_ge(stats, at[0])
                    dve.bn_aggr(mv[:, j], bn[:, j]).then_inc(moments, 1)

            def normalise(b):
                dve.wait_ge(std_ok, b + 1 + START)
                dve.reciprocal(rstd[:], std[:]).then_inc(rstd_ok, 1)
                dve.wait_ge(rstd_ok, b + 1 + START)
                for j in range(TB):
                    dve.tensor_scalar(xn[:, j], x_ln[:, j], mv[:, j, 0:1], rstd[:, j:j + 1],
                                      ALU.subtract, ALU.mult).then_inc(xn_ok, 1)

            def low(kind, n, a, parity, q):
                cols = slice(q * 512, (q + 1) * 512)
                if kind == "q":
                    at = counts(n * 4 + 2 * q + 2 + START)
                    dve.wait_ge(const_in, ALL_CONST)
                    dve.wait_ge(qh_ok, at[0])
                    for h in range(2):
                        dve.scalar_tensor_tensor(Q[HEAD[1 - h], parity, h, cols], bank[q][HEAD[h]],
                                                 b_q[HEAD[h], bass.ds(a, 1)], Q[HEAD[h], parity, h, cols].bitcast(F32),
                                                 ALU.add, ALU.subtract).then_inc(ql_ok, 1)
                if kind == "k":
                    at = counts(n * 8 + 4 * q + 4 + START)
                    dve.wait_ge(const_in, ALL_CONST)
                    dve.wait_ge(kh_ok, at[0])
                    for h in range(2):
                        dve.scalar_tensor_tensor(KL[HEAD[h], parity, h, cols], bank[q][HEAD[h]],
                                                 b_k[HEAD[h], bass.ds(a, 1)], KH[HEAD[h], parity, h, cols].bitcast(F32),
                                                 ALU.add, ALU.subtract).then_inc(kl_ok, 1)
                    for h in range(2):
                        dve.wait_ge(kl_ok, n * 8 + 4 * q + h + 1 + START)
                        dve.tensor_copy(KL[HEAD[1 - h], parity, h, cols],
                                        KL[HEAD[h], parity, h, cols].bitcast(F32)).then_inc(kl_ok, 1)
                if kind == "v":
                    dve.wait_ge(v_ps, n * 2 + q + 1 + START)
                    dve.tensor_tensor(V[:, parity, 4 * q:4 * q + 4], bank[q][:].rearrange("p (j d) -> p j d", j=4),
                                      b_v[:, bass.ts(a, P)].unsqueeze(1).broadcast_to([P, 4, P]),
                                      ALU.add).then_inc(v_ok, 1)

            def maximum(n, t, h):
                i = 2 * t + h
                dve.wait_ge(s_ps, n * UNITS + i + 1 + START)
                dve.tensor_reduce(top[:, i % 4:i % 4 + 1], score[h][:], AX.X, ALU.max).then_inc(top_ok, 1)
                dve.wait_ge(top_ok, n * UNITS + i + 1 + START)
                dve.tensor_scalar(ntop[:, i % 4:i % 4 + 1], top[:, i % 4:i % 4 + 1], -1.0 / 8.0, None,
                                  ALU.mult).then_inc(ntop_ok, 1)

            def scale_values(n, t, parity):
                i = 2 * t % 4
                dve.wait_ge(e_ok, n * UNITS + 2 * t + 2 + START)
                dve.reciprocal(rsum[:, i:i + 2], esum[:, i:i + 2]).then_inc(rsum_ok, 1)
                dve.wait_ge(rsum_ok, n * TB + t + 1 + START)
                dve.wait_ge(v_ok, n * 2 + t // 4 + 1 + START)
                dve.wait_ge(c_ps, n * TB + t - 1 + START)
                for h in range(2):
                    dve.tensor_scalar(Vs[:, i + h], V[:, parity, t, HEAD[h]], rsum[:, i + h:i + h + 1],
                                      None, ALU.mult).then_inc(vs_ok, 1)

            def add_residual(b):
                dve.wait_ge(res_ok, b + 1 + START)
                for j in range(TB):
                    dve.wait_ge(o_ps, b * TB + j + 1 + START)
                    dve.tensor_tensor(x_res[:, j], bank[j % 2][:, 0:D], x_res[:, j], ALU.add).then_inc(y_ok, 1)

            def body(b, a, parity, twos, turn, end):
                n = b * HP + a
                for t in range(TB):
                    after = (n, t + 1) if t + 1 < TB else (n + 1, 0)
                    scale_values(n, t, parity)
                    if not (end and t == TB - 1):
                        maximum(*after, 0)
                        maximum(*after, 1)
                    if turn and t == 0:
                        statistics(b + 1)
                    if turn and t == 1:
                        normalise(b + 1)
                    for kind, q in piece_of(t - 1, turn, end):
                        low(kind, n + 1, 0 if turn else a + 1, 1 - parity, q)
                for kind, q in piece_of(TB - 1, turn, end):
                    low(kind, n + 1, 0 if turn else a + 1, 1 - parity, q)
                if turn or end:
                    add_residual(b)

            dve.memset(eps[:], LN_EPS).then_inc(eps_ok, 1)
            dve.wait_ge(const_in, ALL_CONST)
            statistics(0)
            normalise(0)
            for q in range(QH):
                low("q", 0, 0, 0, q)
            for q in range(QH):
                low("k", 0, 0, 0, q)
            maximum(0, 0, 0)
            maximum(0, 0, 1)
            dve.wait_ge(late_in, ALL_LATE)
            for q in range(QH):
                low("v", 0, 0, 0, q)
            over_pairs(dve, body)

        @block.tensor
        def _(pe):
            counts = Counts(pe, "at")

            def turn_x(b, u):
                if u < 2:
                    pe.wait_ge(v_ok, b * HP * 2 + u - 1 + START)
                else:
                    pe.wait_ge(xT_ok, b * 4 + u - 1 + START)
                pe.wait_ge(xn_ok, b * TB + 2 * u + 2 + START)
                for k in range(KD):
                    for j in range(2):
                        last = pe.transpose(bank[u % 2][:, (k * 2 + j) * P:(k * 2 + j + 1) * P],
                                            xn[:, 2 * u + j, k * P:(k + 1) * P], ident[:])
                last.then_inc(xT_ps, 1)

            def project(kind, b, outputs, n, a, parity, twos, q):
                if kind == "q":
                    at = counts(n * 2 + q - 1 + START, b * 4 + 4 + START, outputs * TB + START)
                    pe.wait_ge(const_in, ALL_CONST)
                    pe.wait_ge(w_in[parity], twos * 32 + 32 + START)
                    pe.wait_ge(v_ok, at[0])
                    pe.wait_ge(xT_ok, at[1])
                    pe.wait_ge(y_ok, at[2])
                if kind == "k":
                    at = counts(n * 4 + 2 * q + 2 + START)
                    pe.wait_ge(const_in, ALL_CONST)
                    pe.wait_ge(ql_ok, at[0])
                if kind == "v":
                    at = counts(n * 8 + 4 * q + 2 + START)
                    pe.wait_ge(const_in, ALL_CONST)
                    pe.wait_ge(kl_ok, at[0])
                    for j in range(4):
                        for k in range(KD):
                            last = pe.matmul(bank[q][:, j * P:(j + 1) * P], xT[:, k, (4 * q + j) * P:(4 * q + j + 1) * P],
                                             wv[:, k, bass.ts(a, P)], start=(k == 0), stop=(k == KD - 1))
                    last.then_inc(v_ps, 1)
                else:
                    for k in range(KD):
                        last = pe.matmul(bank[q][:], wqk[:, parity, 0 if kind == "q" else 1, k],
                                         xT[:, k, q * 512:(q + 1) * 512], start=(k == 0), stop=(k == KD - 1))
                    last.then_inc(q_ps if kind == "q" else k_ps, 1)

            def scores(n, t, h, parity):
                i = 2 * t + h
                pe.wait_ge(e_ok, n * UNITS + i - 1 + START)
                if i == 0:
                    pe.wait_ge(ql_ok, n * 4 + 4 + START)
                    pe.wait_ge(kl_ok, n * 8 + 8 + START)
                for part in (KH, KL):
                    for q in range(QH):
                        last = pe.matmul(score[h][:, q * 512:(q + 1) * 512], part[:, parity, h, t * P:(t + 1) * P],
                                         Q[:, parity, h, q * 512:(q + 1) * 512], start=part is KH, stop=part is KL)
                last.then_inc(s_ps, 1)

            def context(n, t):
                pe.wait_ge(vs_ok, n * UNITS + 2 * t + 2 + START)
                if t == 0:
                    pe.wait_ge(ct_ok, n + START)
                for q in range(QH):
                    for h in range(2):
                        i = (2 * t + h) % 4
                        last = pe.matmul(mix[HEAD[h], q * 512:(q + 1) * 512], Vs[:, i],
                                         E[:, i, q * 512:(q + 1) * 512], start=(t == 0), stop=(t == TB - 1))
                last.then_inc(c_ps, 1)

            def output(b, end):
                pe.wait_ge(ct_ok, b * HP + HP + START)
                for j in range(TB):
                    if j == 0:
                        pe.wait_ge(v_ok, 2 * B * HP + START if end else (b + 1) * HP * 2 + 2 + START)
                    if j >= 2:
                        pe.wait_ge(y_ok, b * TB + j - 1 + START)
                    for a in range(HP):
                        last = pe.matmul(bank[j % 2][:, 0:D], CT[:, a, j * P:(j + 1) * P], wo[:, a],
                                         start=(a == 0), stop=(a == HP - 1))
                    last.then_inc(o_ps, 1)

            def body(b, a, parity, twos, turn, end):
                n = b * HP + a
                for t in range(TB):
                    after = (n, t + 1) if t + 1 < TB else (n + 1, 0)
                    its = parity if t + 1 < TB else 1 - parity
                    last = end and t == TB - 1
                    if not last:
                        scores(*after, 0, its)
                    for kind, q in piece_of(t, turn, end):
                        project(kind, b + 1 if turn else b, b, n + 1, 0 if turn else a + 1, 1 - parity, twos + parity, q)
                    if not last:
                        scores(*after, 1, its)
                    context(n, t)
                    if turn and t in (1, 2):
                        turn_x(b + 1, 2 * t - 2)
                        turn_x(b + 1, 2 * t - 1)
                if turn or end:
                    output(b, end)

            pe.wait_ge(const_in, ALL_CONST)
            for u in range(TB // 2):
                turn_x(0, u)
            for kind in ("q", "k"):
                for q in range(QH):
                    project(kind, 0, 0, 0, 0, 0, 0, q)
            scores(0, 0, 0, 0)
            scores(0, 0, 1, 0)
            pe.wait_ge(late_in, ALL_LATE)
            for q in range(QH):
                project("v", 0, 0, 0, 0, 0, 0, q)
            over_pairs(pe, body)
    clear(nc, held)


def seq_kernel(nc, consts, x, Wq, Wk, Wv, Wbeta, b_beta, Wout, Wr, W1, W2,
               WqT, bq, WkT, bk, WvT, bv, WoT, bo, gate_w, gate_b, w1, b1, w2, b2, out):
    def scratch(name, shape):
        return nc.dram_tensor(name, shape, F32, kind="Internal").ap()

    x1, x2, x3 = (scratch(n, [B, S, D]) for n in ("x1", "x2", "x3"))
    cap0, cap1 = int(1.25 * B * S / E_N), 160
    slots0, answers0 = scratch("slots0", [E_N * cap0, D]), scratch("answers0", [E_N * cap0, D])
    slots1, answers1 = scratch("slots1", [E_N * cap1, D]), scratch("answers1", [E_N * cap1, D])
    delta_layer(nc, consts, x, Wq, Wk, Wv, Wbeta, b_beta, Wout, x1)
    expert_layer(nc, "m0", consts, x1, Wr, None, W1, None, W2, None, cap0, True, x2, slots0, answers0)
    attention_layer(nc, consts, x2, WqT, WkT, WvT, bq, bk, bv, WoT, bo, x3)
    expert_layer(nc, "m1", consts, x3, gate_w, gate_b, w1, b1, w2, b2, cap1, False, out, slots1, answers1)


def kernel(**inputs):
    import concourse.bacc as bacc
    from concourse.bass_utils import run_bass_kernel_spmd

    def rows(name):
        a = np.asarray(inputs[name])
        return np.ascontiguousarray(a.reshape(-1, a.shape[-1]).T)

    flat = lambda name: np.ascontiguousarray(np.asarray(inputs[name]).reshape(-1))
    plain = lambda name: np.ascontiguousarray(inputs[name])
    arrays = {"consts": shape_constants()}
    for n in ("x", "Wq", "Wk", "Wv", "Wbeta", "b_beta", "Wout"):
        arrays["L0_attn_" + n] = plain("L0_attn_" + n)
    for n in ("Wr", "W1", "W2"):
        arrays["L0_ffn_" + n] = plain("L0_ffn_" + n)
    for n in ("q", "k", "v", "l"):
        arrays[f"L1_attn_{n}_w"] = rows(f"L1_attn_{n}_w")
        arrays[f"L1_attn_{n}_b"] = flat(f"L1_attn_{n}_b")
    for n in ("gate_w", "gate_b", "w1", "b1", "w2", "b2"):
        arrays["L1_ffn_" + n] = plain("L1_ffn_" + n)

    nc = bacc.Bacc("TRN2", target_bir_lowering=False, num_devices=1)
    args = [nc.dram_tensor(n, a.shape, mybir.dt.from_np(a.dtype), kind="ExternalInput").ap() for n, a in arrays.items()]
    out = nc.dram_tensor("out", (B, S, D), F32, kind="ExternalOutput").ap()
    seq_kernel(nc, *args, out)
    r = run_bass_kernel_spmd(nc, [arrays], core_ids=[0])
    return r.results[0]["out"]
```
